# Optimizing a Trainium2 kernel written in Bass

```python
import numpy as np
import jax
import jax.numpy as jnp

def _softmax(x, axis=-1):
    return jax.nn.softmax(x, axis=axis)

def _gelu(x):
    return jax.nn.gelu(x, approximate=True)

def _silu(x):
    return jax.nn.silu(x)

def _sigmoid(x):
    return jax.nn.sigmoid(x)

def _layernorm(x, axis=-1, eps=1e-05):
    m = jnp.mean(x, axis=axis, keepdims=True)
    v = jnp.var(x, axis=axis, keepdims=True)
    return (x - m) / jnp.sqrt(v + eps)

def _scatter_add(tgt, idx, src, axis=0):
    return tgt.at[idx].add(src)

def _segment_sum(src, seg, n):
    return jax.ops.segment_sum(src, seg, n)
kernel_name = 'mk_metaformer_d2_conv_nchw512_r4_ae82f1'

def setup_inputs(seed: int=0):
    np.random.seed(seed)
    _w = jnp.asarray

    def _rec_inputs():
        import jax
        import jax.numpy as jnp
        _gk = jax.random.key(seed)
        x = -9.26e-05 + 0.9999 * jax.random.normal(jax.random.fold_in(_gk, 1), (8, 128, 24, 24), jnp.float32)
        return x
    x = _rec_inputs()

    def _L0_conv_setup():
        import jax, jax.numpy as jnp
        import numpy as np
        EPS = 1e-05
        RATES = (1, 6, 12, 18)

        def _bn(x, g, b, m, v):
            inv = g / jnp.sqrt(v + EPS)
            return x * inv[None, :, None, None] + (b - m * inv)[None, :, None, None]
        key = jax.random.key(seed)
        ks = jax.random.split(key, 20)
        B, C, H, W = (8, 128, 24, 24)
        Cq = C // 4
        f32 = jnp.float32
        inp = {}
        inp['x'] = jax.random.normal(ks[0], (B, C, H, W), f32)
        inp['wdw'] = jax.random.normal(ks[1], (4, Cq, 1, 3, 3), f32) * 0.1
        inp['bdw'] = jax.random.normal(ks[2], (4, Cq), f32) * 0.01
        inp['gdw'] = jnp.ones((4, Cq), f32) + 0.1 * jax.random.normal(ks[3], (4, Cq), f32)
        inp['bedw'] = jax.random.normal(ks[4], (4, Cq), f32) * 0.01
        inp['mdw'] = jax.random.normal(ks[5], (4, Cq), f32) * 0.01
        inp['vdw'] = jax.random.uniform(ks[6], (4, Cq), f32, 0.5, 1.5)
        inp['ws'] = jax.random.normal(ks[7], (4, 4, 1, 1), f32) * 0.5
        inp['bs'] = jax.random.normal(ks[8], (4,), f32) * 0.01
        inp['gs'] = jnp.ones((4,), f32) + 0.1 * jax.random.normal(ks[9], (4,), f32)
        inp['bes'] = jax.random.normal(ks[10], (4,), f32) * 0.01
        inp['ms'] = jax.random.normal(ks[11], (4,), f32) * 0.01
        inp['vs'] = jax.random.uniform(ks[12], (4,), f32, 0.5, 1.5)
        inp['wo'] = jax.random.normal(ks[13], (C, C, 1, 1), f32) * (1.0 / np.sqrt(C))
        inp['bo'] = jax.random.normal(ks[14], (C,), f32) * 0.01
        inp['go'] = jnp.ones((C,), f32) + 0.1 * jax.random.normal(ks[15], (C,), f32)
        inp['beo'] = jax.random.normal(ks[16], (C,), f32) * 0.01
        inp['mo'] = jax.random.normal(ks[17], (C,), f32) * 0.01
        inp['vo'] = jax.random.uniform(ks[18], (C,), f32, 0.5, 1.5)
        return inp
    _L0_conv_all = _L0_conv_setup()
    _L0_conv_in = {k: v for k, v in _L0_conv_all.items() if k in ('wdw', 'bdw', 'gdw', 'bedw', 'mdw', 'vdw', 'ws', 'bs', 'gs', 'bes', 'ms', 'vs', 'wo', 'bo', 'go', 'beo', 'mo', 'vo')}
    del _L0_conv_all

    def _L0_ffn_setup():
        import jax, jax.numpy as jnp
        import numpy as np
        TOP_K = 2
        key = jax.random.key(seed)
        ks = jax.random.split(key, 4)
        B, S, D, H, E = (2, 1024, 128, 512, 8)
        scale_in = 1.0 / np.sqrt(D)
        scale_h = 1.0 / np.sqrt(H)
        return {'x': jax.random.normal(ks[0], (B, S, D), dtype=jnp.float32), 'gate_w': jax.random.normal(ks[1], (D, E), dtype=jnp.float32) * scale_in, 'gate_b': jnp.zeros((E,), dtype=jnp.float32), 'w1': jax.random.normal(ks[2], (E, D, H), dtype=jnp.float32) * scale_in, 'b1': jnp.zeros((E, H), dtype=jnp.float32), 'w2': jax.random.normal(ks[3], (E, H, D), dtype=jnp.float32) * scale_h, 'b2': jnp.zeros((E, D), dtype=jnp.float32)}
    _L0_ffn_all = _L0_ffn_setup()
    _L0_ffn_in = {k: v for k, v in _L0_ffn_all.items() if k in ('gate_w', 'gate_b', 'w1', 'b1', 'w2', 'b2')}
    del _L0_ffn_all

    def _L1_conv_setup():
        import jax, jax.numpy as jnp
        import numpy as np
        from jax import lax
        EPS = 1e-05
        GROUPS = 16

        def _batchnorm(x, gamma, beta):
            m = jnp.mean(x, axis=(0, 2, 3), keepdims=True)
            v = jnp.mean((x - m) ** 2, axis=(0, 2, 3), keepdims=True)
            xhat = (x - m) * lax.rsqrt(v + EPS)
            return xhat * gamma[None, :, None, None] + beta[None, :, None, None]

        @jax.custom_vjp
        def binary_act(x):
            return jnp.sign(x)

        def _ba_fwd(x):
            return (jnp.sign(x), x)

        def _ba_bwd(x, g):
            return (jnp.clip(2.0 - 2.0 * jnp.abs(x), a_min=0.0) * g,)
        binary_act.defvjp(_ba_fwd, _ba_bwd)

        @jax.custom_vjp
        def binary_weight(w):
            return jnp.sign(w)

        def _bw_fwd(w):
            return (jnp.sign(w), w)

        def _bw_bwd(w, g):
            mask = jnp.logical_or(w >= 1.0, w <= -1.0)
            return (jnp.where(mask, 0.0, g),)
        binary_weight.defvjp(_bw_fwd, _bw_bwd)

        def _weight_scale(w):
            co = w.shape[0]
            wf = w.reshape(co, -1)
            bw = wf - jnp.mean(wf, axis=-1, keepdims=True)
            std = jnp.std(wf - jnp.mean(wf, axis=-1, keepdims=True), axis=-1, ddof=1, keepdims=True)
            bw = bw / std
            sw = jnp.mean(jnp.abs(bw), axis=-1).reshape(co, 1, 1, 1)
            return lax.stop_gradient(sw)
        key = jax.random.key(seed)
        ks = jax.random.split(key, 7)
        N, C, H, W = (16, 128, 32, 32)
        k = 3
        x = jax.random.normal(ks[0], (N, C, H, W), dtype=jnp.float32)
        conv_w = jax.random.normal(ks[1], (C, C // GROUPS, k, k), dtype=jnp.float32) * 0.1
        bn1_gamma = jnp.ones((C,), jnp.float32)
        bn1_beta = jnp.zeros((C,), jnp.float32)
        bn2_gamma = jnp.ones((C,), jnp.float32)
        bn2_beta = jnp.zeros((C,), jnp.float32)
        prelu_a = jnp.full((C,), 0.25, jnp.float32)
        return {'x': x, 'conv_w': conv_w, 'bn1_gamma': bn1_gamma, 'bn1_beta': bn1_beta, 'bn2_gamma': bn2_gamma, 'bn2_beta': bn2_beta, 'prelu_a': prelu_a}
    _L1_conv_all = _L1_conv_setup()
    _L1_conv_in = {k: v for k, v in _L1_conv_all.items() if k in ('conv_w', 'bn1_gamma', 'bn1_beta', 'bn2_gamma', 'bn2_beta', 'prelu_a')}
    del _L1_conv_all

    def _L1_ffn_setup():
        import jax, jax.numpy as jnp
        import numpy as np
        TOP_K = 2
        key = jax.random.key(seed)
        ks = jax.random.split(key, 4)
        B, S, D, H, E = (2, 1024, 128, 512, 8)
        scale_in = 1.0 / np.sqrt(D)
        scale_h = 1.0 / np.sqrt(H)
        return {'x': jax.random.normal(ks[0], (B, S, D), dtype=jnp.float32), 'gate_w': jax.random.normal(ks[1], (D, E), dtype=jnp.float32) * scale_in, 'gate_b': jnp.zeros((E,), dtype=jnp.float32), 'w1': jax.random.normal(ks[2], (E, D, H), dtype=jnp.float32) * scale_in, 'b1': jnp.zeros((E, H), dtype=jnp.float32), 'w2': jax.random.normal(ks[3], (E, H, D), dtype=jnp.float32) * scale_h, 'b2': jnp.zeros((E, D), dtype=jnp.float32)}
    _L1_ffn_all = _L1_ffn_setup()
    _L1_ffn_in = {k: v for k, v in _L1_ffn_all.items() if k in ('gate_w', 'gate_b', 'w1', 'b1', 'w2', 'b2')}
    del _L1_ffn_all
    return {'x': x, 'L0_conv_wdw': _L0_conv_in['wdw'], 'L0_conv_bdw': _L0_conv_in['bdw'], 'L0_conv_gdw': _L0_conv_in['gdw'], 'L0_conv_bedw': _L0_conv_in['bedw'], 'L0_conv_mdw': _L0_conv_in['mdw'], 'L0_conv_vdw': _L0_conv_in['vdw'], 'L0_conv_ws': _L0_conv_in['ws'], 'L0_conv_bs': _L0_conv_in['bs'], 'L0_conv_gs': _L0_conv_in['gs'], 'L0_conv_bes': _L0_conv_in['bes'], 'L0_conv_ms': _L0_conv_in['ms'], 'L0_conv_vs': _L0_conv_in['vs'], 'L0_conv_wo': _L0_conv_in['wo'], 'L0_conv_bo': _L0_conv_in['bo'], 'L0_conv_go': _L0_conv_in['go'], 'L0_conv_beo': _L0_conv_in['beo'], 'L0_conv_mo': _L0_conv_in['mo'], 'L0_conv_vo': _L0_conv_in['vo'], 'L0_ffn_gate_w': _L0_ffn_in['gate_w'], 'L0_ffn_gate_b': _L0_ffn_in['gate_b'], 'L0_ffn_w1': _L0_ffn_in['w1'], 'L0_ffn_b1': _L0_ffn_in['b1'], 'L0_ffn_w2': _L0_ffn_in['w2'], 'L0_ffn_b2': _L0_ffn_in['b2'], 'L1_conv_conv_w': _L1_conv_in['conv_w'], 'L1_conv_bn1_gamma': _L1_conv_in['bn1_gamma'], 'L1_conv_bn1_beta': _L1_conv_in['bn1_beta'], 'L1_conv_bn2_gamma': _L1_conv_in['bn2_gamma'], 'L1_conv_bn2_beta': _L1_conv_in['bn2_beta'], 'L1_conv_prelu_a': _L1_conv_in['prelu_a'], 'L1_ffn_gate_w': _L1_ffn_in['gate_w'], 'L1_ffn_gate_b': _L1_ffn_in['gate_b'], 'L1_ffn_w1': _L1_ffn_in['w1'], 'L1_ffn_b1': _L1_ffn_in['b1'], 'L1_ffn_w2': _L1_ffn_in['w2'], 'L1_ffn_b2': _L1_ffn_in['b2']}

def reference(x, L0_conv_wdw, L0_conv_bdw, L0_conv_gdw, L0_conv_bedw, L0_conv_mdw, L0_conv_vdw, L0_conv_ws, L0_conv_bs, L0_conv_gs, L0_conv_bes, L0_conv_ms, L0_conv_vs, L0_conv_wo, L0_conv_bo, L0_conv_go, L0_conv_beo, L0_conv_mo, L0_conv_vo, L0_ffn_gate_w, L0_ffn_gate_b, L0_ffn_w1, L0_ffn_b1, L0_ffn_w2, L0_ffn_b2, L1_conv_conv_w, L1_conv_bn1_gamma, L1_conv_bn1_beta, L1_conv_bn2_gamma, L1_conv_bn2_beta, L1_conv_prelu_a, L1_ffn_gate_w, L1_ffn_gate_b, L1_ffn_w1, L1_ffn_b1, L1_ffn_w2, L1_ffn_b2):
    import jax
    import jax.numpy as jnp

    def _L0_conv_ref(x, wdw, bdw, gdw, bedw, mdw, vdw, ws, bs, gs, bes, ms, vs, wo, bo, go, beo, mo, vo):
        import jax, jax.numpy as jnp
        import numpy as np
        EPS = 1e-05
        RATES = (1, 6, 12, 18)

        def _bn(x, g, b, m, v):
            inv = g / jnp.sqrt(v + EPS)
            return x * inv[None, :, None, None] + (b - m * inv)[None, :, None, None]
        B = x.shape[0]
        Cq = wdw.shape[1]
        xs = jnp.split(x, 4, axis=1)
        branches = []
        for i, r in enumerate(RATES):
            y = jax.lax.conv_general_dilated(xs[i], wdw[i], window_strides=(1, 1), padding=[(r, r), (r, r)], rhs_dilation=(r, r), dimension_numbers=('NCHW', 'OIHW', 'NCHW'), feature_group_count=Cq)
            y = y + bdw[i][None, :, None, None]
            y = jax.nn.relu(_bn(y, gdw[i], bedw[i], mdw[i], vdw[i]))
            branches.append(y)
        z = jnp.stack(branches, axis=2)
        W4 = ws[:, :, 0, 0]
        z = jnp.einsum('oi,bcihw->bcohw', W4, z) + bs[None, None, :, None, None]
        inv_s = gs / jnp.sqrt(vs + EPS)
        z = jax.nn.relu(z * inv_s[None, None, :, None, None] + (bes - ms * inv_s)[None, None, :, None, None])
        z = z.reshape(B, Cq * 4, z.shape[3], z.shape[4])
        Wo = wo[:, :, 0, 0]
        out = jnp.einsum('oi,bihw->bohw', Wo, z) + bo[None, :, None, None]
        out = jax.nn.relu(_bn(out, go, beo, mo, vo))
        return out

    def _L0_ffn_ref(x, gate_w, gate_b, w1, b1, w2, b2):
        import jax, jax.numpy as jnp
        import numpy as np
        TOP_K = 2
        B, S, D = x.shape
        E = gate_w.shape[1]
        flat_x = x.reshape(-1, D)
        gate_logits = flat_x @ gate_w + gate_b
        raw_weights = jax.nn.softmax(gate_logits, axis=-1)
        top_w, top_idx = jax.lax.top_k(raw_weights, TOP_K)
        one_hot = jax.nn.one_hot(top_idx, E, dtype=flat_x.dtype)
        gate_output = (one_hot * top_w[..., None]).sum(axis=-2)
        h = jax.nn.gelu(jnp.einsum('td,edh->teh', flat_x, w1) + b1, approximate=False)
        expert_out = jnp.einsum('teh,ehd->ted', h, w2) + b2
        combined = jnp.einsum('ted,te->td', expert_out, gate_output)
        return combined.reshape(B, S, -1)

    def _L1_conv_ref(x, conv_w, bn1_gamma, bn1_beta, bn2_gamma, bn2_beta, prelu_a):
        import jax, jax.numpy as jnp
        import numpy as np
        from jax import lax
        EPS = 1e-05
        GROUPS = 16

        def _batchnorm(x, gamma, beta):
            m = jnp.mean(x, axis=(0, 2, 3), keepdims=True)
            v = jnp.mean((x - m) ** 2, axis=(0, 2, 3), keepdims=True)
            xhat = (x - m) * lax.rsqrt(v + EPS)
            return xhat * gamma[None, :, None, None] + beta[None, :, None, None]

        @jax.custom_vjp
        def binary_act(x):
            return jnp.sign(x)

        def _ba_fwd(x):
            return (jnp.sign(x), x)

        def _ba_bwd(x, g):
            return (jnp.clip(2.0 - 2.0 * jnp.abs(x), a_min=0.0) * g,)
        binary_act.defvjp(_ba_fwd, _ba_bwd)

        @jax.custom_vjp
        def binary_weight(w):
            return jnp.sign(w)

        def _bw_fwd(w):
            return (jnp.sign(w), w)

        def _bw_bwd(w, g):
            mask = jnp.logical_or(w >= 1.0, w <= -1.0)
            return (jnp.where(mask, 0.0, g),)
        binary_weight.defvjp(_bw_fwd, _bw_bwd)

        def _weight_scale(w):
            co = w.shape[0]
            wf = w.reshape(co, -1)
            bw = wf - jnp.mean(wf, axis=-1, keepdims=True)
            std = jnp.std(wf - jnp.mean(wf, axis=-1, keepdims=True), axis=-1, ddof=1, keepdims=True)
            bw = bw / std
            sw = jnp.mean(jnp.abs(bw), axis=-1).reshape(co, 1, 1, 1)
            return lax.stop_gradient(sw)
        res = x
        h = _batchnorm(x, bn1_gamma, bn1_beta)
        h = binary_act(h)
        sw = _weight_scale(conv_w)
        bw = binary_weight(conv_w) * sw
        h = lax.conv_general_dilated(h, bw, window_strides=(1, 1), padding=((1, 1), (1, 1)), feature_group_count=GROUPS, dimension_numbers=('NCHW', 'OIHW', 'NCHW'))
        h = _batchnorm(h, bn2_gamma, bn2_beta)
        h = h + res
        a = prelu_a[None, :, None, None]
        return jnp.where(h > 0, h, a * h)

    def _L1_ffn_ref(x, gate_w, gate_b, w1, b1, w2, b2):
        import jax, jax.numpy as jnp
        import numpy as np
        TOP_K = 2
        B, S, D = x.shape
        E = gate_w.shape[1]
        flat_x = x.reshape(-1, D)
        gate_logits = flat_x @ gate_w + gate_b
        raw_weights = jax.nn.softmax(gate_logits, axis=-1)
        top_w, top_idx = jax.lax.top_k(raw_weights, TOP_K)
        one_hot = jax.nn.one_hot(top_idx, E, dtype=flat_x.dtype)
        gate_output = (one_hot * top_w[..., None]).sum(axis=-2)
        h = jax.nn.gelu(jnp.einsum('td,edh->teh', flat_x, w1) + b1, approximate=False)
        expert_out = jnp.einsum('teh,ehd->ted', h, w2) + b2
        combined = jnp.einsum('ted,te->td', expert_out, gate_output)
        return combined.reshape(B, S, -1)

    def _gn(v, G=32, eps=1e-05):
        B_, C_, H_, W_ = v.shape
        g = v.reshape(B_, G, C_ // G, H_, W_)
        m = jnp.mean(g, axis=(2, 3, 4), keepdims=True)
        s = jnp.var(g, axis=(2, 3, 4), keepdims=True)
        return ((g - m) / jnp.sqrt(s + eps)).reshape(v.shape)

    def _ln_c(v, eps=1e-06):
        m = jnp.mean(v, axis=1, keepdims=True)
        s = jnp.var(v, axis=1, keepdims=True)
        return (v - m) / jnp.sqrt(s + eps)

    def _ln_t(v, eps=1e-05):
        m = jnp.mean(v, axis=-1, keepdims=True)
        s = jnp.var(v, axis=-1, keepdims=True)
        return (v - m) / jnp.sqrt(s + eps)

    def _to_tokens(v):
        B_, C_, H_, W_ = v.shape
        return v.reshape(B_, C_, H_ * W_).transpose(0, 2, 1)

    def _from_tokens(t, like):
        B_, C_, H_, W_ = like.shape
        return t.transpose(0, 2, 1).reshape(B_, C_, H_, W_)
    x = x + _L0_conv_ref(_ln_c(x), L0_conv_wdw, L0_conv_bdw, L0_conv_gdw, L0_conv_bedw, L0_conv_mdw, L0_conv_vdw, L0_conv_ws, L0_conv_bs, L0_conv_gs, L0_conv_bes, L0_conv_ms, L0_conv_vs, L0_conv_wo, L0_conv_bo, L0_conv_go, L0_conv_beo, L0_conv_mo, L0_conv_vo)
    t = _to_tokens(x)
    t = t + _L0_ffn_ref(_ln_t(t), L0_ffn_gate_w, L0_ffn_gate_b, L0_ffn_w1, L0_ffn_b1, L0_ffn_w2, L0_ffn_b2)
    x = _from_tokens(t, x)
    x = x + _L1_conv_ref(_ln_c(x), L1_conv_conv_w, L1_conv_bn1_gamma, L1_conv_bn1_beta, L1_conv_bn2_gamma, L1_conv_bn2_beta, L1_conv_prelu_a)
    t = _to_tokens(x)
    t = t + _L1_ffn_ref(_ln_t(t), L1_ffn_gate_w, L1_ffn_gate_b, L1_ffn_w1, L1_ffn_b1, L1_ffn_w2, L1_ffn_b2)
    x = _from_tokens(t, x)
    return x

_drawn_inputs = setup_inputs


def setup_inputs(seed=0):
    import zlib

    import numpy as np

    out = dict(_drawn_inputs(seed))
    spreads = {'L0_ffn_gate_b': (0.0, 0.1),
     'L0_ffn_b1': (0.0, 0.1),
     'L0_ffn_b2': (0.0, 0.1),
     'L1_conv_bn1_gamma': (1.0, 0.2),
     'L1_conv_bn1_beta': (0.0, 0.1),
     'L1_conv_bn2_gamma': (1.0, 0.2),
     'L1_conv_bn2_beta': (0.0, 0.1),
     'L1_conv_prelu_a': (0.25, 0.2),
     'L1_ffn_gate_b': (0.0, 0.321),
     'L1_ffn_b1': (0.0, 0.511),
     'L1_ffn_b2': (0.0, 0.342)}
    factors = {'L0_conv_bedw': 2.792}
    for name, (base, spread) in spreads.items():
        noise = np.random.default_rng([zlib.crc32(name.encode()), seed]).standard_normal(out[name].shape)
        drawn = base * np.exp(spread * noise) if base else spread * noise
        out[name] = jnp.asarray(drawn.astype(out[name].dtype))
    for name, factor in factors.items():
        out[name] = (out[name] * factor).astype(out[name].dtype)
    return out
```

```python
from contextlib import ExitStack

import concourse.bass as bass
from concourse import mybir

F32 = mybir.dt.float32
F16 = mybir.dt.float16
BF16 = mybir.dt.bfloat16
I32 = mybir.dt.int32
ALU = mybir.AluOpType
ACT = mybir.ActivationFunctionType
AX = mybir.AxisListType

P = 128
B, C, H, W = 8, 128, 24, 24
HW = H * W
T = B * HW
NT = T // P
E, F, TOPK = 8, 512, 2
FC = F // P
CQ = C // 4
RATES = (1, 6, 12, 18)
CONV_GROUPS = 16
GI = C // CONV_GROUPS
CH = HW // 2
NCH = T // CH
RH = H // 2
HALF = B // 4
NBATCH = 4
TB = NT // NBATCH
GT = 3
NGRP = NT // GT
GPB = TB // GT
CPB = NCH // NBATCH
SUB = 2
SR = SUB * P
REGION = T + SR
ROW = C + 2
UNROLL = 4
SLOTS = -(-(T * TOPK // SR + E - 1) // UNROLL) * UNROLL
XS, WS_, HS = 64.0, 64.0, 16.0
LN_EPS_T, LN_EPS_C, BN_EPS = 1e-5, 1e-6, 1e-5
HP, WP = H + 2, W + 2


def metaformer_kernel(nc, t, out):
    x_cm = t["x"].rearrange("b c h w -> c b (h w)")
    x_ic = t["x"].rearrange("(h b) (g c) y x -> h g b c (y x)", b=4, c=CQ)
    out_cm = out.rearrange("b c h w -> c b (h w)")

    with ExitStack() as ctx:
        def sb(name, shape, dt):
            return ctx.enter_context(nc.sbuf_tensor(name, shape, dt))

        def sem(name):
            return ctx.enter_context(nc.semaphore(name))

        ctx.enter_context(nc.allow_non_contiguous_dma(reason="small parameter tables"))

        routed = [nc.dram_tensor(f"routed{l}", (E * REGION + SR, ROW), F32).ap() for l in range(2)]
        expert_out = [nc.dram_tensor(f"expert_out{l}", (TOPK * T, C), F32).ap() for l in range(2)]

        slab_a = sb("slab_a", [P, T], F32)
        slab_t = sb("slab_t", [P, T], F32)
        slab_b = sb("slab_b", [P, T], F32)
        slab_c = sb("slab_c", [P, T], F32)
        slab_d = sb("slab_d", [P, T], F32)
        rows = sb("rows", [P, 2 * TOPK * TB * ROW], F32)
        rows_v = rows[:].rearrange("p (n k t w) -> p n k t w", n=2, k=TOPK, w=ROW)
        w1hi = [sb(f"w1hi{l}", [P, E * F], F16) for l in range(2)]
        w1lo = [sb(f"w1lo{l}", [P, E * F], F16) for l in range(2)]
        w2hi = [sb(f"w2hi{l}", [P, E * F], F16) for l in range(2)]
        w2lo = [sb(f"w2lo{l}", [P, E * F], F16) for l in range(2)]
        b1pad = sb("b1pad", [P, E * F], F16)
        b2pad = [sb(f"b2pad{l}", [P, E * C], F16) for l in range(2)]

        tok = slab_t[:].rearrange("p (t c) -> p t c", c=C)
        tok_b = slab_b[:].rearrange("p (t c) -> p t c", c=C)
        tok_c = slab_c[:].rearrange("p (t c) -> p t c", c=C)
        xic = slab_b[:].rearrange("p (g h n) -> p g h n", g=4, h=HALF)
        yic = slab_c[:].rearrange("p (g h n) -> p g h n", g=4, h=HALF)
        sq = slab_d[:, T // 2:T].rearrange("p (g n) -> p g n", g=4)
        ycm = slab_d[:].rearrange("p (b n) -> p b n", b=B)
        std = slab_t[:, T - 2 * HW:T].rearrange("p (q n) -> p q n", n=CH)
        sign_words = B * HP * WP // 2
        signs = slab_d[:, 0:sign_words].bitcast(BF16).rearrange("p (b y x) -> p b y x", b=B, y=HP)
        tail = slab_d[:, sign_words:sign_words + 6 * CH].rearrange("p (s n) -> p s n", n=CH)
        diag = w2lo[1][:, 0:9 * P * 2].bitcast(F32).rearrange("p (t m) -> p t m", m=P)
        zrelu = w2hi[1][:, 0:4 * CH].bitcast(F32).rearrange("p (s n) -> p s n", n=CH)
        orelu = w2hi[1][:, 4 * CH:8 * CH].bitcast(F32).rearrange("p (s n) -> p s n", n=CH)
        wo_raw = w1hi[1][:, 0:2 * P].bitcast(F32)
        convw = w1hi[1][:, 2 * P:2 * P + 2 * GI * 9].bitcast(F32).rearrange("p (i t) -> p i t", t=9)
        convw_sign = w1hi[1][:, 1024:1024 + GI * 9].bitcast(BF16)
        convw_full = w1hi[1][:, 2048:2048 + 9 * P].bitcast(BF16).rearrange("p (t m) -> p t m", m=P)
        par_rows = w1lo[1][0:40, 0:2 * P].bitcast(F32)
        convw_abs = w1lo[1][:, 512:512 + 2 * GI * 9].bitcast(F32)
        group_mask = w1lo[1][:, 1024:1024 + P].bitcast(BF16)
        ring_rows = slab_c[:, 0:UNROLL * SUB * ROW].rearrange("p (s j w) -> p s j w", j=SUB, w=ROW)
        ring_y = slab_c[:, 2048:2048 + UNROLL * SUB * C].rearrange("p (s j c) -> p s j c", j=SUB, c=C)
        ring_xt = slab_c[:, 3200:3200 + 2 * SR].bitcast(F16).rearrange("p (s k m) -> p s k m", k=2, m=SR)
        ring_h = slab_b[:, 0:2 * FC * SR].rearrange("p (s n) -> p s n", n=FC * SR)
        ring_hhi = slab_b[:, 2048:2048 + FC * SR].bitcast(F16).rearrange("p (s n) -> p s n", n=FC * SR)
        ring_hlo = slab_b[:, 3072:3072 + FC * SR].bitcast(F16).rearrange("p (s n) -> p s n", n=FC * SR)

        ident = sb("ident", [P, P], F32)
        ident16 = sb("ident16", [P, P], F16)
        identb = sb("identb", [P, P], BF16)
        earlier = sb("earlier", [P, P], BF16)
        onesb = sb("onesb", [P, P], BF16)
        bias_one = sb("bias_one", [P, P], F16)
        bias_two = sb("bias_two", [P, P], F16)
        onesf = sb("onesf", [1, E], F32)
        block_mean = sb("block_mean", [P, P], F32)
        all_mean = sb("all_mean", [P, P], F32)
        mix = sb("mix", [P, P], F32)
        wo_t = sb("wo_t", [P, P], F32)
        convw_t = sb("convw_t", [P, 9, P], BF16)
        out_row = sb("out_row", [P, TOPK, NT], I32)
        rev = sb("rev", [P, E], F32)
        tile_no = sb("tile_no", [1, SLOTS], F32)
        fill = sb("fill", [P, SUB, ROW], F32)
        ring_meta = sb("ring_meta", [P, UNROLL, SUB, 2], F32)
        par = sb("par", [P, 40], F32)
        wdw = sb("wdw", [P, 4, 9], F32)
        ws_b = sb("ws_b", [P, 4], F32)
        fold = sb("fold", [P, 16], F32)
        gate_w = [sb(f"gate_w{l}", [P, E], F32) for l in range(2)]
        gate_b = [sb(f"gate_b{l}", [P, E], F32) for l in range(2)]
        sums = sb("sums", [P, NT, 6], F32)
        mv = sb("mv", [P, NT, 2], F32)
        rstd = sb("rstd", [P, TB], F32)
        rstdx = sb("rstdx", [P, TB], F32)
        prob = sb("prob", [P, TB, E], F32)
        tmp = sb("tmp", [P, TB, E], F32)
        best = sb("best", [P, TOPK, TB, E], F32)
        top = sb("top", [P, TOPK, TB], F32)
        red = sb("red", [P, TB], F32)
        chosen = sb("chosen", [P, TB + 1, E], BF16)
        pos = sb("pos", [P, TB + 1, E], F32)
        carry = sb("carry", [P, E], F32)
        slot_f = sb("slot_f", [P, TOPK, TB], F32)
        slot_ix = sb("slot_ix", [P, 2, TOPK, TB], I32)
        fill_ix = sb("fill_ix", [1, E], I32)
        small = sb("small", [P, 16], F32)
        small_i = sb("small_i", [1, E], I32)
        tab_expert = sb("tab_expert", [1, SLOTS + UNROLL + 1], I32)
        tab_row = sb("tab_row", [1, SLOTS + UNROLL + 1], I32)
        bn_sums = sb("bn_sums", [P, NCH, 6], F32)
        bn1 = sb("bn1", [P, 4], F32)
        bn2 = sb("bn2", [P, 8], F32)

        banks = [ctx.enter_context(nc.psum_tensor(f"bank{i}", [P, 512], F32)) for i in range(8)]
        bank_stat = bank_z = (banks[0], banks[1])
        bank_dw = bank_o = bank_conv = (banks[2], banks[3])
        bank_tp = (banks[4], banks[5])
        bank_tn = (banks[0], banks[1])
        bank_lg, bank_rk = banks[6], banks[7]
        bank_xt, bank_y = (banks[0], banks[1]), (banks[2], banks[3])
        bank_h = ((banks[4], banks[5]), (banks[6], banks[7]))

        hi_bias = [sem(f"hi_bias{l}") for l in range(2)]
        consts = sem("consts"); consts_pad = sem("consts_pad")
        ld_par = sem("ld_par"); ld_conv = sem("ld_conv"); ld_gate = sem("ld_gate")
        ld_xic = [sem(f"ld_xic{h}") for h in range(HALF)]
        ld_x = sem("ld_x")
        ld_bias = [sem(f"ld_bias{l}") for l in range(2)]
        ld_w = [[sem(f"ld_w{k}_{l}") for k in (1, 2)] for l in range(2)]
        hi_ready = [sem(f"hi_ready{l}") for l in range(2)]
        lo_ready = [sem(f"lo_ready{l}") for l in range(2)]
        bias_ready = [sem(f"bias_ready{l}") for l in range(2)]
        dve = sem("dve")
        act = sem("act")
        prep_t = sem("prep_t"); prep_c = sem("prep_c"); setup_dve = sem("setup_dve"); setup_act = sem("setup_act")
        setup_sqrt = sem("setup_sqrt"); setup_var = sem("setup_var"); convw_tp = sem("convw_tp")
        mean_ready = sem("mean_ready"); centred = sem("centred"); sq_ready = sem("sq_ready")
        var_ready = sem("var_ready"); vare_ready = sem("vare_ready"); std_ready = sem("std_ready")
        xn_ready = sem("xn_ready"); dw_ready = sem("dw_ready"); taps_ready = sem("taps_ready")
        bn_ready = sem("bn_ready")
        ld_ycm = [sem(f"ld_ycm{b}") for b in range(B)]
        z_ready = sem("z_ready"); zr_ready = sem("zr_ready"); o_ready = sem("o_ready")
        or_ready = sem("or_ready")
        stream = [sem(f"stream{l}") for l in range(2)]
        tp_ready = [sem(f"tp_ready{l}") for l in range(2)]
        tok_ready = [sem(f"tok_ready{l}") for l in range(2)]
        tvar = [sem(f"tvar{l}") for l in range(2)]
        tstd = [sem(f"tstd{l}") for l in range(2)]
        lg_shift = [sem(f"lg_shift{l}") for l in range(2)]
        lg_exp = [sem(f"lg_exp{l}") for l in range(2)]
        chosen_ready = [sem(f"chosen_ready{l}") for l in range(2)]
        rank_ready = [sem(f"rank_ready{l}") for l in range(2)]
        xn_tok = [sem(f"xn_tok{l}") for l in range(2)]
        xhi_ready = [sem(f"xhi_ready{l}") for l in range(2)]
        rows_ready = [sem(f"rows_ready{l}") for l in range(2)]
        scattered = [[sem(f"scattered{l}_{n}") for n in range(2)] for l in range(2)]
        fill_ready = [sem(f"fill_ready{l}") for l in range(2)]
        filled = [sem(f"filled{l}") for l in range(2)]
        table_ready = [sem(f"table_ready{l}") for l in range(2)]
        ld_ring = [sem(f"ld_ring{s}") for s in range(UNROLL)]
        xt_ready = [sem(f"xt_ready{l}") for l in range(2)]
        xt_copied = [sem(f"xt_copied{l}") for l in range(2)]
        h_ready = [sem(f"h_ready{l}") for l in range(2)]
        gelu_ready = [sem(f"gelu_ready{l}") for l in range(2)]
        hhi_ready = [sem(f"hhi_ready{l}") for l in range(2)]
        hlo_ready = [sem(f"hlo_ready{l}") for l in range(2)]
        scatter_turn = sem("scatter_turn")
        y_ready = [sem(f"y_ready{l}") for l in range(2)]
        y_copied = [sem(f"y_copied{l}") for l in range(2)]
        y_stored = [sem(f"y_stored{s}") for s in range(UNROLL)]
        ld_y = [sem(f"ld_y{n}") for n in range(NBATCH)]
        sum_ready = [sem(f"sum_ready{l}") for l in range(2)]
        var1 = sem("var1"); std1 = sem("std1"); xn1_ready = sem("xn1_ready")
        tp1_ready = sem("tp1_ready"); tp1_copied = sem("tp1_copied")
        bn1_var = sem("bn1_var"); bn1_std = sem("bn1_std"); bn1_ready = sem("bn1_ready")
        signs_zero = sem("signs_zero"); signs_ready = sem("signs_ready")
        conv_ready = sem("conv_ready"); conv_copied = sem("conv_copied")
        bn2_var = sem("bn2_var"); bn2_std = sem("bn2_std"); bn2_ready = sem("bn2_ready")
        u_ready = sem("u_ready"); hr_ready = sem("hr_ready")
        tpo_ready = sem("tpo_ready"); out_ready = sem("out_ready"); stored = sem("stored")

        ENG = mybir.EngineType
        N_TAIL = SLOTS - UNROLL

        def table_values(engine, table, base, n, most):
            _, values = nc.values_load_multi_w_load_instructions(
                table[0:1, bass.ds(base, n)], engines=[engine], min_val=0, max_val=most,
                skip_runtime_bounds_check_because="the table's entries are clamped to this range")
            return values

        def ring_round(l, base, k):
            return (base + (l * SLOTS + UNROLL * (k // UNROLL))) * (16 // UNROLL) + 16

        def stored_round(l, base, k):
            return (base + (l * SLOTS + UNROLL * (k // UNROLL))) * (16 * SUB // UNROLL) + 16 * SUB

        N_CONSTS, N_PADS = 21, 9
        N_PAR_DMA = 5 + 5 + 5 + 5
        N_CONV_DMA = 4 + 4 + 1 + 1
        N_SETUP = 9 + 1 + 2 + 9

        def scatter_goal(n):
            return 16 * TOPK * TB * (n // 2 + 1)

        def load_biases(sp, l, first):
            if first:
                for m in range(2):
                    for q in (0, 32):
                        sp.dma_start(slab_d[q:q + 1, m * E * C:(m + 1) * E * C],
                                     t[f"L{m}_ffn_b2"].rearrange("(a e) d -> a (e d)", a=1)).then_inc(ld_bias[0], 16)
            for q in (0, 32):
                sp.dma_start(rows[q:q + 1, 0:E * F],
                             t[f"L{l}_ffn_b1"].rearrange("(a e) f -> a (e f)", a=1)).then_inc(ld_bias[l], 16)

        block = ctx.enter_context(nc.Block())

        @block.sync
        def _(sp):
            for h in range(HALF):
                for g in range(4):
                    for b in range(4):
                        sp.dma_start(xic[CQ * b:CQ * b + CQ, g, h, :], x_ic[h, g, b]).then_inc(ld_xic[h], 16)
                if h == 0:
                    for i, name in enumerate(("bdw", "gdw", "bedw", "mdw", "vdw")):
                        sp.dma_start(par_rows[4 * i:4 * i + 4, :].rearrange("r (b c) -> r b c", b=4),
                                     t["L0_conv_" + name].unsqueeze(1).to_broadcast([4, 4, CQ])).then_inc(ld_par, 16)
                    for i, name in enumerate(("bs", "gs", "bes", "ms", "vs")):
                        sp.dma_start(par_rows[20 + i:21 + i, :].rearrange("r (c o) -> r c o", o=4),
                                     t["L0_conv_" + name].rearrange("(a b o) -> a b o", a=1, b=1)
                                     .to_broadcast([1, CQ, 4])).then_inc(ld_par, 16)
                    for i, name in enumerate(("L0_conv_bo", "L0_conv_go", "L0_conv_beo", "L0_conv_mo", "L0_conv_vo",
                                              "L1_conv_bn1_gamma", "L1_conv_bn1_beta", "L1_conv_bn2_gamma",
                                              "L1_conv_bn2_beta", "L1_conv_prelu_a")):
                        sp.dma_start(par_rows[25 + i:26 + i, :], t[name].rearrange("(a c) -> a c", a=1)).then_inc(ld_par, 16)
                    for b in range(4):
                        sp.dma_start(wdw[CQ * b:CQ * b + CQ, :, :],
                                     t["L0_conv_wdw"].rearrange("g c a y x -> c g (a y x)")).then_inc(ld_conv, 16)
                    for g in range(4):
                        sp.dma_start(ws_b[CQ * g:CQ * g + CQ, :],
                                     t["L0_conv_ws"][:, g:g + 1, 0, 0].rearrange("o g -> g o").to_broadcast([CQ, 4]))\
                          .then_inc(ld_conv, 16)
                    sp.dma_start(wo_raw, t["L0_conv_wo"].rearrange("o i a b -> o (i a b)")).then_inc(ld_conv, 16)
                    sp.dma_start(convw, t["L1_conv_conv_w"].rearrange("o i y x -> o i (y x)")).then_inc(ld_conv, 16)
                    for l in range(2):
                        sp.dma_start(gate_w[l][:], t[f"L{l}_ffn_gate_w"]).then_inc(ld_gate, 16)
                        sp.dma_start(gate_b[l][:], t[f"L{l}_ffn_gate_b"].rearrange("(a e) -> a e", a=1)
                                     .to_broadcast([P, E])).then_inc(ld_gate, 16)
                    load_biases(sp, 0, first=True)
            for b in range(0, B, 2):
                sp.dma_start(slab_a[:, b * HW:(b + 2) * HW].rearrange("p (b n) -> p b n", b=2),
                             x_cm[:, b:b + 2, :]).then_inc(ld_x, 16)

            def shuffle(h):
                for g in range(4):
                    sp.wait_ge(bn_ready, 5 * h + 2 + g)
                    for b in range(4):
                        sp.dma_start(ycm[CQ * g:CQ * g + CQ, 4 * h + b, :],
                                     yic[CQ * b:CQ * b + CQ, g, h, :]).then_inc(ld_ycm[4 * h + b], 16)

            def load_weights(l):
                if l == 0:
                    sp.wait_ge(taps_ready, 6)
                    sp.wait_ge(dw_ready, 4)
                    for b in range(B):
                        sp.wait_ge(ld_ycm[b], 64)
                else:
                    sp.wait_ge(hi_ready[0], 2)
                    sp.wait_ge(lo_ready[0], 2)
                sp.dma_start(slab_b[:, 0:E * F].rearrange("p (e f) -> p e f", e=E),
                             t[f"L{l}_ffn_w1"].rearrange("e d f -> d e f")).then_inc(ld_w[l][0], 16)
                sp.dma_start(slab_c[:, 0:E * F].rearrange("p (e c d) -> p e c d", e=E, c=FC),
                             t[f"L{l}_ffn_w2"].rearrange("e (c p) d -> p e c d", p=P)).then_inc(ld_w[l][1], 16)

            def expert_loads(l):
                sp.wait_ge(fill_ready[l], 1)
                _, ends = nc.values_load_multi_w_load_instructions(
                    fill_ix[0:1, :], engines=[ENG.SP], min_val=0, max_val=E * REGION - SR,
                    skip_runtime_bounds_check_because="a region's rows end at least a slot tile before it does")
                sp.dma_start(routed[l][E * REGION:E * REGION + SR, :].rearrange("(j p) w -> p j w", p=P),
                             fill[:]).then_inc(filled[l], 16)
                for e in range(E):
                    sp.dma_start(routed[l][bass.ds(ends[e], SR), :].rearrange("(j p) w -> p j w", p=P), fill[:])\
                      .then_inc(filled[l], 16)
                sp.wait_ge(table_ready[l], 2)
                for n in range(2):
                    sp.wait_ge(scattered[l][n], scatter_goal(NBATCH - 2 + n))
                sp.wait_ge(filled[l], 16 * (E + 1))
                sp.wait_ge(hi_ready[1], 2)
                sp.wait_ge(lo_ready[1], 2)

                def step(base, k, row, first):
                    if not first:
                        sp.wait_ge(xt_copied[l], base + (k - UNROLL + 1))
                    sp.dma_start(ring_rows[:, k], routed[l][bass.ds(row, SR), :].rearrange("(j p) w -> p j w", p=P))\
                      .then_inc(ld_ring[k], 16)

                first_rows = table_values(ENG.SP, tab_row, 0, UNROLL, E * REGION)
                for k in range(UNROLL):
                    step(0, k, first_rows[k], True)
                with sp.Fori(UNROLL, SLOTS, UNROLL) as i0:
                    row = table_values(ENG.SP, tab_row, i0, UNROLL, E * REGION)
                    for k in range(UNROLL):
                        step(i0, k, row[k], False)

            def load_outputs(l):
                for s in range(UNROLL):
                    sp.wait_ge(y_stored[s], stored_round(l, SLOTS, -1))
                for n in range(NBATCH):
                    for k, dst in enumerate((tok_b, tok_c)):
                        src = expert_out[l][k * T + n * TB * P:k * T + (n + 1) * TB * P, :]
                        sp.dma_start(dst[:, n * TB:(n + 1) * TB, :],
                                     src.rearrange("(t p) c -> p t c", p=P)).then_inc(ld_y[n], 16)

            shuffle(0)
            shuffle(1)
            load_weights(0)
            load_weights(1)
            expert_loads(0)
            load_outputs(0)
            load_biases(sp, 1, first=False)
            expert_loads(1)
            load_outputs(1)
            for n in range(NBATCH):
                sp.wait_ge(out_ready, GPB * (n + 1))
                sp.dma_start(out_cm[:, 2 * n:2 * n + 2, :],
                             slab_a[:, 2 * n * HW:(2 * n + 2) * HW].rearrange("p (b n) -> p b n", b=2)).then_inc(stored, 16)
            sp.wait_ge(stored, 16 * NBATCH)

        @block.gpsimd
        def _(pool):
            count = [0]

            def const(ins):
                ins.then_inc(consts, 1)
                count[0] += 1

            for m in (ident, ident16, identb):
                const(pool.memset(m[:], 0.0))
            const(pool.memset(earlier[:], 1.0))
            pool.wait_ge(consts, 4)
            for m in (ident, ident16, identb):
                const(pool.affine_select(out=m[:], in_=m[:], compare_op=ALU.not_equal, fill=1.0, base=0,
                                         pattern=[[-1, P]], channel_multiplier=1))
            const(pool.affine_select(out=earlier[:], in_=earlier[:], compare_op=ALU.is_gt, fill=0.0, base=0,
                                     pattern=[[1, P]], channel_multiplier=-1))
            const(pool.memset(onesb[:], 1.0))
            const(pool.memset(bias_one[:], XS))
            const(pool.memset(bias_two[:], HS))
            const(pool.memset(all_mean[:], 1.0 / C))
            const(pool.memset(block_mean[:], 0.0))
            const(pool.memset(onesf[:], 1.0))
            const(pool.memset(chosen[:], 0.0))
            for k in range(TOPK):
                const(pool.iota(out_row[:, k, :], pattern=[[P, NT]], base=k * T, channel_multiplier=1))
            const(pool.iota(rev[:], pattern=[[-1, E]], base=E, channel_multiplier=0,
                            allow_small_or_imprecise_dtypes=True))
            const(pool.iota(tile_no[:], pattern=[[1, SLOTS]], base=0, channel_multiplier=0,
                            allow_small_or_imprecise_dtypes=True))
            const(pool.memset(fill[:, :, 0:C + 1], 0.0))
            const(pool.iota(fill[:, :, C + 1].bitcast(I32), pattern=[[P, SUB]], base=TOPK * T, channel_multiplier=1))
            assert count[0] == N_CONSTS
            pads = [pool.memset(b1pad[:], 0.0), pool.memset(b2pad[0][:], 0.0), pool.memset(b2pad[1][:], 0.0)]
            for ins in pads:
                ins.then_inc(consts_pad, 1)
            pool.wait_ge(consts, N_CONSTS)
            for b in range(4):
                pool.wait_ge(consts_pad, 3 + b)
                pool.memset(block_mean[CQ * b:CQ * b + CQ, CQ * b:CQ * b + CQ], 1.0 / C).then_inc(consts_pad, 1)
            pool.wait_ge(consts_pad, 7)
            gm = group_mask.rearrange("p (g i) -> p g i", i=GI)
            pool.affine_select(out=gm, in_=onesb[:].rearrange("p (g i) -> p g i", i=GI), compare_op=ALU.is_ge,
                               fill=0.0, base=0, pattern=[[-GI, CONV_GROUPS], [0, GI]],
                               channel_multiplier=1).then_inc(consts_pad, 1)
            pool.wait_ge(consts_pad, 8)
            pool.affine_select(out=gm, in_=gm, compare_op=ALU.is_ge, fill=0.0, base=GI - 1,
                               pattern=[[GI, CONV_GROUPS], [0, GI]], channel_multiplier=-1).then_inc(consts_pad, 1)

            def scatter_rows(l):
                for n in range(NBATCH):
                    pool.wait_ge(rows_ready[l], n + 1)
                    for j in range(TB):
                        for k in range(TOPK):
                            pool.indirect_dma_start(
                                routed[l], bass.IndirectOffsetOnAxis(ap=slot_ix[:, n % 2, k, j:j + 1], axis=0),
                                rows_v[:, n % 2, k, j, :], None, bounds_check=E * REGION - 1,
                                oob_is_err=False).then_inc(scattered[l][n % 2], 16)

            def scatter_outputs(l):
                def step(i, s, bound):
                    pool.wait_ge(y_copied[l], i + 1)
                    pool.sem_inc(scatter_turn, 1)
                    for j in range(SUB):
                        pool.indirect_dma_start(
                            expert_out[l],
                            bass.IndirectOffsetOnAxis(ap=ring_meta[:, s, j, 1:2].bitcast(I32), axis=0),
                            ring_y[:, s, j, :], None, bounds_check=bound,
                            oob_is_err=False).then_inc(y_stored[s], 16)
                with pool.register(f"last_row{l}") as last_row:
                    pool.reg_mov(last_row, TOPK * T - 1)
                    bound = pool.snap(last_row)
                    with pool.Fori(0, SLOTS, UNROLL) as i0:
                        for k in range(UNROLL):
                            step(i0 + k, k, bound)

            scatter_rows(0)
            scatter_outputs(0)
            pool.memset(slab_d[:, 0:sign_words], 0.0).then_inc(signs_zero, 1)
            scatter_rows(1)
            scatter_outputs(1)

        @block.scalar
        def _(sc):
            def bias_high(l):
                for q in (0, 32):
                    nc.scalar.activation(b1pad[q:q + 1, :], rows[q:q + 1, 0:E * F], ACT.Copy, scale=WS_)\
                      .then_inc(hi_bias[l], 1)

            sc.wait_ge(ld_bias[0], 16 * 6)
            sc.wait_ge(consts_pad, N_PADS)
            for m in range(2):
                for q in (0, 32):
                    nc.scalar.activation(b2pad[m][q:q + 1, :], slab_d[q:q + 1, m * E * C:(m + 1) * E * C], ACT.Copy,
                                         scale=WS_).then_inc(hi_bias[0], 1)
            bias_high(0)
            sc.wait_ge(setup_var, 1)
            nc.scalar.activation(fold[:, 8:15], fold[:, 0:7], ACT.Sqrt).then_inc(setup_sqrt, 1)
            sc.wait_ge(ld_conv, 16 * N_CONV_DMA)
            nc.scalar.activation(convw_sign.rearrange("p (i t) -> p i t", t=9), convw, ACT.Sign).then_inc(setup_act, 1)
            sc.wait_ge(prep_t, 2)
            nc.scalar.activation(wo_t[:], banks[2][:, 0:P], ACT.Copy).then_inc(setup_act, 1)
            for k in range(3):
                sc.wait_ge(convw_tp, k + 1)
                nc.scalar.activation(convw_t[:, 3 * k:3 * k + 3, :],
                                     banks[4 + k][:].bitcast(BF16)[:, 0:3 * P].rearrange("p (t m) -> p t m", m=P),
                                     ACT.Copy).then_inc(setup_act, 1)

            def norm_half(h):
                for q in (2 * h, 2 * h + 1):
                    c0 = (q % 2) * CH
                    sc.wait_ge(centred, q + 1)
                    if q == 0:
                        sc.wait_ge(bias_ready[0], 3)
                    nc.scalar.activation(sq[:, :, c0:c0 + CH], xic[:, :, h, c0:c0 + CH], ACT.Square)\
                      .then_inc(sq_ready, 1)
                for q in (2 * h, 2 * h + 1):
                    sc.wait_ge(vare_ready, q + 1)
                    nc.scalar.activation(std[:, q, :], std[:, q, :], ACT.Sqrt).then_inc(std_ready, 1)

            def bn_half(h):
                for r in range(2):
                    sc.wait_ge(dw_ready, 2 * h + r + 1)
                    nc.scalar.activation(yic[:, 0, h, r * CH:r * CH + CH], bank_dw[r][:, 0:CH], ACT.Relu,
                                         bias=par[:, 8:9], scale=par[:, 4:5]).then_inc(bn_ready, 1)
                for g in range(1, 4):
                    sc.wait_ge(taps_ready, 3 * h + g)
                    nc.scalar.activation(yic[:, g, h, :], yic[:, g, h, :], ACT.Relu,
                                         bias=par[:, 8 + g:9 + g], scale=par[:, 4 + g:5 + g]).then_inc(bn_ready, 1)

            def mix_batch(n):
                for j in range(CPB * n, CPB * n + CPB):
                    sc.wait_ge(z_ready, j + 1)
                    if j >= 2:
                        sc.wait_ge(o_ready, j - 1)
                    nc.scalar.activation(zrelu[:, j % 2, :], bank_z[j % 2][:, 0:CH], ACT.Relu,
                                         bias=par[:, 22:23], scale=par[:, 21:22]).then_inc(zr_ready, 1)
                    sc.wait_ge(o_ready, j + 1)
                    if j >= 2:
                        sc.wait_ge(stream[0], j - 1)
                    nc.scalar.activation(orelu[:, j % 2, :], bank_o[j % 2][:, 0:CH], ACT.Relu,
                                         bias=par[:, 27:28], scale=par[:, 26:27]).then_inc(or_ready, 1)

            def route_batch(l, n):
                for u in range(GPB * n, GPB * n + GPB):
                    sc.wait_ge(tp_ready[l], u + 1)
                    nc.scalar.activation(slab_t[:, u * GT * P:(u + 1) * GT * P], bank_tp[u % 2][:, 0:GT * P],
                                         ACT.Copy).then_inc(tok_ready[l], 1)
                sc.wait_ge(tvar[l], n + 1)
                nc.scalar.activation(rstd[:], rstd[:], ACT.Sqrt).then_inc(tstd[l], 1)
                sc.wait_ge(lg_shift[l], n + 1)
                nc.scalar.activation(prob[:], prob[:], ACT.Exp).then_inc(lg_exp[l], 1)
                sc.wait_ge(xn_tok[l], n + 1)
                r = rows_v[:, n % 2]
                nc.scalar.activation(r[:, 0, :, 0:C // 2].bitcast(F16), r[:, 1, :, 0:C], ACT.Copy)\
                  .then_inc(xhi_ready[l], 1)

            def weights_high(l):
                for k, (src, dst) in enumerate(((slab_b, w1hi[l]), (slab_c, w2hi[l]))):
                    sc.wait_ge(ld_w[l][k], 16)
                    if l == 1 and k == 0:
                        sc.wait_ge(stream[0], NCH)
                    nc.scalar.activation(dst[:], src[:, 0:E * F], ACT.Copy, scale=WS_).then_inc(hi_ready[l], 1)

            def experts(l):
                def step(base, k, first):
                    half = FC * SR // 2
                    for q in range(2):
                        sc.wait_ge(h_ready[l], 2 * base + (2 * k + q + 1))
                        if not (first and k < 2):
                            sc.wait_ge(hlo_ready[l], 2 * base + (2 * k + q - 3))
                        nc.scalar.activation(ring_h[:, k % 2, q * half:(q + 1) * half], bank_h[k % 2][q][:], ACT.Gelu,
                                             scale=1.0 / (XS * WS_)).then_inc(gelu_ready[l], 1)
                    for q in range(2):
                        sc.wait_ge(gelu_ready[l], 2 * base + (2 * k + q + 1))
                        if not (first and k < 2):
                            sc.wait_ge(y_ready[l], base + (k - 1))
                        nc.scalar.activation(ring_hhi[:, k % 2, q * half:(q + 1) * half],
                                             ring_h[:, k % 2, q * half:(q + 1) * half], ACT.Copy, scale=HS)\
                          .then_inc(hhi_ready[l], 1)

                for k in range(UNROLL):
                    step(0, k, True)
                with sc.Fori(UNROLL, SLOTS, UNROLL) as i0:
                    for k in range(UNROLL):
                        step(i0, k, False)

            def norm_tokens():
                for n in range(NBATCH):
                    sc.wait_ge(var1, n + 1)
                    nc.scalar.activation(rstd[:], rstd[:], ACT.Sqrt).then_inc(std1, 1)
                    for u in range(GPB * n, GPB * n + GPB):
                        cols = slice(u * GT * P, (u + 1) * GT * P)
                        sc.wait_ge(tp1_ready, 2 * u + 1)
                        nc.scalar.activation(slab_a[:, cols], bank_tp[u % 2][:, 0:GT * P], ACT.Copy).then_inc(tp1_copied, 1)
                        sc.wait_ge(tp1_ready, 2 * u + 2)
                        nc.scalar.activation(slab_c[:, cols], bank_tn[u % 2][:, 0:GT * P], ACT.Copy).then_inc(tp1_copied, 1)
                sc.wait_ge(bn1_var, 1)
                nc.scalar.activation(bn1[:, 2:3], bn1[:, 2:3], ACT.Sqrt).then_inc(bn1_std, 1)
                sc.wait_ge(signs_zero, 1)
                sc.wait_ge(bn1_ready, 1)
                for b in range(B):
                    nc.scalar.activation(signs[:, b, 1:1 + H, 1:1 + W],
                                         slab_c[:, b * HW:(b + 1) * HW].rearrange("p (y x) -> p y x", x=W),
                                         ACT.Sign, bias=bn1[:, 3:4], scale=bn1[:, 2:3]).then_inc(signs_ready, 1)
                for j in range(NCH):
                    sc.wait_ge(conv_ready, j + 1)
                    nc.scalar.activation(slab_b[:, j * CH:(j + 1) * CH], bank_conv[j % 2][:, 0:CH], ACT.Copy)\
                      .then_inc(conv_copied, 1)
                sc.wait_ge(bn2_var, 1)
                nc.scalar.activation(bn2[:, 2:3], bn2[:, 2:3], ACT.Sqrt).then_inc(bn2_std, 1)

            def prelu_batch(n):
                for j in range(CPB * n, CPB * n + CPB):
                    sc.wait_ge(u_ready, j + 1)
                    if j >= 2:
                        sc.wait_ge(stream[1], j - 1)
                    nc.scalar.activation(tail[:, 2 + j % 2, :], tail[:, j % 2, :], ACT.Identity, bias=bn2[:, 3:4])\
                      .then_inc(hr_ready, 1)
                    nc.scalar.activation(tail[:, 4 + j % 2, :], tail[:, j % 2, :], ACT.Relu, bias=bn2[:, 3:4])\
                      .then_inc(hr_ready, 1)

            norm_half(0)
            bn_half(0)
            mix_batch(0)
            route_batch(0, 0)
            norm_half(1)
            bn_half(1)
            mix_batch(1)
            route_batch(0, 1)
            mix_batch(2)
            route_batch(0, 2)
            mix_batch(3)
            route_batch(0, 3)
            weights_high(0)
            weights_high(1)
            experts(0)
            norm_tokens()
            sc.wait_ge(ld_bias[1], 32)
            bias_high(1)
            for n in range(NBATCH):
                prelu_batch(n)
                route_batch(1, n)
            experts(1)
            for u in range(NGRP):
                sc.wait_ge(tpo_ready, u + 1)
                nc.scalar.activation(slab_a[:, u * GT * P:(u + 1) * GT * P], bank_tp[u % 2][:, 0:GT * P],
                                     ACT.Copy).then_inc(out_ready, 1)

        @block.vector
        def _(v):
            chain = [0]

            def link(ins):
                chain[0] += 1
                ins.then_inc(dve, 1)
                v.wait_ge(dve, chain[0])

            def mark(ins):
                chain[0] += 1
                ins.then_inc(dve, 1)
                return chain[0]

            TT, TS, STT = v.tensor_tensor, v.tensor_scalar, v.scalar_tensor_tensor

            def bias_low(l):
                v.wait_ge(hi_bias[l], 6 if l == 0 else 2)
                if l == 0:
                    for m in range(2):
                        STT(out=b2pad[m][32:33, :], in0=slab_d[32:33, m * E * C:(m + 1) * E * C], scalar=WS_,
                            in1=b2pad[m][32:33, :], op0=ALU.mult, op1=ALU.subtract).then_inc(bias_ready[0], 1)
                STT(out=b1pad[32:33, :], in0=rows[32:33, 0:E * F], scalar=WS_, in1=b1pad[32:33, :],
                    op0=ALU.mult, op1=ALU.subtract).then_inc(bias_ready[l], 1)

            v.wait_ge(prep_t, 1)
            link(v.tensor_copy(par[:, 0:35], banks[3][:, 0:35]))
            for a, b, c in ((0, 4, 16), (4, 5, 24), (5, 6, 29)):
                link(TS(fold[:, a:b], par[:, c:c + b - a], BN_EPS, None, ALU.add))
            nw = GI * 9
            v.wait_ge(ld_conv, 16 * N_CONV_DMA)
            link(v.bn_stats(small[:, 0:6], convw.rearrange("p i t -> p (i t)")))
            link(v.bn_aggr(small[:, 6:8], small[:, 0:6]))
            TS(fold[:, 6:7], small[:, 7:8], nw / (nw - 1.0), None, ALU.mult).then_inc(setup_var, 1)
            v.wait_ge(setup_var, 1)
            v.wait_ge(setup_sqrt, 1)
            link(v.reciprocal(fold[:, 0:7], fold[:, 8:15]))
            for a, s, n in ((0, 0, 4), (4, 20, 1), (5, 25, 1)):
                w = n
                g_, be, m_, bd = ((4, 8, 12, 0) if s == 0 else (s + 1, s + 2, s + 3, s))
                link(TT(par[:, g_:g_ + w], par[:, g_:g_ + w], fold[:, a:a + w], ALU.mult))
                link(TT(par[:, bd:bd + w], par[:, bd:bd + w], par[:, m_:m_ + w], ALU.subtract))
                link(TT(par[:, bd:bd + w], par[:, bd:bd + w], par[:, g_:g_ + w], ALU.mult))
                link(TT(par[:, be:be + w], par[:, be:be + w], par[:, bd:bd + w], ALU.add))
            link(TS(convw_abs, convw.rearrange("p i t -> p (i t)"), small[:, 6:7], None, ALU.subtract))
            link(v.tensor_reduce(small[:, 8:9], convw_abs, AX.X, ALU.add, apply_absolute_value=True))
            link(TS(bn2[:, 4:5], small[:, 8:9], fold[:, 6:7], 1.0 / nw, ALU.mult, ALU.mult))
            v.wait_ge(consts, N_CONSTS)
            v.wait_ge(consts_pad, N_PADS)
            for k in range(9):
                TS(diag[:, k, :], ident[:], wdw[:, 0, k:k + 1], None, ALU.mult).then_inc(setup_dve, 1)
            link(v.tensor_reduce(convw_abs[:, 0:CQ], ident[:].rearrange("p (g c) -> p c g", g=4), AX.X, ALU.add))
            TT(mix[:].rearrange("p (c o) -> p c o", o=4), convw_abs[:, 0:CQ].unsqueeze(2).to_broadcast([P, CQ, 4]),
               ws_b[:].unsqueeze(1).to_broadcast([P, CQ, 4]), ALU.mult).then_inc(setup_dve, 1)
            v.wait_ge(ld_gate, 64)
            v.wait_ge(prep_t, 3)
            for l in range(2):
                TT(gate_w[l][:], gate_w[l][:], banks[7][:, l * E:(l + 1) * E], ALU.subtract)\
                  .then_inc(setup_dve, 1)
            v.wait_ge(setup_act, 1)
            for k in range(9):
                src = convw_sign.rearrange("p (i t) -> p i t", t=9)[:, :, k]
                TT(convw_full[:, k, :].rearrange("p (g i) -> p g i", i=GI),
                   src.unsqueeze(1).to_broadcast([P, CONV_GROUPS, GI]),
                   group_mask.rearrange("p (g i) -> p g i", i=GI), ALU.mult).then_inc(setup_dve, 1)
            bias_low(0)

            def norm_half(h):
                for q in (2 * h, 2 * h + 1):
                    c0 = (q % 2) * CH
                    xq = xic[:, :, h, c0:c0 + CH]
                    v.wait_ge(mean_ready, q + 1)
                    TT(xq, xq, bank_stat[q % 2][:, 0:CH].unsqueeze(1).to_broadcast([P, 4, CH]), ALU.subtract)\
                      .then_inc(centred, 1)
                for q in (2 * h, 2 * h + 1):
                    v.wait_ge(var_ready, q + 1)
                    TS(std[:, q, :], bank_stat[q % 2][:, 0:CH], LN_EPS_C, None, ALU.add).then_inc(vare_ready, 1)
                for q in (2 * h, 2 * h + 1):
                    c0 = (q % 2) * CH
                    xq = xic[:, :, h, c0:c0 + CH]
                    v.wait_ge(std_ready, q + 1)
                    link(v.reciprocal(std[:, q, :], std[:, q, :]))
                    v.wait_ge(sq_ready, q + 1)
                    TT(xq, xq, std[:, q, :].unsqueeze(1).to_broadcast([P, 4, CH]), ALU.mult).then_inc(xn_ready, 1)

            def taps_half(h):
                v.wait_ge(xn_ready, 2 * h + 2)
                last = {}
                order = [4, 0, 1, 2, 3, 5, 6, 7, 8]
                for n, k in enumerate(order):
                    for g in (1, 2, 3):
                        dy, dx = RATES[g] * (k // 3 - 1), RATES[g] * (k % 3 - 1)
                        y0, y1, x0, x1 = max(0, -dy), min(H, H - dy), max(0, -dx), min(W, W - dx)
                        xv = xic[:, g, h, :].rearrange("p (y x) -> p y x", x=W)[:, y0 + dy:y1 + dy, x0 + dx:x1 + dx]
                        yv = yic[:, g, h, :].rearrange("p (y x) -> p y x", x=W)[:, y0:y1, x0:x1]
                        if n == 0:
                            last[g] = mark(TS(yv, xv, wdw[:, g, k:k + 1], None, ALU.mult))
                            continue
                        v.wait_ge(dve, last[g])
                        ins = STT(out=yv, in0=xv, scalar=wdw[:, g, k:k + 1], in1=yv, op0=ALU.mult, op1=ALU.add)
                        if n < 8:
                            last[g] = mark(ins)
                        else:
                            ins.then_inc(taps_ready, 1)

            def add_batch(n):
                v.wait_ge(ld_x, 64)
                for j in range(CPB * n, CPB * n + CPB):
                    v.wait_ge(or_ready, j + 1)
                    a = slab_a[:, j * CH:(j + 1) * CH]
                    TT(a, a, orelu[:, j % 2, :], ALU.add).then_inc(stream[0], 1)

            def token_stats(tiles, eps):
                for j in tiles:
                    m = mark(v.bn_stats(sums[:, j, :], tok[:, j, :]))
                v.wait_ge(dve, m)
                for j in tiles:
                    m = mark(v.bn_aggr(mv[:, j, :], sums[:, j, :]))
                v.wait_ge(dve, m)
                return TS(rstd[:], mv[:, tiles[0]:tiles[-1] + 1, 1], eps, None, ALU.add)

            def route_batch(l, n):
                tiles = list(range(TB * n, TB * n + TB))
                v.wait_ge(tok_ready[l], GPB * (n + 1))
                token_stats(tiles, LN_EPS_T).then_inc(tvar[l], 1)
                v.wait_ge(tstd[l], n + 1)
                link(v.reciprocal(rstd[:], rstd[:]))
                link(TS(rstdx[:], rstd[:], XS, None, ALU.mult))
                over_e = lambda a: a.unsqueeze(2).to_broadcast([P, TB, E])
                over_t = lambda a: a.unsqueeze(1).to_broadcast([P, TB, E])
                v.wait_ge(tp_ready[l], GPB * (n + 1))
                lg = bank_lg[:, n * TB * E:(n + 1) * TB * E].rearrange("p (t e) -> p t e", e=E)
                link(TT(prob[:], lg, over_e(rstd[:]), ALU.mult))
                link(TT(prob[:], prob[:], over_t(gate_b[l][:]), ALU.add))
                link(v.tensor_reduce(red[:], prob[:], AX.X, ALU.max))
                TT(prob[:], prob[:], over_e(red[:]), ALU.subtract).then_inc(lg_shift[l], 1)
                r = rows_v[:, n % 2]
                if n >= 2:
                    v.wait_ge(scattered[l][n % 2], scatter_goal(n - 2))
                if n == 0 and l == 1:
                    v.wait_ge(bias_ready[1], 1)
                for j in range(TB):
                    ins = TS(r[:, 1, j, 0:C], tok[:, TB * n + j, :], mv[:, TB * n + j, 0:1], rstdx[:, j:j + 1],
                             ALU.subtract, ALU.mult)
                    if j < TB - 1:
                        m = mark(ins)
                v.wait_ge(dve, m)
                ins.then_inc(xn_tok[l], 1)
                v.wait_ge(lg_exp[l], n + 1)
                link(v.tensor_reduce(red[:], prob[:], AX.X, ALU.add))
                link(v.reciprocal(red[:], red[:]))
                link(TT(prob[:], prob[:], over_e(red[:]), ALU.mult))
                for k in range(TOPK):
                    link(v.tensor_reduce(top[:, k, :], prob[:], AX.X, ALU.max))
                    link(TT(tmp[:], prob[:], over_e(top[:, k, :]), ALU.is_equal))
                    link(TT(tmp[:], tmp[:], over_t(rev[:]), ALU.mult))
                    link(v.tensor_reduce(red[:], tmp[:], AX.X, ALU.max))
                    link(TT(best[:, k], over_t(rev[:]), over_e(red[:]), ALU.is_equal))
                    if k == 0:
                        link(STT(out=prob[:], in0=best[:, 0], scalar=-2.0, in1=prob[:], op0=ALU.mult, op1=ALU.add))
                TT(chosen[:, 0:TB, :], best[:, 0], best[:, 1], ALU.add).then_inc(chosen_ready[l], 1)
                v.wait_ge(xhi_ready[l], n + 1)
                hi = r[:, 0, :, 0:C // 2].bitcast(F16)
                link(TT(r[:, 0, :, C // 2:C].bitcast(F16), r[:, 1, :, 0:C], hi, ALU.subtract))
                m = mark(v.tensor_copy(r[:, 1, :, 0:C].bitcast(F16), r[:, 0, :, 0:C].bitcast(F16)))
                for k in range(TOPK):
                    m = mark(v.tensor_copy(r[:, k, :, C], top[:, k, :]))
                    m = mark(v.tensor_copy(r[:, k, :, C + 1].bitcast(I32), out_row[:, k, TB * n:TB * n + TB]))
                v.wait_ge(rank_ready[l], n + 1)
                link(TT(pos[:], bank_rk[:, 0:(TB + 1) * E].rearrange("p (t e) -> p t e", e=E),
                        carry[:].unsqueeze(1).to_broadcast([P, TB + 1, E]), ALU.add))
                link(v.tensor_copy(carry[:], pos[:, TB, :]))
                for k in range(TOPK):
                    link(TT(tmp[:], best[:, k], pos[:, 0:TB, :], ALU.mult))
                    link(v.tensor_reduce(slot_f[:, k, :], tmp[:], AX.X, ALU.add))
                v.tensor_copy(slot_ix[:, n % 2], slot_f[:]).then_inc(rows_ready[l], 1)

            def route_start(l):
                link(TS(carry[:], rev[:], -float(REGION), float(E * REGION), ALU.mult, ALU.add))

            def make_table(l):
                v.tensor_copy(fill_ix[0:1, :], carry[0:1, :]).then_inc(fill_ready[l], 1)
                s0 = small[0:1, :]
                v.wait_ge(fill_ready[l], 1)
                link(STT(out=s0[:, 0:E], in0=rev[0:1, :], scalar=float(REGION), in1=carry[0:1, :],
                         op0=ALU.mult, op1=ALU.add))
                link(TS(s0[:, 0:E], s0[:, 0:E], float(SR - 1 - E * REGION), None, ALU.add))
                link(v.tensor_copy(small_i[:], s0[:, 0:E]))
                link(TS(small_i[:], small_i[:], 8, None, ALU.arith_shift_right))
                link(v.tensor_copy(s0[:, 0:E], small_i[:]))
                link(v.tensor_tensor_scan(s0[:, E:2 * E], onesf[0:1, :], s0[:, 0:E], 0.0, ALU.mult, ALU.add))
                link(TS(s0[:, 0:E], s0[:, 0:E], -float(SR), float(REGION), ALU.mult, ALU.add))
                ge = slab_d[0:1, 2800:2800 + SLOTS * E].rearrange("p (i e) -> p i e", e=E)
                g2 = slab_d[0:1, 3500:3500 + SLOTS * E].rearrange("p (i e) -> p i e", e=E)
                rowf = slab_d[0:1, 4200:4200 + SLOTS]
                shape = [1, SLOTS, E]
                link(TT(ge, tile_no[:].unsqueeze(2).to_broadcast(shape),
                        s0[:, E:2 * E].unsqueeze(1).to_broadcast(shape), ALU.is_ge))
                link(TT(g2, ge, s0[:, 0:E].unsqueeze(1).to_broadcast(shape), ALU.mult))
                link(v.tensor_reduce(rowf, g2, AX.X, ALU.add))
                link(STT(out=rowf, in0=tile_no[:], scalar=float(SR), in1=rowf, op0=ALU.mult, op1=ALU.add))
                link(TS(rowf, rowf, float(E * REGION), None, ALU.min))
                v.tensor_copy(tab_row[:, 0:SLOTS], rowf).then_inc(table_ready[l], 1)
                v.wait_ge(table_ready[l], 1)
                link(v.tensor_reduce(rowf, ge, AX.X, ALU.add))
                link(TS(rowf, rowf, float(E - 1), None, ALU.min))
                v.tensor_copy(tab_expert[:, 0:SLOTS], rowf).then_inc(table_ready[l], 1)

            def weights_low(l):
                for k, (src, hi, lo) in enumerate(((slab_b, w1hi[l], w1lo[l]), (slab_c, w2hi[l], w2lo[l]))):
                    v.wait_ge(hi_ready[l], k + 1)
                    STT(out=lo[:], in0=src[:, 0:E * F], scalar=WS_, in1=hi[:], op0=ALU.mult,
                        op1=ALU.subtract).then_inc(lo_ready[l], 1)

            def experts(l):
                def copy_xt(base, k, first):
                    v.wait_ge(xt_ready[l], base + (k + 1))
                    if not first:
                        v.wait_ge(y_stored[k % UNROLL], stored_round(l, base, k - UNROLL))
                    v.tensor_copy(ring_meta[:, k % UNROLL], ring_rows[:, k % UNROLL, :, C:ROW])
                    v.tensor_copy(ring_xt[:, k % 2], bank_xt[k % 2][:].bitcast(F16)[:, 0:2 * SR]
                                  .rearrange("p (k m) -> p k m", k=2)).then_inc(xt_copied[l], 1)

                def low(base, k):
                    half = FC * SR // 2
                    for q in range(2):
                        at = slice(q * half, (q + 1) * half)
                        v.wait_ge(hhi_ready[l], 2 * base + (2 * k + q + 1))
                        STT(out=ring_hlo[:, k % 2, at], in0=ring_h[:, k % 2, at], scalar=HS,
                            in1=ring_hhi[:, k % 2, at], op0=ALU.mult, op1=ALU.subtract).then_inc(hlo_ready[l], 1)

                def gate_y(base, k):
                    v.wait_ge(y_ready[l], base + (k + 1))
                    for j in range(SUB):
                        ins = TS(ring_y[:, k, j, :], bank_y[k % 2][:, j * C:(j + 1) * C], ring_meta[:, k, j, 0:1],
                                 1.0 / (WS_ * HS), ALU.mult, ALU.mult)
                    ins.then_inc(y_copied[l], 1)

                def step(base, k, first, last):
                    if not (last and k + 2 >= UNROLL):
                        copy_xt(base, k + 2, first and k + 2 < UNROLL)
                    gate_y(base, k)
                    if not (last and k + 1 >= UNROLL):
                        low(base, k + 1)

                for k in range(2):
                    copy_xt(0, k, True)
                low(0, 0)
                for k in range(UNROLL):
                    step(0, k, True, False)
                with v.Fori(UNROLL, N_TAIL, UNROLL) as i0:
                    for k in range(UNROLL):
                        step(i0, k, False, False)
                for k in range(UNROLL):
                    step(N_TAIL, k, False, True)

            def sum_batch(l, n):
                cols = slice(n * TB * C, (n + 1) * TB * C)
                v.wait_ge(ld_y[n], 32 * (l + 1))
                link(TT(slab_t[:, cols], slab_t[:, cols], slab_b[:, cols], ALU.add))
                TT(slab_t[:, cols], slab_t[:, cols], slab_c[:, cols], ALU.add).then_inc(sum_ready[l], 1)

            def norm_tokens():
                for n in range(NBATCH):
                    tiles = list(range(TB * n, TB * n + TB))
                    sum_batch(0, n)
                    v.wait_ge(sum_ready[0], n + 1)
                    token_stats(tiles, LN_EPS_C).then_inc(var1, 1)
                    v.wait_ge(std1, n + 1)
                    link(v.reciprocal(rstd[:], rstd[:]))
                    for j in range(TB):
                        i = TB * n + j
                        TS(tok_b[:, i, :], tok[:, i, :], mv[:, i, 0:1], rstd[:, j:j + 1], ALU.subtract,
                           ALU.mult).then_inc(xn1_ready, 1)
                    for u in range(GPB * n, GPB * n + GPB):
                        v.wait_ge(tp1_copied, 2 * u + 2)
                        m = mark(v.bn_stats(bn_sums[:, u, :], slab_c[:, u * GT * P:(u + 1) * GT * P]))
                v.wait_ge(dve, m)
                link(v.bn_aggr(bn1[:, 0:2], bn_sums[:, 0:NGRP, :]))
                TS(bn1[:, 2:3], bn1[:, 1:2], BN_EPS, None, ALU.add).then_inc(bn1_var, 1)
                v.wait_ge(bn1_std, 1)
                link(v.reciprocal(bn1[:, 2:3], bn1[:, 2:3]))
                link(TT(bn1[:, 2:3], bn1[:, 2:3], par[:, 30:31], ALU.mult))
                link(TT(bn1[:, 3:4], bn1[:, 0:1], bn1[:, 2:3], ALU.mult))
                TT(bn1[:, 3:4], par[:, 31:32], bn1[:, 3:4], ALU.subtract).then_inc(bn1_ready, 1)
                for j in range(NCH):
                    v.wait_ge(conv_copied, j + 1)
                    m = mark(v.bn_stats(bn_sums[:, j, :], slab_b[:, j * CH:(j + 1) * CH]))
                v.wait_ge(dve, m)
                link(v.bn_aggr(bn2[:, 0:2], bn_sums[:, 0:NCH, :]))
                link(TT(bn2[:, 2:3], bn2[:, 1:2], bn2[:, 4:5], ALU.mult))
                link(TT(bn2[:, 2:3], bn2[:, 2:3], bn2[:, 4:5], ALU.mult))
                TS(bn2[:, 2:3], bn2[:, 2:3], BN_EPS, None, ALU.add).then_inc(bn2_var, 1)
                v.wait_ge(bn2_std, 1)
                link(v.reciprocal(bn2[:, 2:3], bn2[:, 2:3]))
                link(TT(bn2[:, 2:3], bn2[:, 2:3], bn2[:, 4:5], ALU.mult))
                link(TT(bn2[:, 2:3], bn2[:, 2:3], par[:, 32:33], ALU.mult))
                link(TT(bn2[:, 3:4], bn2[:, 0:1], bn2[:, 2:3], ALU.mult))
                link(TS(bn2[:, 5:6], par[:, 34:35], -1.0, 1.0, ALU.mult, ALU.add))
                TT(bn2[:, 3:4], par[:, 33:34], bn2[:, 3:4], ALU.subtract).then_inc(bn2_ready, 1)

            def prelu_batch(n):
                def u(j):
                    if j >= 2:
                        v.wait_ge(hr_ready, 2 * j - 2)
                    cols = slice(j * CH, (j + 1) * CH)
                    STT(out=tail[:, j % 2, :], in0=slab_b[:, cols], scalar=bn2[:, 2:3], in1=slab_c[:, cols],
                        op0=ALU.mult, op1=ALU.add).then_inc(u_ready, 1)
                for j in range(CPB * n, CPB * n + CPB):
                    if j == CPB * n:
                        u(j)
                    if j + 1 < CPB * n + CPB:
                        u(j + 1)
                    a = slab_a[:, j * CH:(j + 1) * CH]
                    v.wait_ge(hr_ready, 2 * j + 2)
                    link(STT(out=a, in0=tail[:, 2 + j % 2, :], scalar=par[:, 34:35], in1=a, op0=ALU.mult, op1=ALU.add))
                    STT(out=a, in0=tail[:, 4 + j % 2, :], scalar=bn2[:, 5:6], in1=a, op0=ALU.mult,
                        op1=ALU.add).then_inc(stream[1], 1)

            norm_half(0)
            taps_half(0)
            add_batch(0)
            route_start(0)
            route_batch(0, 0)
            norm_half(1)
            taps_half(1)
            for n in range(1, NBATCH):
                add_batch(n)
                route_batch(0, n)
            make_table(0)
            weights_low(0)
            weights_low(1)
            experts(0)
            norm_tokens()
            bias_low(1)
            v.wait_ge(bn2_ready, 1)
            route_start(1)
            for n in range(NBATCH):
                prelu_batch(n)
                route_batch(1, n)
            make_table(1)
            experts(1)
            for n in range(NBATCH):
                sum_batch(1, n)

        @block.tensor
        def _(pe):
            mm, tr = nc.tensor.matmul, nc.tensor.transpose

            pe.wait_ge(consts, N_CONSTS)
            pe.wait_ge(ld_par, 16 * N_PAR_DMA)
            tr(banks[3][:, 0:35], par_rows[0:35, :], ident[0:35, 0:35]).then_inc(prep_t, 1)
            pe.wait_ge(ld_conv, 16 * N_CONV_DMA)
            tr(banks[2][:, 0:P], wo_raw, ident[:]).then_inc(prep_t, 1)
            pe.wait_ge(ld_gate, 64)
            for l in range(2):
                ins = mm(banks[7][:, l * E:(l + 1) * E], all_mean[:], gate_w[l][:], start=True, stop=True)
            ins.then_inc(prep_t, 1)
            pe.wait_ge(setup_dve, N_SETUP)
            for k in range(3):
                for m in range(3):
                    ins = tr(banks[4 + k][:].bitcast(BF16)[:, m * P:(m + 1) * P], convw_full[:, 3 * k + m, :], identb[:])
                ins.then_inc(convw_tp, 1)
            pe.wait_ge(setup_act, 5)

            def norm_half(h):
                pe.wait_ge(ld_xic[h], 16 * 16)
                for q in (2 * h, 2 * h + 1):
                    c0 = (q % 2) * CH
                    if q >= 2:
                        pe.wait_ge(bn_ready, 2)
                        pe.wait_ge(or_ready, CPB)
                    for g in range(4):
                        ins = mm(bank_stat[q % 2][:, 0:CH], block_mean[:], xic[:, g, h, c0:c0 + CH],
                                 start=(g == 0), stop=(g == 3))
                    ins.then_inc(mean_ready, 1)
                for q in (2 * h, 2 * h + 1):
                    c0 = (q % 2) * CH
                    pe.wait_ge(centred, q + 1)
                    pe.wait_ge(sq_ready, q + 1)
                    for g in range(4):
                        ins = mm(bank_stat[q % 2][:, 0:CH], block_mean[:], sq[:, g, c0:c0 + CH],
                                 start=(g == 0), stop=(g == 3))
                    ins.then_inc(var_ready, 1)

            def taps_half(h):
                pe.wait_ge(xn_ready, 2 * h + 2)
                for r in range(2):
                    if h == 1:
                        pe.wait_ge(or_ready, CPB)
                    for n, k in enumerate([4, 0, 1, 2, 3, 5, 6, 7, 8]):
                        dy, dx = k // 3 - 1, k % 3 - 1
                        y0, y1 = max(RH * r, -dy), min(RH * r + RH, H - dy)
                        x0, x1 = max(0, -dx), min(W, W - dx)
                        xv = xic[:, 0, h, :].rearrange("p (y x) -> p y x", x=W)[:, y0 + dy:y1 + dy, x0 + dx:x1 + dx]
                        yv = bank_dw[r][:, 0:CH].rearrange("p (y x) -> p y x", x=W)[:, y0 - RH * r:y1 - RH * r, x0:x1]
                        ins = mm(yv, diag[:, k, :], xv, start=(n == 0), stop=(n == 8))
                    ins.then_inc(dw_ready, 1)

            def mix_batch(n):
                def z(j):
                    b, r = j // 2, j % 2
                    pe.wait_ge(ld_ycm[b], 64)
                    if j >= 2:
                        pe.wait_ge(zr_ready, j - 1)
                    if j == 0:
                        pe.wait_ge(vare_ready, 2)
                    if j == CPB:
                        pe.wait_ge(vare_ready, 4)
                    mm(bank_z[j % 2][:, 0:CH], mix[:], ycm[:, b, r * CH:r * CH + CH], start=True, stop=True)\
                        .then_inc(z_ready, 1)

                def o(j):
                    pe.wait_ge(zr_ready, j + 1)
                    if j >= 2:
                        pe.wait_ge(or_ready, j - 1)
                    pe.wait_ge(bn_ready, 2 if n == 0 else 7)
                    mm(bank_o[j % 2][:, 0:CH], wo_t[:], zrelu[:, j % 2, :], start=True, stop=True)\
                        .then_inc(o_ready, 1)

                z(CPB * n)
                for j in range(CPB * n, CPB * n + CPB):
                    if j + 1 < CPB * n + CPB:
                        z(j + 1)
                    o(j)

            def route_batch(l, n):
                for u in range(GPB * n, GPB * n + GPB):
                    pe.wait_ge(stream[l], ((u + 1) * GT * P + CH - 1) // CH)
                    if u >= 2:
                        pe.wait_ge(tok_ready[l], u - 1)
                    for m in range(GT):
                        i = u * GT + m
                        xv = slab_a[:, i * P:(i + 1) * P]
                        tr(bank_tp[u % 2][:, m * P:(m + 1) * P], xv, ident[:])
                        ins = mm(bank_lg[:, i * E:(i + 1) * E], xv, gate_w[l][:], start=True, stop=True)
                    ins.then_inc(tp_ready[l], 1)
                pe.wait_ge(chosen_ready[l], n + 1)
                flat = chosen[:].rearrange("p t e -> p (t e)")
                mm(bank_rk[:, 0:(TB + 1) * E], earlier[:], flat, start=True, stop=False)
                for j in range(TB):
                    n_after = TB - j
                    ins = mm(bank_rk[:, (j + 1) * E:(TB + 1) * E].rearrange("p (t e) -> p t e", e=E), onesb[:],
                             chosen[:, j:j + 1, :].to_broadcast([P, n_after, E]), start=False, stop=(j == TB - 1))
                ins.then_inc(rank_ready[l], 1)

            def experts(l):
                pe.wait_ge(table_ready[l], 2)
                if l == 0:
                    pe.wait_ge(lo_ready[0], 2)
                    pe.wait_ge(lo_ready[1], 2)
                    pe.wait_ge(hi_ready[1], 2)
                pe.wait_ge(bias_ready[l], 3 if l == 0 else 1)

                def early(base, k, n=2):
                    return isinstance(base, int) and base + k < n

                def turn(base, k):
                    pe.wait_ge(ld_ring[k % UNROLL], ring_round(l, base, k))
                    if not early(base, k):
                        pe.wait_ge(xt_copied[l], base + (k - 1))
                    for part in range(2):
                        for j in range(SUB):
                            src = ring_rows[:, k % UNROLL, j, part * C // 2:(part + 1) * C // 2].bitcast(F16)
                            at = part * SR + j * P
                            ins = tr(bank_xt[k % 2][:].bitcast(F16)[:, at:at + P], src, ident16[:])
                    ins.then_inc(xt_ready[l], 1)

                def hidden(base, k, e):
                    pe.wait_ge(xt_copied[l], base + (k + 1))
                    xhi, xlo = ring_xt[:, k % 2, 0, :], ring_xt[:, k % 2, 1, :]
                    for c in range(FC):
                        q = c // 2
                        if c % 2 == 0 and not early(base, k):
                            pe.wait_ge(gelu_ready[l], 2 * base + (2 * k + q - 3))
                        at = bass.ds(e * F + c * P, P)
                        hv = bank_h[k % 2][q][:, (c % 2) * SR:(c % 2 + 1) * SR]
                        mm(hv, b1pad[:, at], bias_one[:, 0:1].to_broadcast([P, SR]), start=True, stop=False)
                        mm(hv, w1hi[l][:, at], xhi, start=False, stop=False)
                        mm(hv, w1hi[l][:, at], xlo, start=False, stop=False)
                        ins = mm(hv, w1lo[l][:, at], xhi, start=False, stop=True)
                        if c % 2 == 1:
                            ins.then_inc(h_ready[l], 1)

                def output(base, k, e):
                    if not early(base, k):
                        pe.wait_ge(y_copied[l], base + (k - 1))
                    yv = [bank_y[k % 2][:, j * C:(j + 1) * C] for j in range(SUB)]
                    b2v = b2pad[l][:, bass.ds(e * C, C)]
                    for j in range(SUB):
                        pe.wait_ge(hlo_ready[l], 2 * base + (2 * k + 1))
                        mm(yv[j], bias_two[:], b2v, start=True, stop=False)
                        for c in range(FC):
                            if j == 0 and c == FC // 2:
                                pe.wait_ge(hlo_ready[l], 2 * base + (2 * k + 2))
                            at = bass.ds(e * F + c * P, P)
                            h0 = c * SR + j * P
                            hhi, hlo = ring_hhi[:, k % 2, h0:h0 + P], ring_hlo[:, k % 2, h0:h0 + P]
                            mm(yv[j], hhi, w2hi[l][:, at], start=False, stop=False)
                            mm(yv[j], hhi, w2lo[l][:, at], start=False, stop=False)
                            ins = mm(yv[j], hlo, w2hi[l][:, at], start=False, stop=(c == FC - 1))
                    ins.then_inc(y_ready[l], 1)

                e = table_values(ENG.PE, tab_expert, 0, UNROLL + 1, E - 1)
                turn(0, 0)
                turn(0, 1)
                hidden(0, 0, e[0])
                for k in range(UNROLL):
                    turn(0, k + 2)
                    hidden(0, k + 1, e[k + 1])
                    output(0, k, e[k])
                with pe.Fori(UNROLL, N_TAIL, UNROLL) as i0:
                    e = table_values(ENG.PE, tab_expert, i0, UNROLL + 1, E - 1)
                    for k in range(UNROLL):
                        turn(i0, k + 2)
                        hidden(i0, k + 1, e[k + 1])
                        output(i0, k, e[k])
                e = table_values(ENG.PE, tab_expert, N_TAIL, UNROLL, E - 1)
                for k in range(UNROLL):
                    if k + 2 < UNROLL:
                        turn(N_TAIL, k + 2)
                    if k + 1 < UNROLL:
                        hidden(N_TAIL, k + 1, e[k + 1])
                    output(N_TAIL, k, e[k])

            def norm_tokens():
                for u in range(NGRP):
                    n = u // GPB
                    pe.wait_ge(sum_ready[0], n + 1)
                    if u == 0:
                        pe.wait_ge(y_copied[0], SLOTS)
                    if u >= 2:
                        pe.wait_ge(tp1_copied, 2 * u - 3)
                    for m in range(GT):
                        ins = tr(bank_tp[u % 2][:, m * P:(m + 1) * P], tok[:, u * GT + m, :], ident[:])
                    ins.then_inc(tp1_ready, 1)
                    pe.wait_ge(xn1_ready, (u + 1) * GT)
                    if u >= 2:
                        pe.wait_ge(tp1_copied, 2 * u - 2)
                    for m in range(GT):
                        ins = tr(bank_tn[u % 2][:, m * P:(m + 1) * P], tok_b[:, u * GT + m, :], ident[:])
                    ins.then_inc(tp1_ready, 1)
                for j in range(NCH):
                    b, r = j // 2, j % 2
                    pe.wait_ge(signs_ready, b + 1)
                    if j >= 2:
                        pe.wait_ge(conv_copied, j - 1)
                    for k in range(9):
                        ky, kx = k // 3, k % 3
                        ins = mm(bank_conv[j % 2][:, 0:CH].rearrange("p (y x) -> p y x", x=W), convw_t[:, k, :],
                                 signs[:, b, RH * r + ky:RH * r + ky + RH, kx:kx + W], start=(k == 0), stop=(k == 8))
                    ins.then_inc(conv_ready, 1)

            norm_half(0)
            taps_half(0)
            mix_batch(0)
            route_batch(0, 0)
            norm_half(1)
            taps_half(1)
            for n in range(1, NBATCH):
                mix_batch(n)
                route_batch(0, n)
            experts(0)
            norm_tokens()
            for n in range(NBATCH):
                route_batch(1, n)
            experts(1)
            for u in range(NGRP):
                pe.wait_ge(sum_ready[1], u // GPB + 1)
                if u >= 2:
                    pe.wait_ge(out_ready, u - 1)
                if u == 0:
                    pe.wait_ge(y_copied[1], SLOTS)
                for m in range(GT):
                    ins = tr(bank_tp[u % 2][:, m * P:(m + 1) * P], tok[:, u * GT + m, :], ident[:])
                ins.then_inc(tpo_ready, 1)


_INS = ["x",
        *("L0_conv_" + n for n in ("wdw", "bdw", "gdw", "bedw", "mdw", "vdw", "ws", "bs", "gs", "bes", "ms", "vs",
                                   "wo", "bo", "go", "beo", "mo", "vo")),
        *("L0_ffn_" + n for n in ("gate_w", "gate_b", "w1", "b1", "w2", "b2")),
        *("L1_conv_" + n for n in ("conv_w", "bn1_gamma", "bn1_beta", "bn2_gamma", "bn2_beta", "prelu_a")),
        *("L1_ffn_" + n for n in ("gate_w", "gate_b", "w1", "b1", "w2", "b2"))]


def kernel(**inputs):
    import numpy as _np
    import concourse.bacc as _bacc
    from concourse import mybir as _mybir
    from concourse.bass_utils import run_bass_kernel_spmd as _run

    nc = _bacc.Bacc("TRN2", target_bir_lowering=False, num_devices=1)
    arrays, args = {}, {}
    for name in _INS:
        a = _np.ascontiguousarray(inputs[name])
        arrays[f"in_{name}_dram"] = a
        args[name] = nc.dram_tensor(f"in_{name}_dram", a.shape, _mybir.dt.from_np(a.dtype), kind="ExternalInput").ap()
    out = nc.dram_tensor("out_0_dram", (B, C, H, W), F32, kind="ExternalOutput").ap()
    metaformer_kernel(nc, args, out)
    r = _run(nc, [arrays], core_ids=[0])
    return r.results[0]["out_0_dram"]
```

```python
from contextlib import ExitStack

import concourse.bass as bass
from concourse import mybir

F32 = mybir.dt.float32
F16 = mybir.dt.float16
BF16 = mybir.dt.bfloat16
I32 = mybir.dt.int32
ALU = mybir.AluOpType
ACT = mybir.ActivationFunctionType
AX = mybir.AxisListType

P = 128
B, C, H, W = 8, 128, 24, 24
HW = H * W
T = B * HW
NT = T // P
E, F, TOPK = 8, 512, 2
FC = F // P
CQ = C // 4
RATES = (1, 6, 12, 18)
CONV_GROUPS = 16
GI = C // CONV_GROUPS
CH = HW // 2
NCH = T // CH
RH = H // 2
HALF = B // 4
NBATCH = 4
TB = NT // NBATCH
GT = 3
NGRP = NT // GT
GPB = TB // GT
CPB = NCH // NBATCH
SUB = 2
SR = SUB * P
REGION = T + SR
ROW = C + 2
UNROLL = 4
SLOTS = -(-(T * TOPK // SR + E - 1) // UNROLL) * UNROLL
XS, WS_, HS = 64.0, 64.0, 16.0
LN_EPS_T, LN_EPS_C, BN_EPS = 1e-5, 1e-6, 1e-5
LOW = 32
HP, WP = H + 2, W + 2


def metaformer_kernel(nc, t, out):
    x_cm = t["x"].rearrange("b c h w -> c b (h w)")
    x_ic = t["x"].rearrange("(h b) (g c) y x -> h g b c (y x)", b=4, c=CQ)
    out_cm = out.rearrange("b c h w -> c b (h w)")

    with ExitStack() as ctx:
        def sb(name, shape, dt):
            return ctx.enter_context(nc.sbuf_tensor(name, shape, dt))

        def sem(name):
            return ctx.enter_context(nc.semaphore(name))

        ctx.enter_context(nc.allow_non_contiguous_dma(reason="small parameter tables"))

        routed = [nc.dram_tensor(f"routed{l}", (E * REGION + SR, ROW), F32).ap() for l in range(2)]
        expert_out = [nc.dram_tensor(f"expert_out{l}", (TOPK * T, C), F32).ap() for l in range(2)]

        slab_a = sb("slab_a", [P, T], F32)
        slab_t = sb("slab_t", [P, T], F32)
        slab_b = sb("slab_b", [P, T], F32)
        slab_c = sb("slab_c", [P, T], F32)
        slab_d = sb("slab_d", [P, T], F32)
        rows = sb("rows", [P, 2 * TOPK * TB * ROW], F32)
        rows_v = rows[:].rearrange("p (n k t w) -> p n k t w", n=2, k=TOPK, w=ROW)
        w1hi = [sb(f"w1hi{l}", [P, E * F], F16) for l in range(2)]
        w1lo = [sb(f"w1lo{l}", [P, E * F], F16) for l in range(2)]
        w2hi = [sb(f"w2hi{l}", [P, E * F], F16) for l in range(2)]
        w2lo = [sb(f"w2lo{l}", [P, E * F], F16) for l in range(2)]
        b1_cols = sb("b1_cols", [P, 2 * E * FC], F32)
        b2_raw = sb("b2_raw", [P, 2 * E * C], F32)
        b2pad = sb("b2pad", [P, 2 * E * C], F16)

        tok = slab_t[:].rearrange("p (t c) -> p t c", c=C)
        tok_b = slab_b[:].rearrange("p (t c) -> p t c", c=C)
        tok_c = slab_c[:].rearrange("p (t c) -> p t c", c=C)
        xic = slab_b[:].rearrange("p (g h n) -> p g h n", g=4, h=HALF)
        yic = slab_c[:].rearrange("p (g h n) -> p g h n", g=4, h=HALF)
        sq = slab_d[:, T // 2:T].rearrange("p (g n) -> p g n", g=4)
        ycm = slab_d[:].rearrange("p (b n) -> p b n", b=B)
        std = slab_t[:, T - 2 * HW:T].rearrange("p (q n) -> p q n", n=CH)
        sign_words = B * HP * WP // 2
        signs = slab_d[:, 0:sign_words].bitcast(BF16).rearrange("p (b y x) -> p b y x", b=B, y=HP)
        diag = [w[:, 4096 - 9 * P * 2:4096].bitcast(F32).rearrange("p (t m) -> p t m", m=P)
                for w in (w2lo[1], w1lo[1])]
        b1_rows = w1lo[1][0:2 * E * FC, 1280:1280 + 2 * P].bitcast(F32)
        zrelu = w2hi[1][:, 0:4 * CH].bitcast(F32).rearrange("p (s n) -> p s n", n=CH)
        orelu = w2hi[1][:, 4 * CH:4 * CH + 2 * CPB * CH].bitcast(F32).rearrange("p (s n) -> p s n", n=CH)
        wo_raw = w1hi[1][:, 0:2 * P].bitcast(F32)
        convw = w1hi[1][:, 2 * P:2 * P + 2 * GI * 9].bitcast(F32).rearrange("p (i t) -> p i t", t=9)
        convw_sign = w1hi[1][:, 1024:1024 + GI * 9].bitcast(BF16)
        convw_full = w1hi[1][:, 2048:2048 + 9 * P].bitcast(BF16).rearrange("p (t m) -> p t m", m=P)
        par_rows = w1lo[1][0:40, 0:2 * P].bitcast(F32)
        convw_abs = w1lo[1][:, 512:512 + 2 * GI * 9].bitcast(F32)
        group_mask = w1lo[1][:, 1024:1024 + P].bitcast(BF16)
        ring_rows = slab_c[:, 0:UNROLL * SUB * ROW].rearrange("p (s j w) -> p s j w", j=SUB, w=ROW)
        ring_y = slab_c[:, 2048:2048 + UNROLL * SUB * C].rearrange("p (s j c) -> p s j c", j=SUB, c=C)
        ring_xt = slab_c[:, 3200:3200 + 2 * SR].bitcast(F16).rearrange("p (s k m) -> p s k m", k=2, m=SR)
        ring_h = slab_b[:, 0:2 * FC * SR].rearrange("p (s n) -> p s n", n=FC * SR)
        ring_hhi = slab_b[:, 2048:2048 + FC * SR].bitcast(F16).rearrange("p (s n) -> p s n", n=FC * SR)
        ring_hlo = slab_b[:, 3072:3072 + FC * SR].bitcast(F16).rearrange("p (s n) -> p s n", n=FC * SR)

        ident = sb("ident", [P, P], F32)
        ident16 = sb("ident16", [P, P], F16)
        identb = sb("identb", [P, P], BF16)
        earlier = sb("earlier", [P, P], BF16)
        onesb = sb("onesb", [P, P], BF16)
        bias_two = sb("bias_two", [P, P], F16)
        onesf = sb("onesf", [1, E], F32)
        block_mean = sb("block_mean", [P, P], F32)
        all_mean = sb("all_mean", [P, P], F32)
        mix = sb("mix", [P, P], F32)
        wo_t = sb("wo_t", [P, P], F32)
        convw_t = sb("convw_t", [P, 9, P], BF16)
        out_row = sb("out_row", [P, TOPK, NT], I32)
        rev = sb("rev", [P, E], F32)
        tile_no = sb("tile_no", [1, SLOTS], F32)
        fill = sb("fill", [P, SUB, ROW], F32)
        ring_meta = sb("ring_meta", [P, UNROLL, SUB, 2], F32)
        ring_b1 = sb("ring_b1", [P, UNROLL, FC], F32)
        par = sb("par", [P, 40], F32)
        wdw = sb("wdw", [P, 4, 9], F32)
        ws_b = sb("ws_b", [P, 4], F32)
        fold = sb("fold", [P, 16], F32)
        gate_w = [sb(f"gate_w{l}", [P, E], F32) for l in range(2)]
        gate_b = [sb(f"gate_b{l}", [P, E], F32) for l in range(2)]
        sums = sb("sums", [P, NT, 6], F32)
        mv = sb("mv", [P, NT, 2], F32)
        rstd = sb("rstd", [P, 2, TB], F32)
        rstdx = sb("rstdx", [P, 2, TB], F32)
        shift = sb("shift", [P, 2, TB], F32)
        prob = sb("prob", [P, TB, E], F32)
        tmp = sb("tmp", [P, TB, E], F32)
        best = sb("best", [P, TOPK, TB, E], F32)
        top = sb("top", [P, TOPK, TB], F32)
        red = sb("red", [P, TB], F32)
        chosen = sb("chosen", [P, TB + 1, E], BF16)
        pos = sb("pos", [P, TB + 1, E], F32)
        carry = sb("carry", [P, E], F32)
        slot_f = sb("slot_f", [P, TOPK, TB], F32)
        slot_ix = sb("slot_ix", [P, 2, TOPK, TB], I32)
        fill_ix = sb("fill_ix", [1, E], I32)
        small = sb("small", [P, 16], F32)
        small_i = sb("small_i", [1, E], I32)
        tab_expert = sb("tab_expert", [1, SLOTS + UNROLL + 1], I32)
        tab_row = sb("tab_row", [1, SLOTS + UNROLL + 1], I32)
        bn_sums = sb("bn_sums", [P, NCH, 6], F32)
        bn1 = sb("bn1", [P, 4], F32)
        bn2 = sb("bn2", [P, 8], F32)

        banks = [ctx.enter_context(nc.psum_tensor(f"bank{i}", [P, 512], F32)) for i in range(8)]
        bank_stat = bank_z = (banks[0], banks[1])
        bank_dw = bank_o = bank_conv = (banks[2], banks[3])
        bank_tp = (banks[4], banks[5])
        bank_tn = (banks[0], banks[1])
        bank_lg, bank_rk = banks[6], banks[7]
        bank_xt, bank_y = (banks[0], banks[1]), (banks[2], banks[3])
        bank_h = ((banks[4], banks[5]), (banks[6], banks[7]))

        consts = sem("consts"); mean_blocks = sem("mean_blocks"); mask_ready = sem("mask_ready")
        raw_zero = sem("raw_zero"); b2_high = sem("b2_high"); b2_ready = sem("b2_ready")
        par_ready = sem("par_ready"); diag_ready = sem("diag_ready")
        ld_par = sem("ld_par"); ld_branch = sem("ld_branch"); ld_wdw = sem("ld_wdw"); ld_ws = sem("ld_ws"); ld_wo = sem("ld_wo"); ld_conv = sem("ld_conv"); ld_gate = sem("ld_gate")
        ld_xic = [sem(f"ld_xic{h}") for h in range(HALF)]
        ld_x = sem("ld_x")
        ld_b1 = sem("ld_b1"); ld_b2 = sem("ld_b2")
        ld_w = [[sem(f"ld_w{k}_{l}") for k in (1, 2)] for l in range(2)]
        hi_ready = [sem(f"hi_ready{l}") for l in range(2)]
        lo_ready = [sem(f"lo_ready{l}") for l in range(2)]
        dve = sem("dve")
        prep_t = sem("prep_t"); setup_dve = sem("setup_dve"); setup_act = sem("setup_act")
        setup_sqrt = sem("setup_sqrt"); setup_var = sem("setup_var"); convw_tp = sem("convw_tp")
        mean_ready = sem("mean_ready"); centred = sem("centred"); sq_ready = sem("sq_ready")
        var_ready = sem("var_ready"); vare_ready = sem("vare_ready"); std_ready = sem("std_ready")
        xn_ready = sem("xn_ready"); dw_ready = sem("dw_ready"); taps_ready = sem("taps_ready")
        bn_ready = sem("bn_ready")
        ld_ycm = [sem(f"ld_ycm{b}") for b in range(B)]
        z_ready = sem("z_ready"); zr_ready = sem("zr_ready"); o_ready = sem("o_ready")
        or_ready = sem("or_ready")
        stream = [sem(f"stream{l}") for l in range(2)]
        tp_ready = [sem(f"tp_ready{l}") for l in range(2)]
        tok_ready = [sem(f"tok_ready{l}") for l in range(2)]
        tvar = [sem(f"tvar{l}") for l in range(2)]
        tstd = [sem(f"tstd{l}") for l in range(2)]
        lg_shift = [sem(f"lg_shift{l}") for l in range(2)]
        lg_exp = [sem(f"lg_exp{l}") for l in range(2)]
        chosen_ready = [sem(f"chosen_ready{l}") for l in range(2)]
        rank_ready = [sem(f"rank_ready{l}") for l in range(2)]
        tok_scale = [sem(f"tok_scale{l}") for l in range(2)]
        xn_tok = [sem(f"xn_tok{l}") for l in range(2)]
        xhi_ready = [sem(f"xhi_ready{l}") for l in range(2)]
        rows_ready = [sem(f"rows_ready{l}") for l in range(2)]
        scattered = [[sem(f"scattered{l}_{n}") for n in range(2)] for l in range(2)]
        fill_ready = [sem(f"fill_ready{l}") for l in range(2)]
        filled = [sem(f"filled{l}") for l in range(2)]
        table_ready = [sem(f"table_ready{l}") for l in range(2)]
        ld_ring = [sem(f"ld_ring{s}") for s in range(UNROLL)]
        xt_ready = [sem(f"xt_ready{l}") for l in range(2)]
        xt_copied = [sem(f"xt_copied{l}") for l in range(2)]
        h_ready = [sem(f"h_ready{l}") for l in range(2)]
        gelu_ready = [sem(f"gelu_ready{l}") for l in range(2)]
        hhi_ready = [sem(f"hhi_ready{l}") for l in range(2)]
        hlo_ready = [sem(f"hlo_ready{l}") for l in range(2)]
        scatter_turn = sem("scatter_turn")
        y_ready = [sem(f"y_ready{l}") for l in range(2)]
        y_copied = [sem(f"y_copied{l}") for l in range(2)]
        y_stored = [sem(f"y_stored{s}") for s in range(UNROLL)]
        ld_y = [[sem(f"ld_y{k}_{n}") for n in range(NBATCH)] for k in range(TOPK)]
        sum_ready = [sem(f"sum_ready{l}") for l in range(2)]
        var1 = sem("var1"); scale1 = sem("scale1"); std1 = sem("std1"); xn1_ready = sem("xn1_ready")
        tp1_ready = sem("tp1_ready"); tp1_copied = sem("tp1_copied")
        bn1_var = sem("bn1_var"); bn1_std = sem("bn1_std"); bn1_ready = sem("bn1_ready")
        signs_zero = sem("signs_zero"); signs_ready = sem("signs_ready")
        conv_ready = sem("conv_ready"); conv_copied = sem("conv_copied")
        bn2_var = sem("bn2_var"); bn2_std = sem("bn2_std"); bn2_ready = sem("bn2_ready")
        u_ready = sem("u_ready"); relu_ready = sem("relu_ready"); prelu_ready = sem("prelu_ready")
        tpo_ready = sem("tpo_ready"); out_ready = sem("out_ready"); stored = sem("stored")

        ENG = mybir.EngineType
        N_TAIL = SLOTS - UNROLL

        def table_values(engine, table, base, n, most):
            _, values = nc.values_load_multi_w_load_instructions(
                table[0:1, bass.ds(base, n)], engines=[engine], min_val=0, max_val=most,
                skip_runtime_bounds_check_because="the table's entries are clamped to this range")
            return values

        def ring_round(l, base, k):
            return (base + (l * SLOTS + UNROLL * (k // UNROLL))) * (16 // UNROLL) + 16

        def stored_round(l, base, k):
            return (base + (l * SLOTS + UNROLL * (k // UNROLL))) * (16 * SUB // UNROLL) + 16 * SUB

        N_CONSTS = 19
        N_BRANCH, N_PAR = 5 + 5, 5 + 5
        N_SETUP = 1 + 2 + 9

        N_PE, N_DVE = 2, 2
        BN_ORDER = (0, 2, 3, 1)
        N_BN = 2 * N_PE + N_DVE

        def normed(h, g):
            return N_BN * h + sum(2 if m < N_PE else 1 for m in BN_ORDER[:BN_ORDER.index(g) + 1])

        def scatter_goal(n):
            return 16 * TOPK * TB * (n // 2 + 1)

        block = ctx.enter_context(nc.Block())

        @block.sync
        def _(sp):
            for h in range(HALF):
                for b in range(4):
                    sp.dma_start(xic[CQ * b:CQ * b + CQ, :, h, :],
                                 x_ic[h, :, b].rearrange("g c n -> c g n")).then_inc(ld_xic[h], 16)
            for i, name in enumerate(("L0_conv_bo", "L0_conv_go", "L0_conv_beo", "L0_conv_mo", "L0_conv_vo",
                                      "L1_conv_bn1_gamma", "L1_conv_bn1_beta", "L1_conv_bn2_gamma",
                                      "L1_conv_bn2_beta", "L1_conv_prelu_a")):
                sp.dma_start(par_rows[25 + i:26 + i, :], t[name].rearrange("(a c) -> a c", a=1)).then_inc(ld_par, 16)
            sp.dma_start(convw, t["L1_conv_conv_w"].rearrange("o i y x -> o i (y x)")).then_inc(ld_conv, 16)
            sp.dma_start(wo_raw, t["L0_conv_wo"].rearrange("o i a b -> o (i a b)")).then_inc(ld_wo, 16)
            for l in range(2):
                sp.dma_start(gate_w[l][:], t[f"L{l}_ffn_gate_w"]).then_inc(ld_gate, 16)
                sp.dma_start(gate_b[l][:], t[f"L{l}_ffn_gate_b"].rearrange("(a e) -> a e", a=1)
                             .to_broadcast([P, E])).then_inc(ld_gate, 16)
            sp.wait_ge(raw_zero, 1)
            for l in range(2):
                for q in (0, LOW):
                    sp.dma_start(b2_raw[q:q + 1, l * E * C:(l + 1) * E * C],
                                 t[f"L{l}_ffn_b2"].rearrange("(a e) d -> a (e d)", a=1)).then_inc(ld_b2, 16)
            for b in range(0, B, 2):
                sp.dma_start(slab_a[:, b * HW:(b + 2) * HW].rearrange("p (b n) -> p b n", b=2),
                             x_cm[:, b:b + 2, :]).then_inc(ld_x, 16)

            def shuffle(h):
                for g in BN_ORDER:
                    sp.wait_ge(bn_ready, normed(h, g))
                    for b in range(4):
                        sp.dma_start(ycm[CQ * g:CQ * g + CQ, 4 * h + b, :],
                                     yic[CQ * b:CQ * b + CQ, g, h, :]).then_inc(ld_ycm[4 * h + b], 16)

            def load_w1(l, slab):
                sp.dma_start(slab[:, 0:E * F].rearrange("p (e f) -> p e f", e=E),
                             t[f"L{l}_ffn_w1"].rearrange("e d f -> d e f")).then_inc(ld_w[l][0], 16)

            def load_w2(l, slab):
                sp.dma_start(slab[:, 0:E * F].rearrange("p (e c d) -> p e c d", e=E, c=FC),
                             t[f"L{l}_ffn_w2"].rearrange("e (c p) d -> p e c d", p=P)).then_inc(ld_w[l][1], 16)

            def load_weights():
                sp.wait_ge(taps_ready, 2 * N_DVE)
                sp.wait_ge(dw_ready, 4 * N_PE)
                load_w1(0, slab_b)
                for b in range(B):
                    sp.wait_ge(ld_ycm[b], 64)
                load_w2(0, slab_c)
                sp.wait_ge(z_ready, NCH)
                load_w1(1, slab_d)

            def fill_padding(l):
                sp.wait_ge(fill_ready[l], 1)
                _, ends = nc.values_load_multi_w_load_instructions(
                    fill_ix[0:1, :], engines=[ENG.SP], min_val=0, max_val=E * REGION - SR,
                    skip_runtime_bounds_check_because="a region's rows end at least a slot tile before it does")
                sp.dma_start(routed[l][E * REGION:E * REGION + SR, :].rearrange("(j p) w -> p j w", p=P),
                             fill[:]).then_inc(filled[l], 16)
                for e in range(E):
                    sp.dma_start(routed[l][bass.ds(ends[e], SR), :].rearrange("(j p) w -> p j w", p=P), fill[:])\
                      .then_inc(filled[l], 16)

            def expert_loads(l):
                sp.wait_ge(table_ready[l], 2)
                for n in range(2):
                    sp.wait_ge(scattered[l][n], scatter_goal(NBATCH - 2 + n))
                sp.wait_ge(filled[l], 16 * (E + 1))
                sp.wait_ge(lo_ready[0], 2)

                def step(base, k, row, first):
                    if not first:
                        sp.wait_ge(xt_copied[l], base + (k - UNROLL + 1))
                    sp.dma_start(ring_rows[:, k], routed[l][bass.ds(row, SR), :].rearrange("(j p) w -> p j w", p=P))\
                      .then_inc(ld_ring[k], 16)

                first_rows = table_values(ENG.SP, tab_row, 0, UNROLL, E * REGION)
                for k in range(UNROLL):
                    step(0, k, first_rows[k], True)
                with sp.Fori(UNROLL, SLOTS, UNROLL) as i0:
                    row = table_values(ENG.SP, tab_row, i0, UNROLL, E * REGION)
                    for k in range(UNROLL):
                        step(i0, k, row[k], False)

            def load_outputs(l):
                for s in range(UNROLL):
                    sp.wait_ge(y_stored[s], stored_round(l, SLOTS, -1))
                pieces = [(k, n) for n in range(NBATCH) for k in range(TOPK)]
                for k, n in pieces if l == 0 else sorted(pieces):
                    src = expert_out[l][k * T + n * TB * P:k * T + (n + 1) * TB * P, :]
                    sp.dma_start((tok_b, tok_c)[k][:, n * TB:(n + 1) * TB, :],
                                 src.rearrange("(t p) c -> p t c", p=P)).then_inc(ld_y[k][n], 16)

            shuffle(0)
            shuffle(1)
            load_weights()
            sp.wait_ge(hi_ready[0], 1)
            sp.wait_ge(lo_ready[0], 1)
            load_w2(1, slab_b)
            fill_padding(0)
            expert_loads(0)
            load_outputs(0)
            fill_padding(1)
            expert_loads(1)
            load_outputs(1)
            for n in range(NBATCH):
                sp.wait_ge(out_ready, GPB * (n + 1))
                sp.dma_start(out_cm[:, 2 * n:2 * n + 2, :],
                             slab_a[:, 2 * n * HW:(2 * n + 2) * HW].rearrange("p (b n) -> p b n", b=2)).then_inc(stored, 16)
            sp.wait_ge(stored, 16 * NBATCH)

        @block.gpsimd
        def _(pool):
            count = [0]

            def const(ins):
                ins.then_inc(consts, 1)
                count[0] += 1

            pool.memset(block_mean[:], 0.0).then_inc(mean_blocks, 1)
            for b in range(4):
                pool.wait_ge(mean_blocks, 1 + b)
                pool.memset(block_mean[CQ * b:CQ * b + CQ, CQ * b:CQ * b + CQ], 1.0 / C).then_inc(mean_blocks, 1)
            pool.wait_ge(mean_blocks, 5)
            for m in (ident, ident16, identb):
                const(pool.memset(m[:], 0.0))
            const(pool.memset(earlier[:], 1.0))
            pool.wait_ge(consts, 4)
            for m in (ident, ident16, identb):
                const(pool.affine_select(out=m[:], in_=m[:], compare_op=ALU.not_equal, fill=1.0, base=0,
                                         pattern=[[-1, P]], channel_multiplier=1))
            const(pool.affine_select(out=earlier[:], in_=earlier[:], compare_op=ALU.is_gt, fill=0.0, base=0,
                                     pattern=[[1, P]], channel_multiplier=-1))
            const(pool.memset(onesb[:], 1.0))
            const(pool.memset(bias_two[:], HS))
            const(pool.memset(all_mean[:], 1.0 / C))
            const(pool.memset(onesf[:], 1.0))
            const(pool.memset(chosen[:], 0.0))
            for k in range(TOPK):
                const(pool.iota(out_row[:, k, :], pattern=[[P, NT]], base=k * T, channel_multiplier=1))
            const(pool.iota(rev[:], pattern=[[-1, E]], base=E, channel_multiplier=0,
                            allow_small_or_imprecise_dtypes=True))
            const(pool.iota(tile_no[:], pattern=[[1, SLOTS]], base=0, channel_multiplier=0,
                            allow_small_or_imprecise_dtypes=True))
            const(pool.memset(fill[:, :, 0:C + 1], 0.0))
            const(pool.iota(fill[:, :, C + 1].bitcast(I32), pattern=[[P, SUB]], base=TOPK * T, channel_multiplier=1))
            assert count[0] == N_CONSTS
            pool.memset(b2_raw[:], 0.0).then_inc(raw_zero, 1)
            for i, name in enumerate(("bdw", "gdw", "bedw", "mdw", "vdw")):
                pool.dma_start(par_rows[4 * i:4 * i + 4, :].rearrange("r (b c) -> r b c", b=4),
                             t["L0_conv_" + name].unsqueeze(1).to_broadcast([4, 4, CQ])).then_inc(ld_branch, 16)
            for i, name in enumerate(("bs", "gs", "bes", "ms", "vs")):
                pool.dma_start(par_rows[20 + i:21 + i, :].rearrange("r (c o) -> r c o", o=4),
                             t["L0_conv_" + name].rearrange("(a b o) -> a b o", a=1, b=1)
                             .to_broadcast([1, CQ, 4])).then_inc(ld_branch, 16)
            for l in range(2):
                pool.dma_start(b1_rows[l * E * FC:(l + 1) * E * FC, :],
                             t[f"L{l}_ffn_b1"].rearrange("e (c p) -> (e c) p", p=P)).then_inc(ld_b1, 16)
            for g in range(4):
                pool.dma_start(ws_b[CQ * g:CQ * g + CQ, :],
                             t["L0_conv_ws"][:, g:g + 1, 0, 0].rearrange("o g -> g o").to_broadcast([CQ, 4]))\
                  .then_inc(ld_ws, 16)

            pool.wait_ge(consts, N_CONSTS)
            gm = group_mask.rearrange("p (g i) -> p g i", i=GI)
            pool.affine_select(out=gm, in_=onesb[:].rearrange("p (g i) -> p g i", i=GI), compare_op=ALU.is_ge,
                               fill=0.0, base=0, pattern=[[-GI, CONV_GROUPS], [0, GI]],
                               channel_multiplier=1).then_inc(mask_ready, 1)
            pool.wait_ge(mask_ready, 1)
            pool.affine_select(out=gm, in_=gm, compare_op=ALU.is_ge, fill=0.0, base=GI - 1,
                               pattern=[[GI, CONV_GROUPS], [0, GI]], channel_multiplier=-1).then_inc(mask_ready, 1)

            def scatter_rows(l):
                for n in range(NBATCH):
                    pool.wait_ge(rows_ready[l], n + 1)
                    for j in range(TB):
                        for k in range(TOPK):
                            pool.indirect_dma_start(
                                routed[l], bass.IndirectOffsetOnAxis(ap=slot_ix[:, n % 2, k, j:j + 1], axis=0),
                                rows_v[:, n % 2, k, j, :], None, bounds_check=E * REGION - 1,
                                oob_is_err=False).then_inc(scattered[l][n % 2], 16)

            def scatter_outputs(l):
                def step(i, s, bound):
                    pool.wait_ge(y_copied[l], i + 1)
                    pool.sem_inc(scatter_turn, 1)
                    for j in range(SUB):
                        pool.indirect_dma_start(
                            expert_out[l],
                            bass.IndirectOffsetOnAxis(ap=ring_meta[:, s, j, 1:2].bitcast(I32), axis=0),
                            ring_y[:, s, j, :], None, bounds_check=bound,
                            oob_is_err=False).then_inc(y_stored[s], 16)
                with pool.register(f"last_row{l}") as last_row:
                    pool.reg_mov(last_row, TOPK * T - 1)
                    bound = pool.snap(last_row)
                    with pool.Fori(0, SLOTS, UNROLL) as i0:
                        for k in range(UNROLL):
                            step(i0 + k, k, bound)

            scatter_rows(0)
            scatter_outputs(0)
            pool.memset(slab_d[:, 0:sign_words], 0.0).then_inc(signs_zero, 1)
            scatter_rows(1)
            scatter_outputs(1)

        @block.scalar
        def _(sc):
            for b in range(4):
                sc.dma_start(wdw[CQ * b:CQ * b + CQ, :, :],
                             t["L0_conv_wdw"].rearrange("g c a y x -> c g (a y x)")).then_inc(ld_wdw, 16)
            def prepare_0():
                sc.wait_ge(setup_var, 1)
                nc.scalar.activation(fold[:, 8:15], fold[:, 0:7], ACT.Sqrt).then_inc(setup_sqrt, 1)
                sc.wait_ge(prep_t, 2)
                nc.scalar.activation(wo_t[:], banks[5][:, 0:P], ACT.Copy).then_inc(setup_act, 1)
                sc.wait_ge(ld_conv, 16)
                nc.scalar.activation(convw_sign.rearrange("p (i t) -> p i t", t=9), convw, ACT.Sign).then_inc(setup_act, 1)

            def prepare_1():
                for k in range(3):
                    sc.wait_ge(convw_tp, k + 1)
                    nc.scalar.activation(convw_t[:, 3 * k:3 * k + 3, :],
                                         banks[4 + k][:].bitcast(BF16)[:, 0:3 * P].rearrange("p (t m) -> p t m", m=P),
                                         ACT.Copy).then_inc(setup_act, 1)
                sc.wait_ge(raw_zero, 1)
                sc.wait_ge(ld_b2, 64)
                nc.scalar.activation(b2pad[:], b2_raw[:], ACT.Copy, scale=WS_).then_inc(b2_high, 1)

            def norm_half(h):
                for q in (2 * h, 2 * h + 1):
                    c0 = (q % 2) * CH
                    sc.wait_ge(centred, q + 1)
                    nc.scalar.activation(sq[:, :, c0:c0 + CH], xic[:, :, h, c0:c0 + CH], ACT.Square)\
                      .then_inc(sq_ready, 1)

            def norm_half_end(h):
                for q in (2 * h, 2 * h + 1):
                    sc.wait_ge(vare_ready, q + 1)
                    nc.scalar.activation(std[:, q, :], std[:, q, :], ACT.Sqrt).then_inc(std_ready, 1)

            def bn(h, g):
                if h == 0:
                    sc.wait_ge(par_ready, 1)
                if g < N_PE:
                    for r in range(2):
                        sc.wait_ge(dw_ready, 2 * N_PE * h + 2 * g + r + 1)
                        nc.scalar.activation(yic[:, g, h, r * CH:r * CH + CH], bank_dw[r][:, 0:CH], ACT.Relu,
                                             bias=par[:, 8 + g:9 + g], scale=par[:, 4 + g:5 + g]).then_inc(bn_ready, 1)
                else:
                    sc.wait_ge(taps_ready, N_DVE * h + g - N_PE + 1)
                    nc.scalar.activation(yic[:, g, h, :], yic[:, g, h, :], ACT.Relu,
                                         bias=par[:, 8 + g:9 + g], scale=par[:, 4 + g:5 + g]).then_inc(bn_ready, 1)

            def mix_batch(n):
                def z(j):
                    sc.wait_ge(z_ready, j + 1)
                    if j >= 2:
                        sc.wait_ge(o_ready, j - 1)
                    nc.scalar.activation(zrelu[:, j % 2, :], bank_z[j % 2][:, 0:CH], ACT.Relu,
                                         bias=par[:, 22:23], scale=par[:, 21:22]).then_inc(zr_ready, 1)

                def o(j):
                    sc.wait_ge(o_ready, j + 1)
                    nc.scalar.activation(orelu[:, j % CPB, :], bank_o[j % 2][:, 0:CH], ACT.Relu,
                                         bias=par[:, 27:28], scale=par[:, 26:27]).then_inc(or_ready, 1)

                z(CPB * n)
                if n >= 1:
                    sc.wait_ge(stream[0], n)
                for j in range(CPB * n, CPB * n + CPB):
                    if j + 1 < CPB * n + CPB:
                        z(j + 1)
                    o(j)

            def route_batch(l, n):
                for u in range(GPB * n, GPB * n + GPB):
                    sc.wait_ge(tp_ready[l], u + 1)
                    nc.scalar.activation(slab_t[:, u * GT * P:(u + 1) * GT * P], bank_tp[u % 2][:, 0:GT * P],
                                         ACT.Copy).then_inc(tok_ready[l], 1)
                if l == 1 and n + 1 < NBATCH:
                    prelu_batch(n + 1)
                sc.wait_ge(tvar[l], n + 1)
                nc.scalar.activation(rstd[:, n % 2], rstd[:, n % 2], ACT.Sqrt).then_inc(tstd[l], 1)
                sc.wait_ge(lg_shift[l], n + 1)
                nc.scalar.activation(prob[:], prob[:], ACT.Exp).then_inc(lg_exp[l], 1)
                r = rows_v[:, n % 2]
                if n >= 2:
                    sc.wait_ge(scattered[l][n % 2], scatter_goal(n - 2))
                sc.wait_ge(tok_scale[l], n + 1)
                for j in range(TB):
                    ins = nc.scalar.activation(r[:, 1, j, 0:C], tok[:, TB * n + j, :], ACT.Identity,
                                               bias=shift[:, n % 2, j:j + 1], scale=rstdx[:, n % 2, j:j + 1])
                ins.then_inc(xn_tok[l], 1)
                sc.wait_ge(xn_tok[l], n + 1)
                nc.scalar.activation(r[:, 0, :, 0:C // 2].bitcast(F16), r[:, 1, :, 0:C], ACT.Copy)\
                  .then_inc(xhi_ready[l], 1)

            def weights_high(l, k):
                src, dst = (((slab_b, w1hi[0]), (slab_c, w2hi[0])), ((slab_d, w1hi[1]), (slab_b, w2hi[1])))[l][k]
                sc.wait_ge(ld_w[l][k], 16)
                if l == 1 and k == 0:
                    sc.wait_ge(tp_ready[0], NGRP)
                nc.scalar.activation(dst[:], src[:, 0:E * F], ACT.Copy, scale=WS_).then_inc(hi_ready[l], 1)

            def experts(l):
                def step(base, k, first):
                    half = FC * SR // 2
                    for q in range(2):
                        sc.wait_ge(h_ready[l], 2 * base + (2 * k + q + 1))
                        if not (first and k < 2):
                            sc.wait_ge(hlo_ready[l], 2 * base + (2 * k + q - 3))
                        for c in (2 * q, 2 * q + 1):
                            ins = nc.scalar.activation(ring_h[:, k % 2, c * SR:(c + 1) * SR],
                                                       bank_h[k % 2][q][:, (c % 2) * SR:(c % 2 + 1) * SR], ACT.Gelu,
                                                       bias=ring_b1[:, k % UNROLL, c:c + 1], scale=1.0 / (XS * WS_))
                        ins.then_inc(gelu_ready[l], 1)
                    for q in range(2):
                        sc.wait_ge(gelu_ready[l], 2 * base + (2 * k + q + 1))
                        if not (first and k < 2):
                            sc.wait_ge(y_ready[l], base + (k - 1))
                        nc.scalar.activation(ring_hhi[:, k % 2, q * half:(q + 1) * half],
                                             ring_h[:, k % 2, q * half:(q + 1) * half], ACT.Copy, scale=HS)\
                          .then_inc(hhi_ready[l], 1)

                for k in range(UNROLL):
                    step(0, k, True)
                with sc.Fori(UNROLL, SLOTS, UNROLL) as i0:
                    for k in range(UNROLL):
                        step(i0, k, False)

            def norm_tokens():
                for n in range(NBATCH):
                    sc.wait_ge(var1, n + 1)
                    nc.scalar.activation(rstd[:, n % 2], rstd[:, n % 2], ACT.Sqrt).then_inc(std1, 1)
                    sc.wait_ge(scale1, n + 1)
                    for j in range(TB):
                        nc.scalar.activation(tok_b[:, TB * n + j, :], tok[:, TB * n + j, :], ACT.Identity,
                                             bias=shift[:, n % 2, j:j + 1], scale=rstd[:, n % 2, j:j + 1])\
                          .then_inc(xn1_ready, 1)
                    for u in range(GPB * n, GPB * n + GPB):
                        cols = slice(u * GT * P, (u + 1) * GT * P)
                        sc.wait_ge(tp1_ready, 2 * u + 1)
                        nc.scalar.activation(slab_a[:, cols], bank_tp[u % 2][:, 0:GT * P], ACT.Copy).then_inc(tp1_copied, 1)
                        sc.wait_ge(tp1_ready, 2 * u + 2)
                        nc.scalar.activation(slab_c[:, cols], bank_tn[u % 2][:, 0:GT * P], ACT.Copy).then_inc(tp1_copied, 1)
                sc.wait_ge(bn1_var, 1)
                nc.scalar.activation(bn1[:, 2:3], bn1[:, 2:3], ACT.Sqrt).then_inc(bn1_std, 1)
                sc.wait_ge(signs_zero, 1)
                sc.wait_ge(bn1_ready, 1)
                for b in range(B):
                    nc.scalar.activation(signs[:, b, 1:1 + H, 1:1 + W],
                                         slab_c[:, b * HW:(b + 1) * HW].rearrange("p (y x) -> p y x", x=W),
                                         ACT.Sign, bias=bn1[:, 3:4], scale=bn1[:, 2:3]).then_inc(signs_ready, 1)
                for j in range(NCH):
                    sc.wait_ge(conv_ready, j + 1)
                    nc.scalar.activation(slab_b[:, j * CH:(j + 1) * CH], bank_conv[j % 2][:, 0:CH], ACT.Copy)\
                      .then_inc(conv_copied, 1)
                sc.wait_ge(bn2_var, 1)
                nc.scalar.activation(bn2[:, 2:3], bn2[:, 2:3], ACT.Sqrt).then_inc(bn2_std, 1)

            def prelu_batch(n):
                cols = slice(CPB * n * CH, CPB * (n + 1) * CH)
                sc.wait_ge(u_ready, n + 1)
                nc.scalar.activation(slab_c[:, cols], slab_b[:, cols], ACT.Relu, bias=bn2[:, 3:4]).then_inc(relu_ready, 1)
                sc.wait_ge(relu_ready, n + 1)
                nc.scalar.activation(slab_c[:, cols], slab_c[:, cols], ACT.Identity, bias=bn2[:, 6:7],
                                     scale=bn2[:, 5:6]).then_inc(prelu_ready, 1)

            norm_half(0)
            norm_half_end(0)
            norm_half(1)
            prepare_0()
            for g in BN_ORDER:
                bn(0, g)
            norm_half_end(1)
            prepare_1()
            mix_batch(0)
            route_batch(0, 0)
            for g in BN_ORDER[:3]:
                bn(1, g)
            mix_batch(1)
            route_batch(0, 1)
            bn(1, BN_ORDER[3])
            mix_batch(2)
            weights_high(0, 0)
            route_batch(0, 2)
            mix_batch(3)
            weights_high(0, 1)
            route_batch(0, 3)
            weights_high(1, 0)
            weights_high(1, 1)
            experts(0)
            norm_tokens()
            prelu_batch(0)
            for n in range(NBATCH):
                route_batch(1, n)
            experts(1)
            for u in range(NGRP):
                sc.wait_ge(tpo_ready, u + 1)
                nc.scalar.activation(slab_a[:, u * GT * P:(u + 1) * GT * P], bank_tp[u % 2][:, 0:GT * P],
                                     ACT.Copy).then_inc(out_ready, 1)

        @block.vector
        def _(v):
            chain = [0]

            def link(ins):
                chain[0] += 1
                ins.then_inc(dve, 1)
                v.wait_ge(dve, chain[0])

            def mark(ins):
                chain[0] += 1
                ins.then_inc(dve, 1)
                return chain[0]

            TT, TS, STT = v.tensor_tensor, v.tensor_scalar, v.scalar_tensor_tensor

            nw = GI * 9

            def fold_variances():
                v.wait_ge(prep_t, 1)
                link(v.tensor_copy(par[:, 0:35], banks[6][:, 0:35]))
                link(v.tensor_copy(b1_cols[:], banks[6][:, 64:64 + 2 * E * FC]))
                for a, b, c in ((0, 4, 16), (4, 5, 24), (5, 6, 29)):
                    m = mark(TS(fold[:, a:b], par[:, c:c + b - a], BN_EPS, None, ALU.add))
                v.wait_ge(dve, m)
                v.wait_ge(ld_conv, 16)
                link(v.bn_stats(small[:, 0:6], convw.rearrange("p i t -> p (i t)")))
                link(v.bn_aggr(small[:, 6:8], small[:, 0:6]))
                TS(fold[:, 6:7], small[:, 7:8], nw / (nw - 1.0), None, ALU.mult).then_inc(setup_var, 1)

            def diagonals():
                v.wait_ge(consts, N_CONSTS)
                v.wait_ge(ld_wdw, 64)
                for g in range(N_PE):
                    for k in range(9):
                        TS(diag[g][:, k, :], ident[:], wdw[:, g, k:k + 1], None, ALU.mult).then_inc(diag_ready, 1)

            def fold_norms():
                v.wait_ge(setup_var, 1)
                v.wait_ge(setup_sqrt, 1)
                link(v.reciprocal(fold[:, 0:7], fold[:, 8:15]))
                norms = ((4, 8, 12, 0, 4, 0), (21, 22, 23, 20, 1, 4), (26, 27, 28, 25, 1, 5))
                steps = (lambda g, be, me, bi, w, f: TT(par[:, g:g + w], par[:, g:g + w], fold[:, f:f + w], ALU.mult),
                         lambda g, be, me, bi, w, f: TT(par[:, bi:bi + w], par[:, bi:bi + w], par[:, me:me + w], ALU.subtract),
                         lambda g, be, me, bi, w, f: TT(par[:, bi:bi + w], par[:, bi:bi + w], par[:, g:g + w], ALU.mult),
                         lambda g, be, me, bi, w, f: TT(par[:, be:be + w], par[:, be:be + w], par[:, bi:bi + w], ALU.add))
                for s, step in enumerate(steps):
                    for norm in norms:
                        ins = step(*norm)
                        if not (s == 3 and norm is norms[-1]):
                            m = mark(ins)
                    v.wait_ge(dve, m)
                ins.then_inc(par_ready, 1)

            def prepare():
                v.wait_ge(ld_ws, 64)
                link(v.tensor_reduce(convw_abs[:, 0:CQ], ident[:].rearrange("p (g c) -> p c g", g=4), AX.X, ALU.add))
                TT(mix[:].rearrange("p (c o) -> p c o", o=4), convw_abs[:, 0:CQ].unsqueeze(2).to_broadcast([P, CQ, 4]),
                   ws_b[:].unsqueeze(1).to_broadcast([P, CQ, 4]), ALU.mult).then_inc(setup_dve, 1)
                v.wait_ge(ld_gate, 64)
                v.wait_ge(prep_t, 3)
                for l in range(2):
                    TT(gate_w[l][:], gate_w[l][:], banks[7][:, l * E:(l + 1) * E], ALU.subtract)\
                      .then_inc(setup_dve, 1)
                v.wait_ge(mask_ready, 2)
                v.wait_ge(setup_act, 2)
                for k in range(9):
                    src = convw_sign.rearrange("p (i t) -> p i t", t=9)[:, :, k]
                    TT(convw_full[:, k, :].rearrange("p (g i) -> p g i", i=GI),
                       src.unsqueeze(1).to_broadcast([P, CONV_GROUPS, GI]),
                       group_mask.rearrange("p (g i) -> p g i", i=GI), ALU.mult).then_inc(setup_dve, 1)
                v.wait_ge(setup_dve, 1)
                link(TS(convw_abs, convw.rearrange("p i t -> p (i t)"), small[:, 6:7], None, ALU.subtract))
                link(v.tensor_reduce(small[:, 8:9], convw_abs, AX.X, ALU.add, apply_absolute_value=True))
                link(TS(bn2[:, 4:5], small[:, 8:9], fold[:, 6:7], 1.0 / nw, ALU.mult, ALU.mult))

            def b2_low():
                v.wait_ge(b2_high, 1)
                STT(out=b2pad[LOW:LOW + 1, :], in0=b2_raw[LOW:LOW + 1, :], scalar=WS_, in1=b2pad[LOW:LOW + 1, :],
                    op0=ALU.mult, op1=ALU.subtract).then_inc(b2_ready, 1)

            def norm_half(h):
                for q in (2 * h, 2 * h + 1):
                    c0 = (q % 2) * CH
                    xq = xic[:, :, h, c0:c0 + CH]
                    v.wait_ge(mean_ready, q + 1)
                    TT(xq, xq, bank_stat[q % 2][:, 0:CH].unsqueeze(1).to_broadcast([P, 4, CH]), ALU.subtract)\
                      .then_inc(centred, 1)

            def norm_half_end(h):
                for q in (2 * h, 2 * h + 1):
                    v.wait_ge(var_ready, q + 1)
                    TS(std[:, q, :], bank_stat[q % 2][:, 0:CH], LN_EPS_C, None, ALU.add).then_inc(vare_ready, 1)
                for q in (2 * h, 2 * h + 1):
                    c0 = (q % 2) * CH
                    xq = xic[:, :, h, c0:c0 + CH]
                    v.wait_ge(std_ready, q + 1)
                    link(v.reciprocal(std[:, q, :], std[:, q, :]))
                    v.wait_ge(sq_ready, q + 1)
                    TT(xq, xq, std[:, q, :].unsqueeze(1).to_broadcast([P, 4, CH]), ALU.mult).then_inc(xn_ready, 1)

            def taps_half(h):
                v.wait_ge(xn_ready, 2 * h + 2)
                v.wait_ge(ld_wdw, 64)
                last = {}
                order = [4, 0, 1, 2, 3, 5, 6, 7, 8]
                for n, k in enumerate(order):
                    for g in range(N_PE, 4):
                        dy, dx = RATES[g] * (k // 3 - 1), RATES[g] * (k % 3 - 1)
                        y0, y1, x0, x1 = max(0, -dy), min(H, H - dy), max(0, -dx), min(W, W - dx)
                        xv = xic[:, g, h, :].rearrange("p (y x) -> p y x", x=W)[:, y0 + dy:y1 + dy, x0 + dx:x1 + dx]
                        yv = yic[:, g, h, :].rearrange("p (y x) -> p y x", x=W)[:, y0:y1, x0:x1]
                        if n == 0:
                            last[g] = mark(TS(yv, xv, wdw[:, g, k:k + 1], None, ALU.mult))
                            continue
                        v.wait_ge(dve, last[g])
                        ins = STT(out=yv, in0=xv, scalar=wdw[:, g, k:k + 1], in1=yv, op0=ALU.mult, op1=ALU.add)
                        if n < 8:
                            last[g] = mark(ins)
                        else:
                            ins.then_inc(taps_ready, 1)

            def add_batch(l, n):
                cols = slice(CPB * n * CH, CPB * (n + 1) * CH)
                if l == 0:
                    v.wait_ge(ld_x, 64)
                    v.wait_ge(or_ready, CPB * (n + 1))
                    term = orelu.rearrange("p s n -> p (s n)")
                else:
                    v.wait_ge(prelu_ready, n + 1)
                    term = slab_c[:, cols]
                TT(slab_a[:, cols], slab_a[:, cols], term, ALU.add).then_inc(stream[l], 1)

            def token_stats(tiles, eps, ready=None):
                for j in tiles:
                    if ready and j % GT == 0:
                        v.wait_ge(ready, j // GT + 1)
                    m = mark(v.bn_stats(sums[:, j, :], tok[:, j, :]))
                v.wait_ge(dve, m)
                for j in tiles:
                    m = mark(v.bn_aggr(mv[:, j, :], sums[:, j, :]))
                v.wait_ge(dve, m)
                return TS(rstd[:, tiles[0] // TB % 2], mv[:, tiles[0]:tiles[-1] + 1, 1], eps, None, ALU.add)

            def route_batch(l, n, add_next):
                tiles = list(range(TB * n, TB * n + TB))
                if l == 1 and n + 1 < NBATCH:
                    prelu_batch(n + 1)
                token_stats(tiles, LN_EPS_T, tok_ready[l]).then_inc(tvar[l], 1)
                v.wait_ge(tstd[l], n + 1)
                rs = rstd[:, n % 2]
                link(v.reciprocal(rs, rs))
                link(TS(rstdx[:, n % 2], rs, XS, None, ALU.mult))
                STT(out=shift[:, n % 2], in0=mv[:, TB * n:TB * n + TB, 0], scalar=-1.0, in1=rstdx[:, n % 2],
                    op0=ALU.mult, op1=ALU.mult).then_inc(tok_scale[l], 1)
                over_e = lambda a: a.unsqueeze(2).to_broadcast([P, TB, E])
                over_t = lambda a: a.unsqueeze(1).to_broadcast([P, TB, E])
                v.wait_ge(tp_ready[l], GPB * (n + 1))
                lg = bank_lg[:, n * TB * E:(n + 1) * TB * E].rearrange("p (t e) -> p t e", e=E)
                link(TT(prob[:], lg, over_e(rs), ALU.mult))
                link(TT(prob[:], prob[:], over_t(gate_b[l][:]), ALU.add))
                link(v.tensor_reduce(red[:], prob[:], AX.X, ALU.max))
                TT(prob[:], prob[:], over_e(red[:]), ALU.subtract).then_inc(lg_shift[l], 1)
                v.wait_ge(lg_exp[l], n + 1)
                link(v.tensor_reduce(red[:], prob[:], AX.X, ALU.add))
                link(v.reciprocal(red[:], red[:]))
                link(TT(prob[:], prob[:], over_e(red[:]), ALU.mult))
                for k in range(TOPK):
                    link(v.tensor_reduce(top[:, k, :], prob[:], AX.X, ALU.max))
                    link(TT(tmp[:], prob[:], over_e(top[:, k, :]), ALU.is_equal))
                    link(TT(tmp[:], tmp[:], over_t(rev[:]), ALU.mult))
                    link(v.tensor_reduce(red[:], tmp[:], AX.X, ALU.max))
                    link(TT(best[:, k], over_t(rev[:]), over_e(red[:]), ALU.is_equal))
                    if k == 0:
                        link(STT(out=prob[:], in0=best[:, 0], scalar=-2.0, in1=prob[:], op0=ALU.mult, op1=ALU.add))
                TT(chosen[:, 0:TB, :], best[:, 0], best[:, 1], ALU.add).then_inc(chosen_ready[l], 1)
                r = rows_v[:, n % 2]
                v.wait_ge(xhi_ready[l], n + 1)
                hi = r[:, 0, :, 0:C // 2].bitcast(F16)
                link(TT(r[:, 0, :, C // 2:C].bitcast(F16), r[:, 1, :, 0:C], hi, ALU.subtract))
                m = mark(v.tensor_copy(r[:, 1, :, 0:C].bitcast(F16), r[:, 0, :, 0:C].bitcast(F16)))
                for k in range(TOPK):
                    m = mark(v.tensor_copy(r[:, k, :, C], top[:, k, :]))
                    m = mark(v.tensor_copy(r[:, k, :, C + 1].bitcast(I32), out_row[:, k, TB * n:TB * n + TB]))
                if add_next:
                    add_batch(l, n + 1)
                v.wait_ge(rank_ready[l], n + 1)
                link(TT(pos[:], bank_rk[:, 0:(TB + 1) * E].rearrange("p (t e) -> p t e", e=E),
                        carry[:].unsqueeze(1).to_broadcast([P, TB + 1, E]), ALU.add))
                link(v.tensor_copy(carry[:], pos[:, TB, :]))
                for k in range(TOPK):
                    link(TT(tmp[:], best[:, k], pos[:, 0:TB, :], ALU.mult))
                    link(v.tensor_reduce(slot_f[:, k, :], tmp[:], AX.X, ALU.add))
                v.tensor_copy(slot_ix[:, n % 2], slot_f[:]).then_inc(rows_ready[l], 1)

            def route_start(l):
                link(TS(carry[:], rev[:], -float(REGION), float(E * REGION), ALU.mult, ALU.add))

            def make_table(l):
                v.tensor_copy(fill_ix[0:1, :], carry[0:1, :]).then_inc(fill_ready[l], 1)
                s0 = small[0:1, :]
                v.wait_ge(fill_ready[l], 1)
                link(STT(out=s0[:, 0:E], in0=rev[0:1, :], scalar=float(REGION), in1=carry[0:1, :],
                         op0=ALU.mult, op1=ALU.add))
                link(TS(s0[:, 0:E], s0[:, 0:E], float(SR - 1 - E * REGION), None, ALU.add))
                link(v.tensor_copy(small_i[:], s0[:, 0:E]))
                link(TS(small_i[:], small_i[:], 8, None, ALU.arith_shift_right))
                link(v.tensor_copy(s0[:, 0:E], small_i[:]))
                link(v.tensor_tensor_scan(s0[:, E:2 * E], onesf[0:1, :], s0[:, 0:E], 0.0, ALU.mult, ALU.add))
                link(TS(s0[:, 0:E], s0[:, 0:E], -float(SR), float(REGION), ALU.mult, ALU.add))
                ge = slab_b[0:1, E * F:E * F + SLOTS * E].rearrange("p (i e) -> p i e", e=E)
                g2 = slab_c[0:1, E * F:E * F + SLOTS * E].rearrange("p (i e) -> p i e", e=E)
                rowf = slab_c[0:1, E * F + SLOTS * E:E * F + SLOTS * (E + 1)]
                shape = [1, SLOTS, E]
                link(TT(ge, tile_no[:].unsqueeze(2).to_broadcast(shape),
                        s0[:, E:2 * E].unsqueeze(1).to_broadcast(shape), ALU.is_ge))
                link(TT(g2, ge, s0[:, 0:E].unsqueeze(1).to_broadcast(shape), ALU.mult))
                link(v.tensor_reduce(rowf, g2, AX.X, ALU.add))
                link(STT(out=rowf, in0=tile_no[:], scalar=float(SR), in1=rowf, op0=ALU.mult, op1=ALU.add))
                link(TS(rowf, rowf, float(E * REGION), None, ALU.min))
                v.tensor_copy(tab_row[:, 0:SLOTS], rowf).then_inc(table_ready[l], 1)
                v.wait_ge(table_ready[l], 1)
                link(v.tensor_reduce(rowf, ge, AX.X, ALU.add))
                link(TS(rowf, rowf, float(E - 1), None, ALU.min))
                v.tensor_copy(tab_expert[:, 0:SLOTS], rowf).then_inc(table_ready[l], 1)

            def weights_low(l, k):
                src, hi, lo = (((slab_b, w1hi[0], w1lo[0]), (slab_c, w2hi[0], w2lo[0])),
                               ((slab_d, w1hi[1], w1lo[1]), (slab_b, w2hi[1], w2lo[1])))[l][k]
                v.wait_ge(hi_ready[l], k + 1)
                STT(out=lo[:], in0=src[:, 0:E * F], scalar=WS_, in1=hi[:], op0=ALU.mult,
                    op1=ALU.subtract).then_inc(lo_ready[l], 1)

            def experts(l):
                def copy_xt(base, k, first, e):
                    v.wait_ge(xt_ready[l], base + (k + 1))
                    if not first:
                        v.wait_ge(y_stored[k % UNROLL], stored_round(l, base, k - UNROLL))
                    v.tensor_copy(ring_b1[:, k % UNROLL, :], b1_cols[:, bass.ds(e * FC + l * E * FC, FC)])
                    v.tensor_copy(ring_meta[:, k % UNROLL], ring_rows[:, k % UNROLL, :, C:ROW])
                    v.tensor_copy(ring_xt[:, k % 2], bank_xt[k % 2][:].bitcast(F16)[:, 0:2 * SR]
                                  .rearrange("p (k m) -> p k m", k=2)).then_inc(xt_copied[l], 1)

                def low(base, k):
                    half = FC * SR // 2
                    for q in range(2):
                        at = slice(q * half, (q + 1) * half)
                        v.wait_ge(hhi_ready[l], 2 * base + (2 * k + q + 1))
                        STT(out=ring_hlo[:, k % 2, at], in0=ring_h[:, k % 2, at], scalar=HS,
                            in1=ring_hhi[:, k % 2, at], op0=ALU.mult, op1=ALU.subtract).then_inc(hlo_ready[l], 1)

                def gate_y(base, k):
                    v.wait_ge(y_ready[l], base + (k + 1))
                    for j in range(SUB):
                        ins = TS(ring_y[:, k, j, :], bank_y[k % 2][:, j * C:(j + 1) * C], ring_meta[:, k, j, 0:1],
                                 1.0 / (WS_ * HS), ALU.mult, ALU.mult)
                    ins.then_inc(y_copied[l], 1)

                def step(base, k, first, last, e):
                    if not (last and k + 2 >= UNROLL):
                        copy_xt(base, k + 2, first and k + 2 < UNROLL, e[k])
                    gate_y(base, k)
                    if not (last and k + 1 >= UNROLL):
                        low(base, k + 1)

                v.wait_ge(table_ready[l], 2)
                e = table_values(ENG.DVE, tab_expert, 0, UNROLL + 2, E - 1)
                for k in range(2):
                    copy_xt(0, k, True, e[k])
                low(0, 0)
                for k in range(UNROLL):
                    step(0, k, True, False, e[2:])
                with v.Fori(UNROLL, N_TAIL, UNROLL) as i0:
                    e = table_values(ENG.DVE, tab_expert, i0 + 2, UNROLL, E - 1)
                    for k in range(UNROLL):
                        step(i0, k, False, False, e)
                e = table_values(ENG.DVE, tab_expert, N_TAIL + 2, UNROLL - 2, E - 1)
                for k in range(UNROLL):
                    step(N_TAIL, k, False, True, e)

            def add_output(l, k, n):
                cols = slice(n * TB * C, (n + 1) * TB * C)
                v.wait_ge(ld_y[k][n], 16 * (l + 1))
                return TT(slab_t[:, cols], slab_t[:, cols], (slab_b, slab_c)[k][:, cols], ALU.add)

            def sum_batch(l, n):
                link(add_output(l, 0, n))
                add_output(l, 1, n).then_inc(sum_ready[l], 1)

            def norm_tokens():
                def stats(n):
                    sum_batch(0, n)
                    v.wait_ge(sum_ready[0], n + 1)
                    token_stats(list(range(TB * n, TB * n + TB)), LN_EPS_C).then_inc(var1, 1)

                stats(0)
                for n in range(NBATCH):
                    v.wait_ge(std1, n + 1)
                    link(v.reciprocal(rstd[:, n % 2], rstd[:, n % 2]))
                    STT(out=shift[:, n % 2], in0=mv[:, TB * n:TB * n + TB, 0], scalar=-1.0, in1=rstd[:, n % 2],
                        op0=ALU.mult, op1=ALU.mult).then_inc(scale1, 1)
                    if n + 1 < NBATCH:
                        if n >= 1:
                            v.wait_ge(xn1_ready, TB * n)
                        stats(n + 1)
                    for u in range(GPB * n, GPB * n + GPB):
                        v.wait_ge(tp1_copied, 2 * u + 2)
                        m = mark(v.bn_stats(bn_sums[:, u, :], slab_c[:, u * GT * P:(u + 1) * GT * P]))
                v.wait_ge(dve, m)
                link(v.bn_aggr(bn1[:, 0:2], bn_sums[:, 0:NGRP, :]))
                TS(bn1[:, 2:3], bn1[:, 1:2], BN_EPS, None, ALU.add).then_inc(bn1_var, 1)
                v.wait_ge(bn1_std, 1)
                link(v.reciprocal(bn1[:, 2:3], bn1[:, 2:3]))
                link(TT(bn1[:, 2:3], bn1[:, 2:3], par[:, 30:31], ALU.mult))
                link(TT(bn1[:, 3:4], bn1[:, 0:1], bn1[:, 2:3], ALU.mult))
                TT(bn1[:, 3:4], par[:, 31:32], bn1[:, 3:4], ALU.subtract).then_inc(bn1_ready, 1)
                for j in range(NCH):
                    v.wait_ge(conv_copied, j + 1)
                    m = mark(v.bn_stats(bn_sums[:, j, :], slab_b[:, j * CH:(j + 1) * CH]))
                v.wait_ge(dve, m)
                link(v.bn_aggr(bn2[:, 0:2], bn_sums[:, 0:NCH, :]))
                link(TT(bn2[:, 2:3], bn2[:, 1:2], bn2[:, 4:5], ALU.mult))
                link(TT(bn2[:, 2:3], bn2[:, 2:3], bn2[:, 4:5], ALU.mult))
                TS(bn2[:, 2:3], bn2[:, 2:3], BN_EPS, None, ALU.add).then_inc(bn2_var, 1)
                v.wait_ge(bn2_std, 1)
                link(v.reciprocal(bn2[:, 2:3], bn2[:, 2:3]))
                link(TT(bn2[:, 2:3], bn2[:, 2:3], bn2[:, 4:5], ALU.mult))
                link(TT(bn2[:, 2:3], bn2[:, 2:3], par[:, 32:33], ALU.mult))
                link(TT(bn2[:, 3:4], bn2[:, 0:1], bn2[:, 2:3], ALU.mult))
                link(TT(bn2[:, 3:4], par[:, 33:34], bn2[:, 3:4], ALU.subtract))
                link(TS(bn2[:, 5:6], par[:, 34:35], -1.0, 1.0, ALU.mult, ALU.add))
                TT(bn2[:, 6:7], par[:, 34:35], bn2[:, 3:4], ALU.mult).then_inc(bn2_ready, 1)

            def prelu_batch(n):
                cols = slice(CPB * n * CH, CPB * (n + 1) * CH)
                STT(out=slab_b[:, cols], in0=slab_b[:, cols], scalar=bn2[:, 2:3], in1=slab_c[:, cols],
                    op0=ALU.mult, op1=ALU.add).then_inc(u_ready, 1)
                v.wait_ge(u_ready, n + 1)
                link(STT(out=slab_a[:, cols], in0=slab_b[:, cols], scalar=par[:, 34:35], in1=slab_a[:, cols],
                         op0=ALU.mult, op1=ALU.add))

            norm_half(0)
            norm_half_end(0)
            diagonals()
            norm_half(1)
            fold_variances()
            fold_norms()
            taps_half(0)
            prepare()
            norm_half_end(1)
            taps_half(1)
            route_start(0)
            add_batch(0, 0)
            route_batch(0, 0, False)
            add_batch(0, 1)
            route_batch(0, 1, False)
            b2_low()
            add_batch(0, 2)
            route_batch(0, 2, True)
            weights_low(0, 0)
            route_batch(0, 3, False)
            make_table(0)
            weights_low(0, 1)
            weights_low(1, 0)
            weights_low(1, 1)
            experts(0)
            norm_tokens()
            v.wait_ge(bn2_ready, 1)
            route_start(1)
            prelu_batch(0)
            add_batch(1, 0)
            for n in range(NBATCH):
                route_batch(1, n, n + 1 < NBATCH)
            make_table(1)
            experts(1)
            for n in range(NBATCH):
                m = mark(add_output(1, 0, n))
            v.wait_ge(dve, m)
            for n in range(NBATCH):
                add_output(1, 1, n).then_inc(sum_ready[1], 1)

        @block.tensor
        def _(pe):
            mm, tr = nc.tensor.matmul, nc.tensor.transpose

            def prepare_0():
                pe.wait_ge(consts, N_CONSTS)
                pe.wait_ge(ld_branch, 16 * N_BRANCH)
                pe.wait_ge(ld_par, 16 * N_PAR)
                pe.wait_ge(ld_b1, 32)
                tr(banks[6][:, 0:35], par_rows[0:35, :], ident[0:35, 0:35])
                tr(banks[6][:, 64:64 + 2 * E * FC], b1_rows, ident[0:2 * E * FC, 0:2 * E * FC]).then_inc(prep_t, 1)
                pe.wait_ge(ld_wo, 16)
                tr(banks[5][:, 0:P], wo_raw, ident[:]).then_inc(prep_t, 1)
                pe.wait_ge(ld_gate, 64)
                for l in range(2):
                    ins = mm(banks[7][:, l * E:(l + 1) * E], all_mean[:], gate_w[l][:], start=True, stop=True)
                ins.then_inc(prep_t, 1)

            def prepare_1():
                pe.wait_ge(setup_dve, N_SETUP)
                pe.wait_ge(setup_act, 1)
                for k in range(3):
                    for m in range(3):
                        ins = tr(banks[4 + k][:].bitcast(BF16)[:, m * P:(m + 1) * P], convw_full[:, 3 * k + m, :], identb[:])
                    ins.then_inc(convw_tp, 1)

            def norm_half(h):
                pe.wait_ge(ld_xic[h], 16 * 4)
                if h == 0:
                    pe.wait_ge(mean_blocks, 5)
                for q in (2 * h, 2 * h + 1):
                    c0 = (q % 2) * CH
                    if q >= 2:
                        pe.wait_ge(vare_ready, q - 1)
                    for g in range(4):
                        ins = mm(bank_stat[q % 2][:, 0:CH], block_mean[:], xic[:, g, h, c0:c0 + CH],
                                 start=(g == 0), stop=(g == 3))
                    ins.then_inc(mean_ready, 1)

            def norm_half_end(h):
                for q in (2 * h, 2 * h + 1):
                    c0 = (q % 2) * CH
                    pe.wait_ge(centred, q + 1)
                    pe.wait_ge(sq_ready, q + 1)
                    for g in range(4):
                        ins = mm(bank_stat[q % 2][:, 0:CH], block_mean[:], sq[:, g, c0:c0 + CH],
                                 start=(g == 0), stop=(g == 3))
                    ins.then_inc(var_ready, 1)

            def taps(h, g):
                pe.wait_ge(xn_ready, 2 * h + 2)
                pe.wait_ge(diag_ready, 9 * N_PE)
                if h == 1:
                    pe.wait_ge(or_ready, CPB * (g + 1))
                for r in range(2):
                    if g >= 1:
                        pe.wait_ge(bn_ready, normed(h, g - 1) - 1 + r)
                    taps = []
                    for k in (4, 0, 1, 2, 3, 5, 6, 7, 8):
                        dy, dx = RATES[g] * (k // 3 - 1), RATES[g] * (k % 3 - 1)
                        y0, y1 = max(RH * r, -dy), min(RH * r + RH, H - dy)
                        x0, x1 = max(0, -dx), min(W, W - dx)
                        if y1 > y0 and x1 > x0:
                            taps.append((k, dy, dx, y0, y1, x0, x1))
                    for n, (k, dy, dx, y0, y1, x0, x1) in enumerate(taps):
                        xv = xic[:, g, h, :].rearrange("p (y x) -> p y x", x=W)[:, y0 + dy:y1 + dy, x0 + dx:x1 + dx]
                        yv = bank_dw[r][:, 0:CH].rearrange("p (y x) -> p y x", x=W)[:, y0 - RH * r:y1 - RH * r, x0:x1]
                        ins = mm(yv, diag[g][:, k, :], xv, start=(n == 0), stop=(n == len(taps) - 1))
                    ins.then_inc(dw_ready, 1)

            def mix_batch(n):
                def z(j):
                    b, r = j // 2, j % 2
                    pe.wait_ge(ld_ycm[b], 64)
                    if j >= 2:
                        pe.wait_ge(zr_ready, j - 1)
                    if j == 0:
                        pe.wait_ge(vare_ready, 4)
                    mm(bank_z[j % 2][:, 0:CH], mix[:], ycm[:, b, r * CH:r * CH + CH], start=True, stop=True)\
                        .then_inc(z_ready, 1)

                def o(j):
                    pe.wait_ge(zr_ready, j + 1)
                    if j >= 2:
                        pe.wait_ge(or_ready, j - 1)
                    pe.wait_ge(bn_ready, (normed(0, N_PE - 1), normed(1, 0), normed(1, 1), normed(1, 1))[n])
                    mm(bank_o[j % 2][:, 0:CH], wo_t[:], zrelu[:, j % 2, :], start=True, stop=True)\
                        .then_inc(o_ready, 1)

                z(CPB * n)
                for j in range(CPB * n, CPB * n + CPB):
                    if j + 1 < CPB * n + CPB:
                        z(j + 1)
                    o(j)

            def transpose_batch(l, n):
                pe.wait_ge(stream[l], n + 1)
                for u in range(GPB * n, GPB * n + GPB):
                    if u >= 2:
                        pe.wait_ge(tok_ready[l], u - 1)
                    for m in range(GT):
                        i = u * GT + m
                        xv = slab_a[:, i * P:(i + 1) * P]
                        tr(bank_tp[u % 2][:, m * P:(m + 1) * P], xv, ident[:])
                        ins = mm(bank_lg[:, i * E:(i + 1) * E], xv, gate_w[l][:], start=True, stop=True)
                    ins.then_inc(tp_ready[l], 1)

            def rank_batch(l, n):
                pe.wait_ge(chosen_ready[l], n + 1)
                flat = chosen[:].rearrange("p t e -> p (t e)")
                mm(bank_rk[:, 0:(TB + 1) * E], earlier[:], flat, start=True, stop=False)
                for j in range(TB):
                    n_after = TB - j
                    ins = mm(bank_rk[:, (j + 1) * E:(TB + 1) * E].rearrange("p (t e) -> p t e", e=E), onesb[:],
                             chosen[:, j:j + 1, :].to_broadcast([P, n_after, E]), start=False, stop=(j == TB - 1))
                ins.then_inc(rank_ready[l], 1)

            def experts(l):
                pe.wait_ge(table_ready[l], 2)
                if l == 0:
                    pe.wait_ge(lo_ready[0], 2)
                    pe.wait_ge(lo_ready[1], 2)
                    pe.wait_ge(hi_ready[1], 2)
                    pe.wait_ge(b2_ready, 1)

                def early(base, k, n=2):
                    return isinstance(base, int) and base + k < n

                def turn(base, k):
                    pe.wait_ge(ld_ring[k % UNROLL], ring_round(l, base, k))
                    if not early(base, k):
                        pe.wait_ge(xt_copied[l], base + (k - 1))
                    for part in range(2):
                        for j in range(SUB):
                            src = ring_rows[:, k % UNROLL, j, part * C // 2:(part + 1) * C // 2].bitcast(F16)
                            at = part * SR + j * P
                            ins = tr(bank_xt[k % 2][:].bitcast(F16)[:, at:at + P], src, ident16[:])
                    ins.then_inc(xt_ready[l], 1)

                def hidden(base, k, e):
                    pe.wait_ge(xt_copied[l], base + (k + 1))
                    xhi, xlo = ring_xt[:, k % 2, 0, :], ring_xt[:, k % 2, 1, :]
                    for c in range(FC):
                        q = c // 2
                        if c % 2 == 0 and not early(base, k):
                            pe.wait_ge(gelu_ready[l], 2 * base + (2 * k + q - 3))
                        at = bass.ds(e * F + c * P, P)
                        hv = bank_h[k % 2][q][:, (c % 2) * SR:(c % 2 + 1) * SR]
                        mm(hv, w1hi[l][:, at], xhi, start=True, stop=False)
                        mm(hv, w1hi[l][:, at], xlo, start=False, stop=False)
                        ins = mm(hv, w1lo[l][:, at], xhi, start=False, stop=True)
                        if c % 2 == 1:
                            ins.then_inc(h_ready[l], 1)

                def output(base, k, e):
                    if not early(base, k):
                        pe.wait_ge(y_copied[l], base + (k - 1))
                    yv = [bank_y[k % 2][:, j * C:(j + 1) * C] for j in range(SUB)]
                    b2v = b2pad[:, bass.ds(e * C + l * E * C, C)]
                    w = [bass.ds(e * F + c * P, P) for c in range(FC)]
                    for j in range(SUB):
                        h = [slice(c * SR + j * P, c * SR + j * P + P) for c in range(FC)]
                        mm(yv[j], bias_two[:], b2v, start=True, stop=False)
                        for c in range(FC):
                            if j == 0 and c % 2 == 0:
                                pe.wait_ge(hhi_ready[l], 2 * base + (2 * k + c // 2 + 1))
                            mm(yv[j], ring_hhi[:, k % 2, h[c]], w2hi[l][:, w[c]], start=False, stop=False)
                            mm(yv[j], ring_hhi[:, k % 2, h[c]], w2lo[l][:, w[c]], start=False, stop=False)
                        for c in range(FC):
                            if j == 0 and c % 2 == 0:
                                pe.wait_ge(hlo_ready[l], 2 * base + (2 * k + c // 2 + 1))
                            ins = mm(yv[j], ring_hlo[:, k % 2, h[c]], w2hi[l][:, w[c]], start=False, stop=(c == FC - 1))
                    ins.then_inc(y_ready[l], 1)

                e = table_values(ENG.PE, tab_expert, 0, UNROLL + 1, E - 1)
                turn(0, 0)
                turn(0, 1)
                hidden(0, 0, e[0])
                for k in range(UNROLL):
                    turn(0, k + 2)
                    hidden(0, k + 1, e[k + 1])
                    output(0, k, e[k])
                with pe.Fori(UNROLL, N_TAIL, UNROLL) as i0:
                    e = table_values(ENG.PE, tab_expert, i0, UNROLL + 1, E - 1)
                    for k in range(UNROLL):
                        turn(i0, k + 2)
                        hidden(i0, k + 1, e[k + 1])
                        output(i0, k, e[k])
                e = table_values(ENG.PE, tab_expert, N_TAIL, UNROLL, E - 1)
                for k in range(UNROLL):
                    if k + 2 < UNROLL:
                        turn(N_TAIL, k + 2)
                    if k + 1 < UNROLL:
                        hidden(N_TAIL, k + 1, e[k + 1])
                    output(N_TAIL, k, e[k])

            def norm_tokens():
                for u in range(NGRP):
                    n = u // GPB
                    pe.wait_ge(sum_ready[0], n + 1)
                    if u == 0:
                        pe.wait_ge(y_copied[0], SLOTS)
                    if u >= 2:
                        pe.wait_ge(tp1_copied, 2 * u - 3)
                    for m in range(GT):
                        ins = tr(bank_tp[u % 2][:, m * P:(m + 1) * P], tok[:, u * GT + m, :], ident[:])
                    ins.then_inc(tp1_ready, 1)
                    pe.wait_ge(xn1_ready, (u + 1) * GT)
                    if u >= 2:
                        pe.wait_ge(tp1_copied, 2 * u - 2)
                    for m in range(GT):
                        ins = tr(bank_tn[u % 2][:, m * P:(m + 1) * P], tok_b[:, u * GT + m, :], ident[:])
                    ins.then_inc(tp1_ready, 1)
                for j in range(NCH):
                    b, r = j // 2, j % 2
                    pe.wait_ge(signs_ready, b + 1)
                    if j >= 2:
                        pe.wait_ge(conv_copied, j - 1)
                    for k in range(9):
                        ky, kx = k // 3, k % 3
                        ins = mm(bank_conv[j % 2][:, 0:CH].rearrange("p (y x) -> p y x", x=W), convw_t[:, k, :],
                                 signs[:, b, RH * r + ky:RH * r + ky + RH, kx:kx + W], start=(k == 0), stop=(k == 8))
                    ins.then_inc(conv_ready, 1)

            norm_half(0)
            norm_half_end(0)
            norm_half(1)
            prepare_0()
            taps(0, 0)
            taps(0, 1)
            norm_half_end(1)
            prepare_1()
            pe.wait_ge(setup_act, 5)
            mix_batch(0)
            transpose_batch(0, 0)
            taps(1, 0)
            rank_batch(0, 0)
            mix_batch(1)
            transpose_batch(0, 1)
            taps(1, 1)
            rank_batch(0, 1)
            mix_batch(2)
            transpose_batch(0, 2)
            mix_batch(3)
            rank_batch(0, 2)
            transpose_batch(0, 3)
            rank_batch(0, 3)
            experts(0)
            norm_tokens()
            for n in range(NBATCH):
                transpose_batch(1, n)
                rank_batch(1, n)
            experts(1)
            for u in range(NGRP):
                pe.wait_ge(sum_ready[1], u // GPB + 1)
                if u >= 2:
                    pe.wait_ge(out_ready, u - 1)
                if u == 0:
                    pe.wait_ge(y_copied[1], SLOTS)
                for m in range(GT):
                    ins = tr(bank_tp[u % 2][:, m * P:(m + 1) * P], tok[:, u * GT + m, :], ident[:])
                ins.then_inc(tpo_ready, 1)


_INS = ["x",
        *("L0_conv_" + n for n in ("wdw", "bdw", "gdw", "bedw", "mdw", "vdw", "ws", "bs", "gs", "bes", "ms", "vs",
                                   "wo", "bo", "go", "beo", "mo", "vo")),
        *("L0_ffn_" + n for n in ("gate_w", "gate_b", "w1", "b1", "w2", "b2")),
        *("L1_conv_" + n for n in ("conv_w", "bn1_gamma", "bn1_beta", "bn2_gamma", "bn2_beta", "prelu_a")),
        *("L1_ffn_" + n for n in ("gate_w", "gate_b", "w1", "b1", "w2", "b2"))]


def kernel(**inputs):
    import numpy as _np
    import concourse.bacc as _bacc
    from concourse import mybir as _mybir
    from concourse.bass_utils import run_bass_kernel_spmd as _run

    nc = _bacc.Bacc("TRN2", target_bir_lowering=False, num_devices=1)
    arrays, args = {}, {}
    for name in _INS:
        a = _np.ascontiguousarray(inputs[name])
        arrays[f"in_{name}_dram"] = a
        args[name] = nc.dram_tensor(f"in_{name}_dram", a.shape, _mybir.dt.from_np(a.dtype), kind="ExternalInput").ap()
    out = nc.dram_tensor("out_0_dram", (B, C, H, W), F32, kind="ExternalOutput").ap()
    metaformer_kernel(nc, args, out)
    r = _run(nc, [arrays], core_ids=[0])
    return r.results[0]["out_0_dram"]
```

```python
from contextlib import ExitStack

import concourse.bass as bass
from concourse import mybir

F32 = mybir.dt.float32
F16 = mybir.dt.float16
BF16 = mybir.dt.bfloat16
I32 = mybir.dt.int32
ALU = mybir.AluOpType
ACT = mybir.ActivationFunctionType
AX = mybir.AxisListType

P = 128
B, C, H, W = 8, 128, 24, 24
HW = H * W
T = B * HW
NT = T // P
E, F, TOPK = 8, 512, 2
FC = F // P
CQ = C // 4
RATES = (1, 6, 12, 18)
CONV_GROUPS = 16
GI = C // CONV_GROUPS
CH = HW // 2
NCH = T // CH
RH = H // 2
HALF = B // 4
NBATCH = 4
TB = NT // NBATCH
GT = 3
NGRP = NT // GT
GPB = TB // GT
CPB = NCH // NBATCH
SUB = 2
SR = SUB * P
REGION = T + SR
ROW = C + 2
RING = 4
UNROLL = 2 * RING
SLOTS = T * TOPK // SR + E - 1
XS, WS_, HS = 64.0, 64.0, 16.0
LN_EPS_T, LN_EPS_C, BN_EPS = 1e-5, 1e-6, 1e-5
HP, WP = H + 2, W + 2


def metaformer_kernel(nc, t, out):
    x_cm = t["x"].rearrange("b c h w -> c b (h w)")
    x_ic = t["x"].rearrange("(h b) (g c) y x -> h g b c (y x)", b=4, c=CQ)
    out_cm = out.rearrange("b c h w -> c b (h w)")

    with ExitStack() as ctx:
        def sb(name, shape, dt):
            return ctx.enter_context(nc.sbuf_tensor(name, shape, dt))

        def sem(name):
            return ctx.enter_context(nc.semaphore(name))

        ctx.enter_context(nc.allow_non_contiguous_dma(reason="small parameter tables"))

        routed = [nc.dram_tensor(f"routed{l}", (E * REGION + SR, ROW), F32).ap() for l in range(2)]
        expert_out = [nc.dram_tensor(f"expert_out{l}", (TOPK * T, C), F32).ap() for l in range(2)]

        slab_a = sb("slab_a", [P, T], F32)
        slab_t = sb("slab_t", [P, T], F32)
        slab_b = sb("slab_b", [P, T], F32)
        slab_c = sb("slab_c", [P, T], F32)
        slab_d = sb("slab_d", [P, T], F32)
        rows = sb("rows", [P, 2 * TOPK * TB * ROW], F32)
        rows_v = rows[:].rearrange("p (n k t w) -> p n k t w", n=2, k=TOPK, w=ROW)
        w1hi = [sb(f"w1hi{l}", [P, E * F], F16) for l in range(2)]
        w1lo = [sb(f"w1lo{l}", [P, E * F], F16) for l in range(2)]
        w2hi = [sb(f"w2hi{l}", [P, E * F], F16) for l in range(2)]
        w2lo = [sb(f"w2lo{l}", [P, E * F], F16) for l in range(2)]
        b1_cols = sb("b1_cols", [P, 2 * E * FC], F32)
        b2_all = sb("b2_all", [P, 2 * E * C], F32)
        ring_yb = sb("ring_yb", [P, 2, SUB, C], F32)

        tok = slab_t[:].rearrange("p (t c) -> p t c", c=C)
        tok_b = slab_b[:].rearrange("p (t c) -> p t c", c=C)
        tok_c = slab_c[:].rearrange("p (t c) -> p t c", c=C)
        xic = slab_b[:].rearrange("p (g h n) -> p g h n", g=4, h=HALF)
        yic = slab_c[:].rearrange("p (g h n) -> p g h n", g=4, h=HALF)
        sq = slab_d[:, T // 2:T].rearrange("p (g n) -> p g n", g=4)
        ycm = slab_d[:].rearrange("p (b n) -> p b n", b=B)
        std = slab_t[:, T - 2 * HW:T].rearrange("p (q n) -> p q n", n=CH)
        sign_words = B * HP * WP // 2
        signs = slab_d[:, 0:sign_words].bitcast(BF16).rearrange("p (b y x) -> p b y x", b=B, y=HP)
        diag = [w[:, E * F - 9 * P * 2:E * F].bitcast(F32).rearrange("p (t m) -> p t m", m=P)
                for w in (w2lo[1], w1lo[1])]
        b1_rows = w1lo[1][0:2 * E * FC, 1280:1280 + 2 * P].bitcast(F32)
        zrelu = w2hi[1][:, 0:4 * CH].bitcast(F32).rearrange("p (s n) -> p s n", n=CH)
        orelu = [w[:, 4 * CH:4 * CH + 2 * CPB * CH].bitcast(F32) for w in (w2hi[1], w2lo[0])]
        wo_raw = w1hi[1][:, 0:2 * P].bitcast(F32)
        convw = w1hi[1][:, 2 * P:2 * P + 2 * GI * 9].bitcast(F32).rearrange("p (i t) -> p i t", t=9)
        convw_sign = w1hi[1][:, 1024:1024 + GI * 9].bitcast(BF16)
        convw_full = w1hi[1][:, 2048:2048 + 9 * P].bitcast(BF16).rearrange("p (t m) -> p t m", m=P)
        par_rows = w1lo[1][0:40, 0:2 * P].bitcast(F32)
        convw_abs = w1lo[1][:, 512:512 + 2 * GI * 9].bitcast(F32)
        group_mask = w1lo[1][:, 1024:1024 + P].bitcast(BF16)
        ring_rows = slab_c[:, 0:RING * SUB * ROW].rearrange("p (s j w) -> p s j w", j=SUB, w=ROW)
        ring_y = slab_c[:, 2048:2048 + RING * SUB * C].rearrange("p (s j c) -> p s j c", j=SUB, c=C)
        ring_xt = slab_c[:, 3200:3200 + 2 * SR].bitcast(F16).rearrange("p (s k m) -> p s k m", k=2, m=SR)
        ring_h = slab_b[:, 0:2 * FC * SR].rearrange("p (s n) -> p s n", n=FC * SR)
        ring_hhi = slab_b[:, 2048:2048 + FC * SR].bitcast(F16).rearrange("p (s n) -> p s n", n=FC * SR)
        ring_hlo = slab_b[:, 3072:3072 + FC * SR].bitcast(F16).rearrange("p (s n) -> p s n", n=FC * SR)

        ident = sb("ident", [P, P], F32)
        ident16 = sb("ident16", [P, P], F16)
        identb = sb("identb", [P, P], BF16)
        earlier = sb("earlier", [P, P], BF16)
        onesb = sb("onesb", [P, P], BF16)
        onesf = sb("onesf", [1, E], F32)
        block_mean = sb("block_mean", [P, P], F32)
        all_mean = sb("all_mean", [P, P], F32)
        mix = sb("mix", [P, P], F32)
        wo_t = sb("wo_t", [P, P], F32)
        convw_t = sb("convw_t", [P, 9, P], BF16)
        out_row = sb("out_row", [P, TOPK, NT], I32)
        rev = sb("rev", [P, E], F32)
        tile_no = sb("tile_no", [1, SLOTS], F32)
        fill = sb("fill", [P, SUB, ROW], F32)
        ring_meta = sb("ring_meta", [P, RING, SUB, 2], F32)
        ring_b1 = sb("ring_b1", [P, RING, FC], F32)
        par = sb("par", [P, 40], F32)
        wdw = sb("wdw", [P, 4, 9], F32)
        ws_b = sb("ws_b", [P, 4], F32)
        fold = sb("fold", [P, 16], F32)
        gate_w = [sb(f"gate_w{l}", [P, E], F32) for l in range(2)]
        gate_b = [sb(f"gate_b{l}", [P, E], F32) for l in range(2)]
        sums = sb("sums", [P, NT, 6], F32)
        mv = sb("mv", [P, NT, 2], F32)
        rstd = sb("rstd", [P, 2, TB], F32)
        rstdx = sb("rstdx", [P, 2, TB], F32)
        shift = sb("shift", [P, 2, TB], F32)
        prob = sb("prob", [P, TB, E], F32)
        tmp = sb("tmp", [P, TB, E], F32)
        best = sb("best", [P, TOPK, TB, E], F32)
        top = sb("top", [P, TOPK, TB], F32)
        red = sb("red", [P, TB], F32)
        chosen = sb("chosen", [P, TB + 1, E], BF16)
        pos = sb("pos", [P, TB + 1, E], F32)
        carry = sb("carry", [P, E], F32)
        slot_f = sb("slot_f", [P, TOPK, TB], F32)
        slot_ix = sb("slot_ix", [P, 2, TOPK, TB], I32)
        fill_ix = sb("fill_ix", [1, E], I32)
        small = sb("small", [P, 16], F32)
        small_i = sb("small_i", [1, E], I32)
        tab_expert = sb("tab_expert", [1, SLOTS + UNROLL + 1], I32)
        tab_row = sb("tab_row", [1, SLOTS + UNROLL + 1], I32)
        bn_sums = sb("bn_sums", [P, NCH, 6], F32)
        bn1 = sb("bn1", [P, 4], F32)
        bn2 = sb("bn2", [P, 8], F32)

        banks = [ctx.enter_context(nc.psum_tensor(f"bank{i}", [P, 512], F32)) for i in range(8)]
        bank_stat = bank_z = (banks[0], banks[1])
        bank_dw = bank_o = bank_conv = (banks[2], banks[3])
        bank_tp = (banks[4], banks[5])
        bank_tn = (banks[0], banks[1])
        bank_lg, bank_rk = banks[6], banks[7]
        bank_xt, bank_y = (banks[0], banks[1]), (banks[2], banks[3])
        bank_h = ((banks[4], banks[5]), (banks[6], banks[7]))

        consts = sem("consts"); mean_blocks = sem("mean_blocks"); mask_ready = sem("mask_ready")
        par_ready = sem("par_ready"); diag_ready = sem("diag_ready")
        ld_par = sem("ld_par"); ld_branch = sem("ld_branch"); ld_wdw = sem("ld_wdw")
        ld_ws = sem("ld_ws"); ld_wo = sem("ld_wo"); ld_conv = sem("ld_conv"); ld_gate = sem("ld_gate")
        ld_xic = [sem(f"ld_xic{h}") for h in range(HALF)]
        ld_x = sem("ld_x")
        ld_b1 = sem("ld_b1"); ld_b2 = sem("ld_b2")
        ld_w = [[sem(f"ld_w{k}_{l}") for k in (1, 2)] for l in range(2)]
        hi_ready = [sem(f"hi_ready{l}") for l in range(2)]
        lo_ready = [sem(f"lo_ready{l}") for l in range(2)]
        dve = sem("dve")
        prep_t = sem("prep_t"); setup_dve = sem("setup_dve"); setup_act = sem("setup_act")
        setup_sqrt = sem("setup_sqrt"); setup_var = sem("setup_var"); convw_tp = sem("convw_tp")
        mean_ready = sem("mean_ready"); centred = sem("centred"); sq_ready = sem("sq_ready")
        var_ready = sem("var_ready"); vare_ready = sem("vare_ready"); std_ready = sem("std_ready")
        xn_ready = sem("xn_ready"); dw_ready = sem("dw_ready"); taps_ready = sem("taps_ready")
        bn_ready = sem("bn_ready")
        ld_ycm = [sem(f"ld_ycm{b}") for b in range(B)]
        z_ready = sem("z_ready"); zr_ready = sem("zr_ready"); o_ready = sem("o_ready")
        or_ready = sem("or_ready")
        stream = [sem(f"stream{l}") for l in range(2)]
        tp_ready = [sem(f"tp_ready{l}") for l in range(2)]
        tok_ready = [sem(f"tok_ready{l}") for l in range(2)]
        tvar = [sem(f"tvar{l}") for l in range(2)]
        tstd = [sem(f"tstd{l}") for l in range(2)]
        lg_shift = [sem(f"lg_shift{l}") for l in range(2)]
        lg_exp = [sem(f"lg_exp{l}") for l in range(2)]
        chosen_ready = [sem(f"chosen_ready{l}") for l in range(2)]
        rank_ready = [sem(f"rank_ready{l}") for l in range(2)]
        tok_scale = [sem(f"tok_scale{l}") for l in range(2)]
        xn_tok = [sem(f"xn_tok{l}") for l in range(2)]
        xhi_ready = [sem(f"xhi_ready{l}") for l in range(2)]
        rows_ready = [sem(f"rows_ready{l}") for l in range(2)]
        scattered = [[sem(f"scattered{l}_{n}") for n in range(2)] for l in range(2)]
        fill_ready = [sem(f"fill_ready{l}") for l in range(2)]
        filled = [sem(f"filled{l}") for l in range(2)]
        table_ready = [sem(f"table_ready{l}") for l in range(2)]
        ld_ring = [sem(f"ld_ring{s}") for s in range(RING)]
        xt_ready = [sem(f"xt_ready{l}") for l in range(2)]
        meta_copied = [sem(f"meta_copied{l}") for l in range(2)]
        xt_copied = [sem(f"xt_copied{l}") for l in range(2)]
        h_ready = [sem(f"h_ready{l}") for l in range(2)]
        gelu_ready = [sem(f"gelu_ready{l}") for l in range(2)]
        hhi_ready = [sem(f"hhi_ready{l}") for l in range(2)]
        hlo_ready = [sem(f"hlo_ready{l}") for l in range(2)]
        scatter_turn = sem("scatter_turn")
        y_ready = [sem(f"y_ready{l}") for l in range(2)]
        y_biased = [sem(f"y_biased{l}") for l in range(2)]
        y_copied = [sem(f"y_copied{l}") for l in range(2)]
        y_stored = [sem(f"y_stored{s}") for s in range(RING)]
        ld_last = [sem(f"ld_last{u}") for u in range(GPB)]
        ld_y = [[sem(f"ld_y{k}_{n}") for n in range(NBATCH)] for k in range(TOPK)]
        sum_ready = [sem(f"sum_ready{l}") for l in range(2)]
        var1 = sem("var1"); scale1 = sem("scale1"); std1 = sem("std1"); xn1_ready = sem("xn1_ready")
        tp1_ready = sem("tp1_ready"); tp1_copied = sem("tp1_copied")
        bn1_var = sem("bn1_var"); bn1_std = sem("bn1_std"); bn1_ready = sem("bn1_ready")
        signs_zero = sem("signs_zero"); signs_ready = sem("signs_ready")
        conv_ready = sem("conv_ready"); conv_copied = sem("conv_copied")
        bn2_var = sem("bn2_var"); bn2_std = sem("bn2_std"); bn2_ready = sem("bn2_ready")
        u_ready = sem("u_ready"); relu_ready = sem("relu_ready"); prelu_ready = sem("prelu_ready")
        tpo_ready = sem("tpo_ready"); out_ready = sem("out_ready"); stored = sem("stored")

        ENG = mybir.EngineType
        N_TAIL = (SLOTS - 1) // UNROLL * UNROLL
        REST = SLOTS - N_TAIL

        def table_values(engine, table, base, n, most):
            _, values = nc.values_load_multi_w_load_instructions(
                table[0:1, bass.ds(base, n)], engines=[engine], min_val=0, max_val=most,
                skip_runtime_bounds_check_because="the table's entries are clamped to this range")
            return values

        def slot_tiles(s):
            return len(range(s, SLOTS, RING))

        def ring_round(l, base, k):
            return base * (16 // RING) + 16 * (k // RING + l * slot_tiles(k % RING) + 1)

        def stored_round(l, base, k):
            return base * (16 * SUB // RING) + 16 * SUB * (k // RING + l * slot_tiles(k % RING) + 1)

        N_CONSTS = 18
        N_BRANCH, N_PAR = 5 + 5, 5 + 5
        N_SETUP = 1 + 2 + 9

        N_PE = (1, 2)
        BN_ORDER = ((0, 1, 2, 3), (0, 2, 3, 1))

        def normed(h, g):
            before = h * (4 + N_PE[0])
            return before + sum(2 if m < N_PE[h] else 1 for m in BN_ORDER[h][:BN_ORDER[h].index(g) + 1])

        def scatter_goal(n):
            return 16 * TOPK * TB * (n // 2 + 1)

        block = ctx.enter_context(nc.Block())

        @block.sync
        def _(sp):
            for h in range(HALF):
                for b in range(4):
                    sp.dma_start(xic[CQ * b:CQ * b + CQ, :, h, :],
                                 x_ic[h, :, b].rearrange("g c n -> c g n")).then_inc(ld_xic[h], 16)
            for i, name in enumerate(("L0_conv_bo", "L0_conv_go", "L0_conv_beo", "L0_conv_mo", "L0_conv_vo",
                                      "L1_conv_bn1_gamma", "L1_conv_bn1_beta", "L1_conv_bn2_gamma",
                                      "L1_conv_bn2_beta", "L1_conv_prelu_a")):
                sp.dma_start(par_rows[25 + i:26 + i, :], t[name].rearrange("(a c) -> a c", a=1)).then_inc(ld_par, 16)
            sp.dma_start(convw, t["L1_conv_conv_w"].rearrange("o i y x -> o i (y x)")).then_inc(ld_conv, 16)
            sp.dma_start(wo_raw, t["L0_conv_wo"].rearrange("o i a b -> o (i a b)")).then_inc(ld_wo, 16)
            for l in range(2):
                sp.dma_start(gate_w[l][:], t[f"L{l}_ffn_gate_w"]).then_inc(ld_gate, 16)
                sp.dma_start(gate_b[l][:], t[f"L{l}_ffn_gate_b"].rearrange("(a e) -> a e", a=1)
                             .to_broadcast([P, E])).then_inc(ld_gate, 16)
            for l in range(2):
                sp.dma_start(b2_all[:, l * E * C:(l + 1) * E * C],
                             t[f"L{l}_ffn_b2"].rearrange("(a e) d -> a (e d)", a=1).to_broadcast([P, E * C]))\
                  .then_inc(ld_b2, 16)
            for b in range(0, B, 2):
                sp.dma_start(slab_a[:, b * HW:(b + 2) * HW].rearrange("p (b n) -> p b n", b=2),
                             x_cm[:, b:b + 2, :]).then_inc(ld_x, 16)

            def shuffle(h):
                for g in BN_ORDER[h]:
                    sp.wait_ge(bn_ready, normed(h, g))
                    for b in range(4):
                        sp.dma_start(ycm[CQ * g:CQ * g + CQ, 4 * h + b, :],
                                     yic[CQ * b:CQ * b + CQ, g, h, :]).then_inc(ld_ycm[4 * h + b], 16)

            def load_w1(l, slab):
                sp.dma_start(slab[:, 0:E * F].rearrange("p (e f) -> p e f", e=E),
                             t[f"L{l}_ffn_w1"].rearrange("e d f -> d e f")).then_inc(ld_w[l][0], 16)

            def load_w2(l, slab):
                sp.dma_start(slab[:, 0:E * F].rearrange("p (e c d) -> p e c d", e=E, c=FC),
                             t[f"L{l}_ffn_w2"].rearrange("e (c p) d -> p e c d", p=P)).then_inc(ld_w[l][1], 16)

            def load_weights():
                sp.wait_ge(taps_ready, 8 - sum(N_PE))
                sp.wait_ge(dw_ready, 2 * sum(N_PE))
                load_w1(0, slab_b)
                for b in range(B):
                    sp.wait_ge(ld_ycm[b], 64)
                load_w2(0, slab_c)
                sp.wait_ge(z_ready, NCH)
                load_w1(1, slab_d)

            def fill_padding(l):
                sp.wait_ge(fill_ready[l], 1)
                _, ends = nc.values_load_multi_w_load_instructions(
                    fill_ix[0:1, :], engines=[ENG.SP], min_val=0, max_val=E * REGION - SR,
                    skip_runtime_bounds_check_because="a region's rows end at least a slot tile before it does")
                sp.dma_start(routed[l][E * REGION:E * REGION + SR, :].rearrange("(j p) w -> p j w", p=P),
                             fill[:]).then_inc(filled[l], 16)
                for e in range(E):
                    sp.dma_start(routed[l][bass.ds(ends[e], SR), :].rearrange("(j p) w -> p j w", p=P), fill[:])\
                      .then_inc(filled[l], 16)

            def expert_loads(l):
                sp.wait_ge(table_ready[l], 2)
                for n in range(2):
                    sp.wait_ge(scattered[l][n], scatter_goal(NBATCH - 2 + n))
                sp.wait_ge(filled[l], 16 * (E + 1))
                sp.wait_ge(lo_ready[0], 2)

                def step(base, k, row, first):
                    if not first:
                        sp.wait_ge(meta_copied[l], base + (k - RING + 1))
                    sp.dma_start(ring_rows[:, k % RING],
                                 routed[l][bass.ds(row, SR), :].rearrange("(j p) w -> p j w", p=P))\
                      .then_inc(ld_ring[k % RING], 16)

                first_rows = table_values(ENG.SP, tab_row, 0, UNROLL, E * REGION)
                for k in range(UNROLL):
                    step(0, k, first_rows[k], k < RING)
                with sp.Fori(UNROLL, N_TAIL, UNROLL) as i0:
                    row = table_values(ENG.SP, tab_row, i0, UNROLL, E * REGION)
                    for k in range(UNROLL):
                        step(i0, k, row[k], False)
                row = table_values(ENG.SP, tab_row, N_TAIL, REST, E * REGION)
                for k in range(REST):
                    step(N_TAIL, k, row[k], False)

            def load_outputs(l):
                for s in range(RING):
                    sp.wait_ge(y_stored[s], 16 * SUB * (l + 1) * slot_tiles(s))
                pieces = [(k, n) for n in range(NBATCH) for k in range(TOPK)]
                for k, n in pieces if l == 0 else sorted(pieces)[:-1]:
                    src = expert_out[l][k * T + n * TB * P:k * T + (n + 1) * TB * P, :]
                    sp.dma_start((tok_b, tok_c)[k][:, n * TB:(n + 1) * TB, :],
                                 src.rearrange("(t p) c -> p t c", p=P)).then_inc(ld_y[k][n], 16)
                if l == 1:
                    for m in range(GPB):
                        u = NGRP - GPB + m
                        src = expert_out[1][T + u * GT * P:T + (u + 1) * GT * P, :]
                        sp.dma_start(tok_c[:, u * GT:(u + 1) * GT, :],
                                     src.rearrange("(t p) c -> p t c", p=P)).then_inc(ld_last[m], 16)

            shuffle(0)
            shuffle(1)
            load_weights()
            sp.wait_ge(hi_ready[0], 1)
            sp.wait_ge(lo_ready[0], 1)
            load_w2(1, slab_b)
            fill_padding(0)
            expert_loads(0)
            load_outputs(0)
            fill_padding(1)
            expert_loads(1)
            load_outputs(1)
            for b, images in ((0, 2), (2, 2), (4, 2), (6, 1), (7, 1)):
                sp.wait_ge(out_ready, -(-(b + images) * HW // (GT * P)))
                sp.dma_start(out_cm[:, b:b + images, :],
                             slab_a[:, b * HW:(b + images) * HW].rearrange("p (b n) -> p b n", b=images))\
                  .then_inc(stored, 16)
            sp.wait_ge(stored, 16 * 5)

        @block.gpsimd
        def _(pool):
            count = [0]

            def const(ins):
                ins.then_inc(consts, 1)
                count[0] += 1

            pool.memset(block_mean[:], 0.0).then_inc(mean_blocks, 1)
            for b in range(4):
                pool.wait_ge(mean_blocks, 1 + b)
                pool.memset(block_mean[CQ * b:CQ * b + CQ, CQ * b:CQ * b + CQ], 1.0 / C).then_inc(mean_blocks, 1)
            pool.wait_ge(mean_blocks, 5)
            for m in (ident, ident16, identb):
                const(pool.memset(m[:], 0.0))
            const(pool.memset(earlier[:], 1.0))
            pool.wait_ge(consts, 4)
            for m in (ident, ident16, identb):
                const(pool.affine_select(out=m[:], in_=m[:], compare_op=ALU.not_equal, fill=1.0, base=0,
                                         pattern=[[-1, P]], channel_multiplier=1))
            const(pool.affine_select(out=earlier[:], in_=earlier[:], compare_op=ALU.is_gt, fill=0.0, base=0,
                                     pattern=[[1, P]], channel_multiplier=-1))
            const(pool.memset(onesb[:], 1.0))
            const(pool.memset(all_mean[:], 1.0 / C))
            const(pool.memset(onesf[:], 1.0))
            const(pool.memset(chosen[:], 0.0))
            for k in range(TOPK):
                const(pool.iota(out_row[:, k, :], pattern=[[P, NT]], base=k * T, channel_multiplier=1))
            const(pool.iota(rev[:], pattern=[[-1, E]], base=E, channel_multiplier=0,
                            allow_small_or_imprecise_dtypes=True))
            const(pool.iota(tile_no[:], pattern=[[1, SLOTS]], base=0, channel_multiplier=0,
                            allow_small_or_imprecise_dtypes=True))
            const(pool.memset(fill[:, :, 0:C + 1], 0.0))
            const(pool.iota(fill[:, :, C + 1].bitcast(I32), pattern=[[P, SUB]], base=TOPK * T, channel_multiplier=1))
            assert count[0] == N_CONSTS
            for i, name in enumerate(("bdw", "gdw", "bedw", "mdw", "vdw")):
                pool.dma_start(par_rows[4 * i:4 * i + 4, :].rearrange("r (b c) -> r b c", b=4),
                             t["L0_conv_" + name].unsqueeze(1).to_broadcast([4, 4, CQ])).then_inc(ld_branch, 16)
            for i, name in enumerate(("bs", "gs", "bes", "ms", "vs")):
                pool.dma_start(par_rows[20 + i:21 + i, :].rearrange("r (c o) -> r c o", o=4),
                             t["L0_conv_" + name].rearrange("(a b o) -> a b o", a=1, b=1)
                             .to_broadcast([1, CQ, 4])).then_inc(ld_branch, 16)
            for l in range(2):
                pool.dma_start(b1_rows[l * E * FC:(l + 1) * E * FC, :],
                             t[f"L{l}_ffn_b1"].rearrange("e (c p) -> (e c) p", p=P)).then_inc(ld_b1, 16)
            for g in range(4):
                pool.dma_start(ws_b[CQ * g:CQ * g + CQ, :],
                             t["L0_conv_ws"][:, g:g + 1, 0, 0].rearrange("o g -> g o").to_broadcast([CQ, 4]))\
                  .then_inc(ld_ws, 16)

            pool.wait_ge(consts, N_CONSTS)
            gm = group_mask.rearrange("p (g i) -> p g i", i=GI)
            pool.affine_select(out=gm, in_=onesb[:].rearrange("p (g i) -> p g i", i=GI), compare_op=ALU.is_ge,
                               fill=0.0, base=0, pattern=[[-GI, CONV_GROUPS], [0, GI]],
                               channel_multiplier=1).then_inc(mask_ready, 1)
            pool.wait_ge(mask_ready, 1)
            pool.affine_select(out=gm, in_=gm, compare_op=ALU.is_ge, fill=0.0, base=GI - 1,
                               pattern=[[GI, CONV_GROUPS], [0, GI]], channel_multiplier=-1).then_inc(mask_ready, 1)

            def scatter_rows(l):
                for n in range(NBATCH):
                    pool.wait_ge(rows_ready[l], n + 1)
                    for j in range(TB):
                        for k in range(TOPK):
                            pool.indirect_dma_start(
                                routed[l], bass.IndirectOffsetOnAxis(ap=slot_ix[:, n % 2, k, j:j + 1], axis=0),
                                rows_v[:, n % 2, k, j, :], None, bounds_check=E * REGION - 1,
                                oob_is_err=False).then_inc(scattered[l][n % 2], 16)

            def scatter_outputs(l):
                def step(i, s, bound):
                    pool.wait_ge(y_copied[l], i + 1)
                    pool.sem_inc(scatter_turn, 1)
                    for j in range(SUB):
                        pool.indirect_dma_start(
                            expert_out[l],
                            bass.IndirectOffsetOnAxis(ap=ring_meta[:, s, j, 1:2].bitcast(I32), axis=0),
                            ring_y[:, s, j, :], None, bounds_check=bound,
                            oob_is_err=False).then_inc(y_stored[s], 16)
                with pool.register(f"last_row{l}") as last_row:
                    pool.reg_mov(last_row, TOPK * T - 1)
                    bound = pool.snap(last_row)
                    with pool.Fori(0, N_TAIL, UNROLL) as i0:
                        for k in range(UNROLL):
                            step(i0 + k, k % RING, bound)
                    for k in range(REST):
                        step(N_TAIL + k, k, bound)

            scatter_rows(0)
            scatter_outputs(0)
            pool.memset(slab_d[:, 0:sign_words], 0.0).then_inc(signs_zero, 1)
            scatter_rows(1)
            scatter_outputs(1)

        @block.scalar
        def _(sc):
            for b in range(4):
                sc.dma_start(wdw[CQ * b:CQ * b + CQ, :, :],
                             t["L0_conv_wdw"].rearrange("g c a y x -> c g (a y x)")).then_inc(ld_wdw, 16)

            def prepare_0():
                sc.wait_ge(setup_var, 1)
                nc.scalar.activation(fold[:, 8:15], fold[:, 0:7], ACT.Sqrt).then_inc(setup_sqrt, 1)
                sc.wait_ge(prep_t, 2)
                nc.scalar.activation(wo_t[:], banks[5][:, 0:P], ACT.Copy).then_inc(setup_act, 1)
                sc.wait_ge(ld_conv, 16)
                nc.scalar.activation(convw_sign.rearrange("p (i t) -> p i t", t=9), convw, ACT.Sign)\
                  .then_inc(setup_act, 1)

            def prepare_1():
                for k in range(3):
                    sc.wait_ge(convw_tp, k + 1)
                    nc.scalar.activation(convw_t[:, 3 * k:3 * k + 3, :],
                                         banks[4 + k][:].bitcast(BF16)[:, 0:3 * P].rearrange("p (t m) -> p t m", m=P),
                                         ACT.Copy).then_inc(setup_act, 1)

            def norm_half(h):
                for q in (2 * h, 2 * h + 1):
                    c0 = (q % 2) * CH
                    sc.wait_ge(centred, q + 1)
                    nc.scalar.activation(sq[:, :, c0:c0 + CH], xic[:, :, h, c0:c0 + CH], ACT.Square)\
                      .then_inc(sq_ready, 1)

            def norm_half_end(h):
                for q in (2 * h, 2 * h + 1):
                    sc.wait_ge(vare_ready, q + 1)
                    nc.scalar.activation(std[:, q, :], std[:, q, :], ACT.Sqrt).then_inc(std_ready, 1)

            def bn(h, g):
                if h == 0:
                    sc.wait_ge(par_ready, 1)
                if g < N_PE[h]:
                    for r in range(2):
                        sc.wait_ge(dw_ready, 2 * N_PE[0] * h + 2 * g + r + 1)
                        nc.scalar.activation(yic[:, g, h, r * CH:r * CH + CH], bank_dw[r][:, 0:CH], ACT.Relu,
                                             bias=par[:, 8 + g:9 + g], scale=par[:, 4 + g:5 + g]).then_inc(bn_ready, 1)
                else:
                    sc.wait_ge(taps_ready, (4 - N_PE[0]) * h + g - N_PE[h] + 1)
                    nc.scalar.activation(yic[:, g, h, :], yic[:, g, h, :], ACT.Relu,
                                         bias=par[:, 8 + g:9 + g], scale=par[:, 4 + g:5 + g]).then_inc(bn_ready, 1)

            def mix_batch(n):
                def z(j):
                    sc.wait_ge(z_ready, j + 1)
                    if j >= 2:
                        sc.wait_ge(o_ready, j - 1)
                    nc.scalar.activation(zrelu[:, j % 2, :], bank_z[j % 2][:, 0:CH], ACT.Relu,
                                         bias=par[:, 22:23], scale=par[:, 21:22]).then_inc(zr_ready, 1)

                def o(j):
                    sc.wait_ge(o_ready, j + 1)
                    at = slice((j % CPB) * CH, (j % CPB + 1) * CH)
                    nc.scalar.activation(orelu[n % 2][:, at], bank_o[j % 2][:, 0:CH], ACT.Relu,
                                         bias=par[:, 27:28], scale=par[:, 26:27]).then_inc(or_ready, 1)

                z(CPB * n)
                if n >= 2:
                    sc.wait_ge(stream[0], n - 1)
                for j in range(CPB * n, CPB * n + CPB):
                    if j + 1 < CPB * n + CPB:
                        z(j + 1)
                    o(j)

            def copy_tokens(l, n):
                for u in range(GPB * n, GPB * n + GPB):
                    sc.wait_ge(tp_ready[l], u + 1)
                    nc.scalar.activation(slab_t[:, u * GT * P:(u + 1) * GT * P], bank_tp[u % 2][:, 0:GT * P],
                                         ACT.Copy).then_inc(tok_ready[l], 1)

            def route_batch(l, n):
                if l == 1 and n + 1 < NBATCH:
                    prelu_batch(n + 1)
                sc.wait_ge(tvar[l], n + 1)
                nc.scalar.activation(rstd[:, n % 2], rstd[:, n % 2], ACT.Sqrt).then_inc(tstd[l], 1)
                sc.wait_ge(lg_shift[l], n + 1)
                nc.scalar.activation(prob[:], prob[:], ACT.Exp).then_inc(lg_exp[l], 1)
                r = rows_v[:, n % 2]
                if n >= 2:
                    sc.wait_ge(scattered[l][n % 2], scatter_goal(n - 2))
                sc.wait_ge(tok_scale[l], n + 1)
                for j in range(TB):
                    ins = nc.scalar.activation(r[:, 1, j, 0:C], tok[:, TB * n + j, :], ACT.Identity,
                                               bias=shift[:, n % 2, j:j + 1], scale=rstdx[:, n % 2, j:j + 1])
                ins.then_inc(xn_tok[l], 1)
                sc.wait_ge(xn_tok[l], n + 1)
                nc.scalar.activation(r[:, 0, :, 0:C // 2].bitcast(F16), r[:, 1, :, 0:C], ACT.Copy)\
                  .then_inc(xhi_ready[l], 1)

            def weights_high(l, k):
                src, dst = (((slab_b, w1hi[0]), (slab_c, w2hi[0])), ((slab_d, w1hi[1]), (slab_b, w2hi[1])))[l][k]
                sc.wait_ge(ld_w[l][k], 16)
                if l == 1 and k == 0:
                    sc.wait_ge(tp_ready[0], NGRP)
                nc.scalar.activation(dst[:], src[:, 0:E * F], ACT.Copy, scale=WS_).then_inc(hi_ready[l], 1)

            def experts(l):
                def step(base, k, first):
                    half = FC * SR // 2

                    def gelu(c):
                        q = c // 2
                        if c % 2 == 0:
                            sc.wait_ge(h_ready[l], 2 * base + (2 * k + q + 1))
                            if not (first and k < 2):
                                sc.wait_ge(hlo_ready[l], 2 * base + (2 * k + q - 3))
                        ins = nc.scalar.activation(ring_h[:, k % 2, c * SR:(c + 1) * SR],
                                                   bank_h[k % 2][q][:, (c % 2) * SR:(c % 2 + 1) * SR], ACT.Gelu,
                                                   bias=ring_b1[:, k % RING, c:c + 1], scale=1.0 / (XS * WS_))
                        if c % 2 == 1:
                            ins.then_inc(gelu_ready[l], 1)

                    def high(q):
                        sc.wait_ge(gelu_ready[l], 2 * base + (2 * k + q + 1))
                        if not (first and k < 2):
                            sc.wait_ge(y_ready[l], base + (k - 1))
                        nc.scalar.activation(ring_hhi[:, k % 2, q * half:(q + 1) * half],
                                             ring_h[:, k % 2, q * half:(q + 1) * half], ACT.Copy, scale=HS)\
                          .then_inc(hhi_ready[l], 1)

                    gelu(0)
                    gelu(1)
                    gelu(2)
                    high(0)
                    gelu(3)
                    high(1)

                for k in range(UNROLL):
                    step(0, k, True)
                with sc.Fori(UNROLL, N_TAIL, UNROLL) as i0:
                    for k in range(UNROLL):
                        step(i0, k, False)
                for k in range(REST):
                    step(N_TAIL, k, False)

            def norm_tokens():
                for n in range(NBATCH):
                    sc.wait_ge(var1, n + 1)
                    nc.scalar.activation(rstd[:, n % 2], rstd[:, n % 2], ACT.Sqrt).then_inc(std1, 1)
                    sc.wait_ge(scale1, n + 1)
                    for j in range(TB):
                        nc.scalar.activation(tok_b[:, TB * n + j, :], tok[:, TB * n + j, :], ACT.Identity,
                                             bias=shift[:, n % 2, j:j + 1], scale=rstd[:, n % 2, j:j + 1])\
                          .then_inc(xn1_ready, 1)
                    for u in range(GPB * n, GPB * n + GPB):
                        cols = slice(u * GT * P, (u + 1) * GT * P)
                        sc.wait_ge(tp1_ready, 2 * u + 1)
                        nc.scalar.activation(slab_a[:, cols], bank_tp[u % 2][:, 0:GT * P], ACT.Copy)\
                          .then_inc(tp1_copied, 1)
                        sc.wait_ge(tp1_ready, 2 * u + 2)
                        nc.scalar.activation(slab_c[:, cols], bank_tn[u % 2][:, 0:GT * P], ACT.Copy)\
                          .then_inc(tp1_copied, 1)
                sc.wait_ge(bn1_var, 1)
                nc.scalar.activation(bn1[:, 2:3], bn1[:, 2:3], ACT.Sqrt).then_inc(bn1_std, 1)
                sc.wait_ge(signs_zero, 1)
                sc.wait_ge(bn1_ready, 1)
                for b in range(B):
                    nc.scalar.activation(signs[:, b, 1:1 + H, 1:1 + W],
                                         slab_c[:, b * HW:(b + 1) * HW].rearrange("p (y x) -> p y x", x=W),
                                         ACT.Sign, bias=bn1[:, 3:4], scale=bn1[:, 2:3]).then_inc(signs_ready, 1)
                for j in range(NCH):
                    sc.wait_ge(conv_ready, j + 1)
                    nc.scalar.activation(slab_b[:, j * CH:(j + 1) * CH], bank_conv[j % 2][:, 0:CH], ACT.Copy)\
                      .then_inc(conv_copied, 1)
                sc.wait_ge(bn2_var, 1)
                nc.scalar.activation(bn2[:, 2:3], bn2[:, 2:3], ACT.Sqrt).then_inc(bn2_std, 1)

            def prelu_batch(n):
                cols = slice(CPB * n * CH, CPB * (n + 1) * CH)
                sc.wait_ge(u_ready, n + 1)
                nc.scalar.activation(slab_c[:, cols], slab_b[:, cols], ACT.Relu, bias=bn2[:, 3:4])\
                  .then_inc(relu_ready, 1)
                sc.wait_ge(relu_ready, n + 1)
                nc.scalar.activation(slab_c[:, cols], slab_c[:, cols], ACT.Identity, bias=bn2[:, 6:7],
                                     scale=bn2[:, 5:6]).then_inc(prelu_ready, 1)

            norm_half(0)
            norm_half_end(0)
            norm_half(1)
            prepare_0()
            for g in BN_ORDER[0]:
                bn(0, g)
            norm_half_end(1)
            for n in (0, 1):
                mix_batch(n)
            for n in (0, 1):
                copy_tokens(0, n)
            route_batch(0, 0)
            for g in BN_ORDER[1]:
                bn(1, g)
            route_batch(0, 1)
            for n in (2, 3):
                mix_batch(n)
            for n in (2, 3):
                copy_tokens(0, n)
            route_batch(0, 2)
            weights_high(0, 0)
            route_batch(0, 3)
            prepare_1()
            weights_high(0, 1)
            weights_high(1, 0)
            weights_high(1, 1)
            experts(0)
            norm_tokens()
            prelu_batch(0)
            for n in range(NBATCH):
                copy_tokens(1, n)
                route_batch(1, n)
            experts(1)
            for u in range(NGRP):
                sc.wait_ge(tpo_ready, u + 1)
                nc.scalar.activation(slab_a[:, u * GT * P:(u + 1) * GT * P], bank_tp[u % 2][:, 0:GT * P],
                                     ACT.Copy).then_inc(out_ready, 1)

        @block.vector
        def _(v):
            chain = [0]

            def link(ins):
                chain[0] += 1
                ins.then_inc(dve, 1)
                v.wait_ge(dve, chain[0])

            def mark(ins):
                chain[0] += 1
                ins.then_inc(dve, 1)
                return chain[0]

            TT, TS, STT = v.tensor_tensor, v.tensor_scalar, v.scalar_tensor_tensor

            nw = GI * 9

            def fold_variances():
                v.wait_ge(prep_t, 1)
                link(v.tensor_copy(par[:, 0:35], banks[6][:, 0:35]))
                link(v.tensor_copy(b1_cols[:], banks[6][:, 64:64 + 2 * E * FC]))
                for a, b, c in ((0, 4, 16), (4, 5, 24), (5, 6, 29)):
                    m = mark(TS(fold[:, a:b], par[:, c:c + b - a], BN_EPS, None, ALU.add))
                v.wait_ge(dve, m)
                v.wait_ge(ld_conv, 16)
                link(v.bn_stats(small[:, 0:6], convw.rearrange("p i t -> p (i t)")))
                link(v.bn_aggr(small[:, 6:8], small[:, 0:6]))
                TS(fold[:, 6:7], small[:, 7:8], nw / (nw - 1.0), None, ALU.mult).then_inc(setup_var, 1)

            def diagonals(g):
                v.wait_ge(consts, N_CONSTS)
                v.wait_ge(ld_wdw, 64)
                for k in range(9):
                    TS(diag[g][:, k, :], ident[:], wdw[:, g, k:k + 1], None, ALU.mult).then_inc(diag_ready, 1)

            def fold_norms():
                v.wait_ge(setup_var, 1)
                v.wait_ge(setup_sqrt, 1)
                link(v.reciprocal(fold[:, 0:7], fold[:, 8:15]))
                norms = ((4, 8, 12, 0, 4, 0), (21, 22, 23, 20, 1, 4), (26, 27, 28, 25, 1, 5))

                def col(a, w):
                    return par[:, a:a + w]

                for g, be, me, bi, w, f in norms:
                    TT(col(g, w), col(g, w), fold[:, f:f + w], ALU.mult)
                    m = mark(TT(col(bi, w), col(bi, w), col(me, w), ALU.subtract))
                v.wait_ge(dve, m)
                for g, be, me, bi, w, f in norms:
                    m = mark(TT(col(bi, w), col(bi, w), col(g, w), ALU.mult))
                v.wait_ge(dve, m)
                for g, be, me, bi, w, f in norms:
                    ins = TT(col(be, w), col(be, w), col(bi, w), ALU.add)
                ins.then_inc(par_ready, 1)

            def prepare_0():
                v.wait_ge(ld_ws, 64)
                link(v.tensor_reduce(convw_abs[:, 0:CQ], ident[:].rearrange("p (g c) -> p c g", g=4), AX.X, ALU.add))
                TT(mix[:].rearrange("p (c o) -> p c o", o=4), convw_abs[:, 0:CQ].unsqueeze(2).to_broadcast([P, CQ, 4]),
                   ws_b[:].unsqueeze(1).to_broadcast([P, CQ, 4]), ALU.mult).then_inc(setup_dve, 1)
                v.wait_ge(ld_gate, 64)
                v.wait_ge(prep_t, 3)
                for l in range(2):
                    TT(gate_w[l][:], gate_w[l][:], banks[7][:, l * E:(l + 1) * E], ALU.subtract)\
                      .then_inc(setup_dve, 1)

            def prepare_1():
                v.wait_ge(mask_ready, 2)
                v.wait_ge(setup_act, 2)
                for k in range(9):
                    src = convw_sign.rearrange("p (i t) -> p i t", t=9)[:, :, k]
                    TT(convw_full[:, k, :].rearrange("p (g i) -> p g i", i=GI),
                       src.unsqueeze(1).to_broadcast([P, CONV_GROUPS, GI]),
                       group_mask.rearrange("p (g i) -> p g i", i=GI), ALU.mult).then_inc(setup_dve, 1)
                v.wait_ge(setup_dve, 1)
                link(TS(convw_abs, convw.rearrange("p i t -> p (i t)"), small[:, 6:7], None, ALU.subtract))
                link(v.tensor_reduce(small[:, 8:9], convw_abs, AX.X, ALU.add, apply_absolute_value=True))
                link(TS(bn2[:, 4:5], small[:, 8:9], fold[:, 6:7], 1.0 / nw, ALU.mult, ALU.mult))

            def norm_half(h):
                for q in (2 * h, 2 * h + 1):
                    c0 = (q % 2) * CH
                    xq = xic[:, :, h, c0:c0 + CH]
                    v.wait_ge(mean_ready, q + 1)
                    TT(xq, xq, bank_stat[q % 2][:, 0:CH].unsqueeze(1).to_broadcast([P, 4, CH]), ALU.subtract)\
                      .then_inc(centred, 1)

            def norm_half_end(h):
                for q in (2 * h, 2 * h + 1):
                    v.wait_ge(var_ready, q + 1)
                    TS(std[:, q, :], bank_stat[q % 2][:, 0:CH], LN_EPS_C, None, ALU.add).then_inc(vare_ready, 1)
                for q in (2 * h, 2 * h + 1):
                    c0 = (q % 2) * CH
                    xq = xic[:, :, h, c0:c0 + CH]
                    v.wait_ge(std_ready, q + 1)
                    link(v.reciprocal(std[:, q, :], std[:, q, :]))
                    v.wait_ge(sq_ready, q + 1)
                    TT(xq, xq, std[:, q, :].unsqueeze(1).to_broadcast([P, 4, CH]), ALU.mult).then_inc(xn_ready, 1)

            def taps_half(h):
                v.wait_ge(xn_ready, 2 * h + 2)
                v.wait_ge(ld_wdw, 64)
                last = {}
                order = [4, 0, 1, 2, 3, 5, 6, 7, 8]
                together = ((1, 2), (3,)) if h == 0 else ((2, 3),)
                steps = [(n, k, g) for branches in together for n, k in enumerate(order) for g in branches]
                for n, k, g in steps:
                    dy, dx = RATES[g] * (k // 3 - 1), RATES[g] * (k % 3 - 1)
                    y0, y1, x0, x1 = max(0, -dy), min(H, H - dy), max(0, -dx), min(W, W - dx)
                    xv = xic[:, g, h, :].rearrange("p (y x) -> p y x", x=W)[:, y0 + dy:y1 + dy, x0 + dx:x1 + dx]
                    yv = yic[:, g, h, :].rearrange("p (y x) -> p y x", x=W)[:, y0:y1, x0:x1]
                    if n == 0:
                        last[g] = mark(TS(yv, xv, wdw[:, g, k:k + 1], None, ALU.mult))
                        continue
                    v.wait_ge(dve, last[g])
                    ins = STT(out=yv, in0=xv, scalar=wdw[:, g, k:k + 1], in1=yv, op0=ALU.mult, op1=ALU.add)
                    if n < 8:
                        last[g] = mark(ins)
                    else:
                        ins.then_inc(taps_ready, 1)

            def add_batch(l, n):
                cols = slice(CPB * n * CH, CPB * (n + 1) * CH)
                if l == 0:
                    v.wait_ge(ld_x, 64)
                    v.wait_ge(or_ready, CPB * (n + 1))
                    term = orelu[n % 2]
                else:
                    v.wait_ge(prelu_ready, n + 1)
                    term = slab_c[:, cols]
                TT(slab_a[:, cols], slab_a[:, cols], term, ALU.add).then_inc(stream[l], 1)

            def token_stats(tiles, eps, ready=None):
                for j in tiles:
                    if ready and j % GT == 0:
                        v.wait_ge(ready, j // GT + 1)
                    m = mark(v.bn_stats(sums[:, j, :], tok[:, j, :]))
                v.wait_ge(dve, m)
                for j in tiles:
                    m = mark(v.bn_aggr(mv[:, j, :], sums[:, j, :]))
                v.wait_ge(dve, m)
                return TS(rstd[:, tiles[0] // TB % 2], mv[:, tiles[0]:tiles[-1] + 1, 1], eps, None, ALU.add)

            def route_batch(l, n, add_next):
                tiles = list(range(TB * n, TB * n + TB))
                if l == 1 and n + 1 < NBATCH:
                    prelu_batch(n + 1)
                token_stats(tiles, LN_EPS_T, tok_ready[l]).then_inc(tvar[l], 1)
                v.wait_ge(tstd[l], n + 1)
                rs = rstd[:, n % 2]
                link(v.reciprocal(rs, rs))
                link(TS(rstdx[:, n % 2], rs, XS, None, ALU.mult))
                STT(out=shift[:, n % 2], in0=mv[:, TB * n:TB * n + TB, 0], scalar=-1.0, in1=rstdx[:, n % 2],
                    op0=ALU.mult, op1=ALU.mult).then_inc(tok_scale[l], 1)
                over_e = lambda a: a.unsqueeze(2).to_broadcast([P, TB, E])
                over_t = lambda a: a.unsqueeze(1).to_broadcast([P, TB, E])
                v.wait_ge(tp_ready[l], GPB * (n // 2 * 2 + 2 if l == 0 else n + 1))
                lg = bank_lg[:, n * TB * E:(n + 1) * TB * E].rearrange("p (t e) -> p t e", e=E)
                link(TT(prob[:], lg, over_e(rs), ALU.mult))
                link(TT(prob[:], prob[:], over_t(gate_b[l][:]), ALU.add))
                link(v.tensor_reduce(red[:], prob[:], AX.X, ALU.max))
                TT(prob[:], prob[:], over_e(red[:]), ALU.subtract).then_inc(lg_shift[l], 1)
                v.wait_ge(lg_exp[l], n + 1)
                link(v.tensor_reduce(red[:], prob[:], AX.X, ALU.add))
                link(v.reciprocal(red[:], red[:]))
                link(TT(prob[:], prob[:], over_e(red[:]), ALU.mult))
                for k in range(TOPK):
                    link(v.tensor_reduce(top[:, k, :], prob[:], AX.X, ALU.max))
                    link(TT(tmp[:], prob[:], over_e(top[:, k, :]), ALU.is_equal))
                    link(TT(tmp[:], tmp[:], over_t(rev[:]), ALU.mult))
                    link(v.tensor_reduce(red[:], tmp[:], AX.X, ALU.max))
                    link(TT(best[:, k], over_t(rev[:]), over_e(red[:]), ALU.is_equal))
                    if k == 0:
                        link(STT(out=prob[:], in0=best[:, 0], scalar=-2.0, in1=prob[:], op0=ALU.mult, op1=ALU.add))
                TT(chosen[:, 0:TB, :], best[:, 0], best[:, 1], ALU.add).then_inc(chosen_ready[l], 1)
                r = rows_v[:, n % 2]
                v.wait_ge(xhi_ready[l], n + 1)
                hi = r[:, 0, :, 0:C // 2].bitcast(F16)
                link(TT(r[:, 0, :, C // 2:C].bitcast(F16), r[:, 1, :, 0:C], hi, ALU.subtract))
                m = mark(v.tensor_copy(r[:, 1, :, 0:C].bitcast(F16), r[:, 0, :, 0:C].bitcast(F16)))
                for k in range(TOPK):
                    m = mark(v.tensor_copy(r[:, k, :, C], top[:, k, :]))
                    m = mark(v.tensor_copy(r[:, k, :, C + 1].bitcast(I32), out_row[:, k, TB * n:TB * n + TB]))
                if add_next:
                    add_batch(l, n + 1)
                v.wait_ge(rank_ready[l], n + 1)
                link(TT(pos[:], bank_rk[:, 0:(TB + 1) * E].rearrange("p (t e) -> p t e", e=E),
                        carry[:].unsqueeze(1).to_broadcast([P, TB + 1, E]), ALU.add))
                link(v.tensor_copy(carry[:], pos[:, TB, :]))
                for k in range(TOPK):
                    link(TT(tmp[:], best[:, k], pos[:, 0:TB, :], ALU.mult))
                    link(v.tensor_reduce(slot_f[:, k, :], tmp[:], AX.X, ALU.add))
                v.tensor_copy(slot_ix[:, n % 2], slot_f[:]).then_inc(rows_ready[l], 1)

            def route_start(l):
                link(TS(carry[:], rev[:], -float(REGION), float(E * REGION), ALU.mult, ALU.add))

            def make_table(l):
                v.tensor_copy(fill_ix[0:1, :], carry[0:1, :]).then_inc(fill_ready[l], 1)
                s0 = small[0:1, :]
                v.wait_ge(fill_ready[l], 1)
                link(STT(out=s0[:, 0:E], in0=rev[0:1, :], scalar=float(REGION), in1=carry[0:1, :],
                         op0=ALU.mult, op1=ALU.add))
                link(TS(s0[:, 0:E], s0[:, 0:E], float(SR - 1 - E * REGION), None, ALU.add))
                link(v.tensor_copy(small_i[:], s0[:, 0:E]))
                link(TS(small_i[:], small_i[:], 8, None, ALU.arith_shift_right))
                link(v.tensor_copy(s0[:, 0:E], small_i[:]))
                link(v.tensor_tensor_scan(s0[:, E:2 * E], onesf[0:1, :], s0[:, 0:E], 0.0, ALU.mult, ALU.add))
                link(TS(s0[:, 0:E], s0[:, 0:E], -float(SR), float(REGION), ALU.mult, ALU.add))
                ge = slab_b[0:1, E * F:E * F + SLOTS * E].rearrange("p (i e) -> p i e", e=E)
                g2 = slab_c[0:1, E * F:E * F + SLOTS * E].rearrange("p (i e) -> p i e", e=E)
                rowf = slab_c[0:1, E * F + SLOTS * E:E * F + SLOTS * (E + 1)]
                shape = [1, SLOTS, E]
                link(TT(ge, tile_no[:].unsqueeze(2).to_broadcast(shape),
                        s0[:, E:2 * E].unsqueeze(1).to_broadcast(shape), ALU.is_ge))
                link(TT(g2, ge, s0[:, 0:E].unsqueeze(1).to_broadcast(shape), ALU.mult))
                link(v.tensor_reduce(rowf, g2, AX.X, ALU.add))
                link(STT(out=rowf, in0=tile_no[:], scalar=float(SR), in1=rowf, op0=ALU.mult, op1=ALU.add))
                link(TS(rowf, rowf, float(E * REGION), None, ALU.min))
                v.tensor_copy(tab_row[:, 0:SLOTS], rowf).then_inc(table_ready[l], 1)
                v.wait_ge(table_ready[l], 1)
                link(v.tensor_reduce(rowf, ge, AX.X, ALU.add))
                link(TS(rowf, rowf, float(E - 1), None, ALU.min))
                v.tensor_copy(tab_expert[:, 0:SLOTS], rowf).then_inc(table_ready[l], 1)

            def weights_low(l, k):
                src, hi, lo = (((slab_b, w1hi[0], w1lo[0]), (slab_c, w2hi[0], w2lo[0])),
                               ((slab_d, w1hi[1], w1lo[1]), (slab_b, w2hi[1], w2lo[1])))[l][k]
                v.wait_ge(hi_ready[l], k + 1)
                STT(out=lo[:], in0=src[:, 0:E * F], scalar=WS_, in1=hi[:], op0=ALU.mult,
                    op1=ALU.subtract).then_inc(lo_ready[l], 1)

            def experts(l):
                def copy_xt(base, k, e):
                    v.wait_ge(xt_ready[l], base + (k + 1))
                    v.tensor_copy(ring_b1[:, k % RING, :], b1_cols[:, bass.ds(e * FC + l * E * FC, FC)])
                    v.tensor_copy(ring_xt[:, k % 2], bank_xt[k % 2][:].bitcast(F16)[:, 0:2 * SR]
                                  .rearrange("p (k m) -> p k m", k=2)).then_inc(xt_copied[l], 1)

                def copy_meta(base, k, first):
                    if first:
                        v.wait_ge(xt_ready[l], base + (k + 1))
                    else:
                        v.wait_ge(y_stored[k % RING], stored_round(l, base, k - RING))
                    v.tensor_copy(ring_meta[:, k % RING], ring_rows[:, k % RING, :, C:ROW]).then_inc(meta_copied[l], 1)

                def low(base, k, q):
                    half = FC * SR // 2
                    at = slice(q * half, (q + 1) * half)
                    v.wait_ge(hhi_ready[l], 2 * base + (2 * k + q + 1))
                    STT(out=ring_hlo[:, k % 2, at], in0=ring_h[:, k % 2, at], scalar=HS,
                        in1=ring_hhi[:, k % 2, at], op0=ALU.mult, op1=ALU.subtract).then_inc(hlo_ready[l], 1)

                def bias_y(base, k, e):
                    v.wait_ge(y_ready[l], base + (k + 1))
                    STT(out=ring_yb[:, k % 2],
                        in0=bank_y[k % 2][:, 0:SUB * C].rearrange("p (j c) -> p j c", j=SUB),
                        scalar=1.0 / (WS_ * HS),
                        in1=b2_all[:, bass.ds(e * C + l * E * C, C)].unsqueeze(1).to_broadcast([P, SUB, C]),
                        op0=ALU.mult, op1=ALU.add).then_inc(y_biased[l], 1)

                def gate_y(base, k):
                    v.wait_ge(y_biased[l], base + (k + 1))
                    for j in range(SUB):
                        ins = TS(ring_y[:, k % RING, j, :], ring_yb[:, k % 2, j, :], ring_meta[:, k % RING, j, 0:1],
                                 None, ALU.mult)
                    ins.then_inc(y_copied[l], 1)

                def step(base, k, first, last, e):
                    ahead = not (last and k + 2 >= REST)
                    if ahead:
                        copy_xt(base, k + 2, e[k + 2])
                    more = not (last and k + 1 >= REST)
                    if more:
                        low(base, k + 1, 0)
                    bias_y(base, k, e[k])
                    if more:
                        low(base, k + 1, 1)
                    gate_y(base, k)
                    if ahead:
                        copy_meta(base, k + 2, first and k + 2 < RING)

                v.wait_ge(table_ready[l], 2)
                v.wait_ge(ld_b2, 32)
                e = table_values(ENG.DVE, tab_expert, 0, UNROLL + 2, E - 1)
                for k in range(2):
                    copy_xt(0, k, e[k])
                    copy_meta(0, k, True)
                for q in range(2):
                    low(0, 0, q)
                for k in range(UNROLL):
                    step(0, k, True, False, e)
                with v.Fori(UNROLL, N_TAIL, UNROLL) as i0:
                    e = table_values(ENG.DVE, tab_expert, i0, UNROLL + 2, E - 1)
                    for k in range(UNROLL):
                        step(i0, k, False, False, e)
                e = table_values(ENG.DVE, tab_expert, N_TAIL, REST, E - 1)
                for k in range(REST):
                    step(N_TAIL, k, False, True, e)

            def add_output(l, k, n):
                cols = slice(n * TB * C, (n + 1) * TB * C)
                v.wait_ge(ld_y[k][n], 16 * (l + 1))
                return TT(slab_t[:, cols], slab_t[:, cols], (slab_b, slab_c)[k][:, cols], ALU.add)

            def sum_batch(l, n):
                link(add_output(l, 0, n))
                add_output(l, 1, n).then_inc(sum_ready[l], 1)

            def norm_tokens():
                def stats(n):
                    sum_batch(0, n)
                    v.wait_ge(sum_ready[0], n + 1)
                    token_stats(list(range(TB * n, TB * n + TB)), LN_EPS_C).then_inc(var1, 1)

                stats(0)
                for n in range(NBATCH):
                    v.wait_ge(std1, n + 1)
                    link(v.reciprocal(rstd[:, n % 2], rstd[:, n % 2]))
                    STT(out=shift[:, n % 2], in0=mv[:, TB * n:TB * n + TB, 0], scalar=-1.0, in1=rstd[:, n % 2],
                        op0=ALU.mult, op1=ALU.mult).then_inc(scale1, 1)
                    if n + 1 < NBATCH:
                        if n >= 1:
                            v.wait_ge(xn1_ready, TB * n)
                        stats(n + 1)
                    for u in range(GPB * n, GPB * n + GPB):
                        v.wait_ge(tp1_copied, 2 * u + 2)
                        m = mark(v.bn_stats(bn_sums[:, u, :], slab_c[:, u * GT * P:(u + 1) * GT * P]))
                v.wait_ge(dve, m)
                link(v.bn_aggr(bn1[:, 0:2], bn_sums[:, 0:NGRP, :]))
                TS(bn1[:, 2:3], bn1[:, 1:2], BN_EPS, None, ALU.add).then_inc(bn1_var, 1)
                v.wait_ge(bn1_std, 1)
                link(v.reciprocal(bn1[:, 2:3], bn1[:, 2:3]))
                link(TT(bn1[:, 2:3], bn1[:, 2:3], par[:, 30:31], ALU.mult))
                link(TT(bn1[:, 3:4], bn1[:, 0:1], bn1[:, 2:3], ALU.mult))
                TT(bn1[:, 3:4], par[:, 31:32], bn1[:, 3:4], ALU.subtract).then_inc(bn1_ready, 1)
                for j in range(NCH):
                    v.wait_ge(conv_copied, j + 1)
                    m = mark(v.bn_stats(bn_sums[:, j, :], slab_b[:, j * CH:(j + 1) * CH]))
                v.wait_ge(dve, m)
                link(v.bn_aggr(bn2[:, 0:2], bn_sums[:, 0:NCH, :]))
                link(TT(bn2[:, 2:3], bn2[:, 1:2], bn2[:, 4:5], ALU.mult))
                link(TT(bn2[:, 2:3], bn2[:, 2:3], bn2[:, 4:5], ALU.mult))
                TS(bn2[:, 2:3], bn2[:, 2:3], BN_EPS, None, ALU.add).then_inc(bn2_var, 1)
                v.wait_ge(bn2_std, 1)
                link(v.reciprocal(bn2[:, 2:3], bn2[:, 2:3]))
                link(TT(bn2[:, 2:3], bn2[:, 2:3], bn2[:, 4:5], ALU.mult))
                link(TT(bn2[:, 2:3], bn2[:, 2:3], par[:, 32:33], ALU.mult))
                link(TT(bn2[:, 3:4], bn2[:, 0:1], bn2[:, 2:3], ALU.mult))
                link(TT(bn2[:, 3:4], par[:, 33:34], bn2[:, 3:4], ALU.subtract))
                link(TS(bn2[:, 5:6], par[:, 34:35], -1.0, 1.0, ALU.mult, ALU.add))
                TT(bn2[:, 6:7], par[:, 34:35], bn2[:, 3:4], ALU.mult).then_inc(bn2_ready, 1)

            def prelu_batch(n):
                cols = slice(CPB * n * CH, CPB * (n + 1) * CH)
                STT(out=slab_b[:, cols], in0=slab_b[:, cols], scalar=bn2[:, 2:3], in1=slab_c[:, cols],
                    op0=ALU.mult, op1=ALU.add).then_inc(u_ready, 1)
                v.wait_ge(u_ready, n + 1)
                link(STT(out=slab_a[:, cols], in0=slab_b[:, cols], scalar=par[:, 34:35], in1=slab_a[:, cols],
                         op0=ALU.mult, op1=ALU.add))

            norm_half(0)
            norm_half_end(0)
            diagonals(0)
            norm_half(1)
            fold_variances()
            fold_norms()
            taps_half(0)
            diagonals(1)
            prepare_0()
            norm_half_end(1)
            taps_half(1)
            route_start(0)
            add_batch(0, 0)
            add_batch(0, 1)
            route_batch(0, 0, False)
            route_batch(0, 1, False)
            prepare_1()
            add_batch(0, 2)
            add_batch(0, 3)
            route_batch(0, 2, False)
            weights_low(0, 0)
            route_batch(0, 3, False)
            make_table(0)
            weights_low(0, 1)
            weights_low(1, 0)
            weights_low(1, 1)
            experts(0)
            norm_tokens()
            v.wait_ge(bn2_ready, 1)
            route_start(1)
            prelu_batch(0)
            add_batch(1, 0)
            for n in range(NBATCH):
                route_batch(1, n, 1 <= n < NBATCH - 1)
                if n == 0:
                    add_batch(1, 1)
            make_table(1)
            experts(1)
            for n in range(NBATCH):
                m = mark(add_output(1, 0, n))
            v.wait_ge(dve, m)
            for n in range(NBATCH - 1):
                add_output(1, 1, n).then_inc(sum_ready[1], GPB)
            for m in range(GPB):
                u = NGRP - GPB + m
                cols = slice(u * GT * P, (u + 1) * GT * P)
                v.wait_ge(ld_last[m], 16)
                TT(slab_t[:, cols], slab_t[:, cols], slab_c[:, cols], ALU.add).then_inc(sum_ready[1], 1)

        @block.tensor
        def _(pe):
            mm, tr = nc.tensor.matmul, nc.tensor.transpose

            def prepare_0():
                pe.wait_ge(consts, N_CONSTS)
                pe.wait_ge(ld_branch, 16 * N_BRANCH)
                pe.wait_ge(ld_par, 16 * N_PAR)
                pe.wait_ge(ld_b1, 32)
                tr(banks[6][:, 0:35], par_rows[0:35, :], ident[0:35, 0:35])
                tr(banks[6][:, 64:64 + 2 * E * FC], b1_rows, ident[0:2 * E * FC, 0:2 * E * FC]).then_inc(prep_t, 1)
                pe.wait_ge(ld_wo, 16)
                tr(banks[5][:, 0:P], wo_raw, ident[:]).then_inc(prep_t, 1)
                pe.wait_ge(ld_gate, 64)
                for l in range(2):
                    ins = mm(banks[7][:, l * E:(l + 1) * E], all_mean[:], gate_w[l][:], start=True, stop=True)
                ins.then_inc(prep_t, 1)

            def prepare_1():
                pe.wait_ge(setup_dve, N_SETUP)
                for k in range(3):
                    for m in range(3):
                        ins = tr(banks[4 + k][:].bitcast(BF16)[:, m * P:(m + 1) * P], convw_full[:, 3 * k + m, :],
                                 identb[:])
                    ins.then_inc(convw_tp, 1)

            def norm_half(h):
                pe.wait_ge(ld_xic[h], 16 * 4)
                if h == 0:
                    pe.wait_ge(mean_blocks, 5)
                for q in (2 * h, 2 * h + 1):
                    c0 = (q % 2) * CH
                    if q >= 2:
                        pe.wait_ge(vare_ready, q - 1)
                    for g in range(4):
                        ins = mm(bank_stat[q % 2][:, 0:CH], block_mean[:], xic[:, g, h, c0:c0 + CH],
                                 start=(g == 0), stop=(g == 3))
                    ins.then_inc(mean_ready, 1)

            def norm_half_end(h):
                for q in (2 * h, 2 * h + 1):
                    c0 = (q % 2) * CH
                    pe.wait_ge(centred, q + 1)
                    pe.wait_ge(sq_ready, q + 1)
                    for g in range(4):
                        ins = mm(bank_stat[q % 2][:, 0:CH], block_mean[:], sq[:, g, c0:c0 + CH],
                                 start=(g == 0), stop=(g == 3))
                    ins.then_inc(var_ready, 1)

            def taps(h, g):
                pe.wait_ge(xn_ready, 2 * h + 2)
                pe.wait_ge(diag_ready, 9 * (g + 1))
                if h == 1:
                    pe.wait_ge(or_ready, 2 * CPB)
                for r in range(2):
                    if g >= 1:
                        pe.wait_ge(bn_ready, normed(h, g - 1) - 1 + r)
                    inside = []
                    for k in (4, 0, 1, 2, 3, 5, 6, 7, 8):
                        dy, dx = RATES[g] * (k // 3 - 1), RATES[g] * (k % 3 - 1)
                        y0, y1 = max(RH * r, -dy), min(RH * r + RH, H - dy)
                        x0, x1 = max(0, -dx), min(W, W - dx)
                        if y1 > y0 and x1 > x0:
                            inside.append((k, dy, dx, y0, y1, x0, x1))
                    for n, (k, dy, dx, y0, y1, x0, x1) in enumerate(inside):
                        xv = xic[:, g, h, :].rearrange("p (y x) -> p y x", x=W)[:, y0 + dy:y1 + dy, x0 + dx:x1 + dx]
                        yv = bank_dw[r][:, 0:CH].rearrange("p (y x) -> p y x", x=W)[:, y0 - RH * r:y1 - RH * r, x0:x1]
                        ins = mm(yv, diag[g][:, k, :], xv, start=(n == 0), stop=(n == len(inside) - 1))
                    ins.then_inc(dw_ready, 1)

            def mix_batch(n):
                def z(j):
                    b, r = j // 2, j % 2
                    pe.wait_ge(ld_ycm[b], 64)
                    if j >= 2:
                        pe.wait_ge(zr_ready, j - 1)
                    if j == 0:
                        pe.wait_ge(vare_ready, 4)
                    mm(bank_z[j % 2][:, 0:CH], mix[:], ycm[:, b, r * CH:r * CH + CH], start=True, stop=True)\
                        .then_inc(z_ready, 1)

                def o(j):
                    pe.wait_ge(zr_ready, j + 1)
                    if j >= 2:
                        pe.wait_ge(or_ready, j - 1)
                    pe.wait_ge(bn_ready, normed(0, 0) if n < 2 else normed(1, 1))
                    mm(bank_o[j % 2][:, 0:CH], wo_t[:], zrelu[:, j % 2, :], start=True, stop=True)\
                        .then_inc(o_ready, 1)

                z(CPB * n)
                for j in range(CPB * n, CPB * n + CPB):
                    if j + 1 < CPB * n + CPB:
                        z(j + 1)
                    o(j)

            def transpose_batch(l, n):
                pe.wait_ge(stream[l], n + 1)
                for u in range(GPB * n, GPB * n + GPB):
                    if u >= 2:
                        pe.wait_ge(tok_ready[l], u - 1)
                    for m in range(GT):
                        i = u * GT + m
                        xv = slab_a[:, i * P:(i + 1) * P]
                        tr(bank_tp[u % 2][:, m * P:(m + 1) * P], xv, ident[:])
                        ins = mm(bank_lg[:, i * E:(i + 1) * E], xv, gate_w[l][:], start=True, stop=True)
                    ins.then_inc(tp_ready[l], 1)

            def rank_batch(l, n):
                pe.wait_ge(chosen_ready[l], n + 1)
                flat = chosen[:].rearrange("p t e -> p (t e)")
                mm(bank_rk[:, 0:(TB + 1) * E], earlier[:], flat, start=True, stop=False)
                for j in range(TB):
                    n_after = TB - j
                    ins = mm(bank_rk[:, (j + 1) * E:(TB + 1) * E].rearrange("p (t e) -> p t e", e=E), onesb[:],
                             chosen[:, j:j + 1, :].to_broadcast([P, n_after, E]), start=False, stop=(j == TB - 1))
                ins.then_inc(rank_ready[l], 1)

            def experts(l):
                pe.wait_ge(table_ready[l], 2)
                if l == 0:
                    pe.wait_ge(lo_ready[0], 2)
                    pe.wait_ge(lo_ready[1], 2)
                    pe.wait_ge(hi_ready[1], 2)

                def early(base, k, n=2):
                    return isinstance(base, int) and base + k < n

                def turn(base, k):
                    pe.wait_ge(ld_ring[k % RING], ring_round(l, base, k))
                    if not early(base, k):
                        pe.wait_ge(xt_copied[l], base + (k - 1))
                    for part in range(2):
                        for j in range(SUB):
                            src = ring_rows[:, k % RING, j, part * C // 2:(part + 1) * C // 2].bitcast(F16)
                            at = part * SR + j * P
                            ins = tr(bank_xt[k % 2][:].bitcast(F16)[:, at:at + P], src, ident16[:])
                    ins.then_inc(xt_ready[l], 1)

                def hidden(base, k, e):
                    pe.wait_ge(xt_copied[l], base + (k + 1))
                    xhi, xlo = ring_xt[:, k % 2, 0, :], ring_xt[:, k % 2, 1, :]
                    for c in range(FC):
                        q = c // 2
                        if c % 2 == 0 and not early(base, k):
                            pe.wait_ge(gelu_ready[l], 2 * base + (2 * k + q - 3))
                        at = bass.ds(e * F + c * P, P)
                        hv = bank_h[k % 2][q][:, (c % 2) * SR:(c % 2 + 1) * SR]
                        mm(hv, w1hi[l][:, at], xhi, start=True, stop=False)
                        mm(hv, w1hi[l][:, at], xlo, start=False, stop=False)
                        ins = mm(hv, w1lo[l][:, at], xhi, start=False, stop=True)
                        if c % 2 == 1:
                            ins.then_inc(h_ready[l], 1)

                def output(base, k, e):
                    if not early(base, k):
                        pe.wait_ge(y_biased[l], base + (k - 1))
                    yv = [bank_y[k % 2][:, j * C:(j + 1) * C] for j in range(SUB)]
                    w = [bass.ds(e * F + c * P, P) for c in range(FC)]
                    for j in range(SUB):
                        h = [slice(c * SR + j * P, c * SR + j * P + P) for c in range(FC)]
                        for c in range(FC):
                            if j == 0 and c % 2 == 0:
                                pe.wait_ge(hhi_ready[l], 2 * base + (2 * k + c // 2 + 1))
                            mm(yv[j], ring_hhi[:, k % 2, h[c]], w2hi[l][:, w[c]], start=(c == 0), stop=False)
                            mm(yv[j], ring_hhi[:, k % 2, h[c]], w2lo[l][:, w[c]], start=False, stop=False)
                        for c in range(FC):
                            if j == 0 and c % 2 == 0:
                                pe.wait_ge(hlo_ready[l], 2 * base + (2 * k + c // 2 + 1))
                            ins = mm(yv[j], ring_hlo[:, k % 2, h[c]], w2hi[l][:, w[c]], start=False, stop=(c == FC - 1))
                    ins.then_inc(y_ready[l], 1)

                e = table_values(ENG.PE, tab_expert, 0, UNROLL + 1, E - 1)
                turn(0, 0)
                turn(0, 1)
                hidden(0, 0, e[0])
                for k in range(UNROLL):
                    turn(0, k + 2)
                    hidden(0, k + 1, e[k + 1])
                    output(0, k, e[k])
                with pe.Fori(UNROLL, N_TAIL, UNROLL) as i0:
                    e = table_values(ENG.PE, tab_expert, i0, UNROLL + 1, E - 1)
                    for k in range(UNROLL):
                        turn(i0, k + 2)
                        hidden(i0, k + 1, e[k + 1])
                        output(i0, k, e[k])
                e = table_values(ENG.PE, tab_expert, N_TAIL, REST, E - 1)
                for k in range(REST):
                    if k + 2 < REST:
                        turn(N_TAIL, k + 2)
                    if k + 1 < REST:
                        hidden(N_TAIL, k + 1, e[k + 1])
                    output(N_TAIL, k, e[k])

            def norm_tokens():
                for u in range(NGRP):
                    n = u // GPB
                    pe.wait_ge(sum_ready[0], n + 1)
                    if u == 0:
                        pe.wait_ge(y_copied[0], SLOTS)
                    if u >= 2:
                        pe.wait_ge(tp1_copied, 2 * u - 3)
                    for m in range(GT):
                        ins = tr(bank_tp[u % 2][:, m * P:(m + 1) * P], tok[:, u * GT + m, :], ident[:])
                    ins.then_inc(tp1_ready, 1)
                    pe.wait_ge(xn1_ready, (u + 1) * GT)
                    if u >= 2:
                        pe.wait_ge(tp1_copied, 2 * u - 2)
                    for m in range(GT):
                        ins = tr(bank_tn[u % 2][:, m * P:(m + 1) * P], tok_b[:, u * GT + m, :], ident[:])
                    ins.then_inc(tp1_ready, 1)
                for j in range(NCH):
                    b, r = j // 2, j % 2
                    pe.wait_ge(signs_ready, b + 1)
                    if j >= 2:
                        pe.wait_ge(conv_copied, j - 1)
                    for k in range(9):
                        ky, kx = k // 3, k % 3
                        ins = mm(bank_conv[j % 2][:, 0:CH].rearrange("p (y x) -> p y x", x=W), convw_t[:, k, :],
                                 signs[:, b, RH * r + ky:RH * r + ky + RH, kx:kx + W], start=(k == 0), stop=(k == 8))
                    ins.then_inc(conv_ready, 1)

            norm_half(0)
            norm_half_end(0)
            norm_half(1)
            prepare_0()
            taps(0, 0)
            norm_half_end(1)
            pe.wait_ge(setup_dve, 3)
            pe.wait_ge(setup_act, 1)
            for n in (0, 1):
                mix_batch(n)
            for n in (0, 1):
                transpose_batch(0, n)
            taps(1, 0)
            rank_batch(0, 0)
            taps(1, 1)
            rank_batch(0, 1)
            for n in (2, 3):
                mix_batch(n)
            for n in (2, 3):
                transpose_batch(0, n)
            rank_batch(0, 2)
            rank_batch(0, 3)
            prepare_1()
            pe.wait_ge(setup_act, 5)
            experts(0)
            norm_tokens()
            for n in range(NBATCH):
                transpose_batch(1, n)
                rank_batch(1, n)
            experts(1)
            for u in range(NGRP):
                pe.wait_ge(sum_ready[1], u + 1 if u >= NGRP - GPB else GPB * (u // GPB + 1))
                if u >= 2:
                    pe.wait_ge(out_ready, u - 1)
                if u == 0:
                    pe.wait_ge(y_copied[1], SLOTS)
                for m in range(GT):
                    ins = tr(bank_tp[u % 2][:, m * P:(m + 1) * P], tok[:, u * GT + m, :], ident[:])
                ins.then_inc(tpo_ready, 1)


_INS = ["x",
        *("L0_conv_" + n for n in ("wdw", "bdw", "gdw", "bedw", "mdw", "vdw", "ws", "bs", "gs", "bes", "ms", "vs",
                                   "wo", "bo", "go", "beo", "mo", "vo")),
        *("L0_ffn_" + n for n in ("gate_w", "gate_b", "w1", "b1", "w2", "b2")),
        *("L1_conv_" + n for n in ("conv_w", "bn1_gamma", "bn1_beta", "bn2_gamma", "bn2_beta", "prelu_a")),
        *("L1_ffn_" + n for n in ("gate_w", "gate_b", "w1", "b1", "w2", "b2"))]


def kernel(**inputs):
    import numpy as _np
    import concourse.bacc as _bacc
    from concourse import mybir as _mybir
    from concourse.bass_utils import run_bass_kernel_spmd as _run

    nc = _bacc.Bacc("TRN2", target_bir_lowering=False, num_devices=1)
    arrays, args = {}, {}
    for name in _INS:
        a = _np.ascontiguousarray(inputs[name])
        arrays[f"in_{name}_dram"] = a
        args[name] = nc.dram_tensor(f"in_{name}_dram", a.shape, _mybir.dt.from_np(a.dtype), kind="ExternalInput").ap()
    out = nc.dram_tensor("out_0_dram", (B, C, H, W), F32, kind="ExternalOutput").ap()
    metaformer_kernel(nc, args, out)
    r = _run(nc, [arrays], core_ids=[0])
    return r.results[0]["out_0_dram"]
```
